# Optimizing a Trainium2 kernel written in Bass

```python
import numpy as np
import jax
import jax.numpy as jnp

def _softmax(x, axis=-1):
    return jax.nn.softmax(x, axis=axis)

def _gelu(x):
    return jax.nn.gelu(x, approximate=True)

def _silu(x):
    return jax.nn.silu(x)

def _sigmoid(x):
    return jax.nn.sigmoid(x)

def _layernorm(x, axis=-1, eps=1e-05):
    m = jnp.mean(x, axis=axis, keepdims=True)
    v = jnp.var(x, axis=axis, keepdims=True)
    return (x - m) / jnp.sqrt(v + eps)

def _scatter_add(tgt, idx, src, axis=0):
    return tgt.at[idx].add(src)

def _segment_sum(src, seg, n):
    return jax.ops.segment_sum(src, seg, n)
kernel_name = 'mk_macaron_d2_jaxref_r8_7c55b8'

def setup_inputs(seed: int=0):
    np.random.seed(seed)
    _w = jnp.asarray

    def _L0_attn_setup():
        import jax, jax.numpy as jnp
        import numpy as np
        from jax.lax import associative_scan
        B, S, D, F, G = (4, 512, 128, 512, 32)
        EPS = 1e-06

        def _gate_loop(k, v, q, a):
            kv = (k * v).astype(jnp.complex64)

            def op(e1, e2):
                a1, x1 = e1
                a2, x2 = e2
                return (a1 * a2, a2 * x1 + x2)
            _, h = associative_scan(op, (a, kv), axis=1)
            return q.astype(jnp.complex64) * h

        def _layernorm(x, scale, bias):
            mu = jnp.mean(x, axis=-1, keepdims=True)
            var = jnp.mean(jnp.square(x - mu), axis=-1, keepdims=True)
            return (x - mu) * jax.lax.rsqrt(var + EPS) * scale + bias

        def _groupnorm_complex(y, scale, bias):
            b, s, d = y.shape
            yr = y.reshape(b, s, G, d // G)
            mean = jnp.mean(yr, axis=(1, 3), keepdims=True)
            mean2 = jnp.mean(yr.real ** 2 + yr.imag ** 2, axis=(1, 3), keepdims=True)
            var = mean2 - (mean.real ** 2 + mean.imag ** 2)
            yn = (yr - mean) * jax.lax.rsqrt(var + EPS)
            return yn.reshape(b, s, d) * scale + bias
        key = jax.random.key(seed)
        ks = jax.random.split(key, 16)
        xn = lambda k, shp: jax.random.normal(k, shp, jnp.float32) / np.sqrt(shp[0])
        return {'x': jax.random.normal(ks[0], (B, S, D), jnp.float32), 'Wq': xn(ks[1], (D, D)), 'Wk': xn(ks[2], (D, D)), 'Wv': xn(ks[3], (D, D)), 'Wa': xn(ks[4], (D, 2 * D)), 'Wg': xn(ks[5], (D, D)), 'Wo': xn(ks[6], (D, D)), 'gn_scale': jnp.ones((D,), jnp.float32), 'gn_bias': jnp.zeros((D,), jnp.float32), 'ln1_scale': jnp.ones((D,), jnp.float32), 'ln1_bias': jnp.zeros((D,), jnp.float32), 'W1': xn(ks[7], (D, F)), 'b1': jax.random.normal(ks[8], (F,), jnp.float32) * 1e-06, 'W2': xn(ks[9], (F, D)), 'b2': jax.random.normal(ks[10], (D,), jnp.float32) * 1e-06, 'ln2_scale': jnp.ones((D,), jnp.float32), 'ln2_bias': jnp.zeros((D,), jnp.float32)}
    _L0_attn_in = _L0_attn_setup()

    def _L0_ffn_setup():
        import jax, jax.numpy as jnp
        import numpy as np
        TOPK = 2
        EPS = 1e-06
        key = jax.random.key(seed)
        ks = jax.random.split(key, 8)
        b, t, d, h, n = (2, 128, 128, 256, 16)
        x = jax.random.normal(ks[0], (b, t, d), dtype=jnp.float32)
        router_w = jax.random.normal(ks[1], (n, d), dtype=jnp.float32) * (1.0 / np.sqrt(d))
        router_bias = jnp.zeros((n,), dtype=jnp.float32)
        bank_mag = jax.random.normal(ks[2], (n, d, h), dtype=jnp.float32) * (1.0 / np.sqrt(d))
        bank_freq = jax.random.uniform(ks[3], (n, d, h), dtype=jnp.float32, minval=0.5, maxval=2.0) * (1.0 / np.sqrt(d))
        bank_phase = jax.random.uniform(ks[4], (n, h), dtype=jnp.float32, minval=-0.3, maxval=0.3)
        bank_down = jax.random.normal(ks[5], (n, h, d), dtype=jnp.float32) * (1.0 / np.sqrt(h))
        norm_w = jnp.ones((d,), dtype=jnp.float32)
        return {'x': x, 'router_w': router_w, 'router_bias': router_bias, 'bank_mag': bank_mag, 'bank_freq': bank_freq, 'bank_phase': bank_phase, 'bank_down': bank_down, 'norm_w': norm_w}
    _L0_ffn_in = _L0_ffn_setup()

    def _L1_attn_setup():
        import jax, jax.numpy as jnp
        import numpy as np
        B, T, DIM, H = (2, 256, 128, 16)
        HD = DIM // H

        def _custom_softmax(a):
            a = jnp.clip(a, -100.0, 100.0)
            m = jnp.max(a, axis=-1, keepdims=True)
            e = jnp.exp(a - m)
            p = e / (jnp.sum(e, axis=-1, keepdims=True) + 1e-06)
            p = p + 1e-08
            return p / jnp.sum(p, axis=-1, keepdims=True)
        key = jax.random.key(seed)
        k1, k2, k3 = jax.random.split(key, 3)
        x = jax.random.normal(k1, (B, T, DIM), dtype=jnp.float32)
        w_qkv = jax.random.normal(k2, (3 * DIM, DIM), dtype=jnp.float32) / np.sqrt(DIM)
        w_proj = jax.random.normal(k3, (DIM, DIM), dtype=jnp.float32) / np.sqrt(DIM)
        return {'x': x, 'w_qkv': w_qkv, 'w_proj': w_proj}
    _L1_attn_in = _L1_attn_setup()

    def _L1_ffn_setup():
        import jax, jax.numpy as jnp
        import numpy as np
        E = 8
        K = 2
        R = 64
        ALPHA = 128.0
        SCALING = ALPHA / R
        key = jax.random.key(seed)
        k0, k1, k2, k3 = jax.random.split(key, 4)
        B, S, D = (4, 512, 128)
        x = jax.random.normal(k0, (B, S, D), jnp.float32)
        Wg = jax.random.normal(k1, (E, D), jnp.float32) * 0.02
        bg = jnp.zeros((E,), jnp.float32)
        W1 = jax.random.normal(k2, (E, R, D), jnp.float32) * (1.0 / np.sqrt(D))
        W2 = jax.random.normal(k3, (E, D, R), jnp.float32) * 0.02
        return {'x': x, 'Wg': Wg, 'bg': bg, 'W1': W1, 'W2': W2}
    _L1_ffn_in = _L1_ffn_setup()
    _d = {'L0_attn_x': _L0_attn_in['x'], 'L0_attn_Wq': _L0_attn_in['Wq'], 'L0_attn_Wk': _L0_attn_in['Wk'], 'L0_attn_Wv': _L0_attn_in['Wv'], 'L0_attn_Wa': _L0_attn_in['Wa'], 'L0_attn_Wg': _L0_attn_in['Wg'], 'L0_attn_Wo': _L0_attn_in['Wo'], 'L0_attn_gn_scale': _L0_attn_in['gn_scale'], 'L0_attn_gn_bias': _L0_attn_in['gn_bias'], 'L0_attn_ln1_scale': _L0_attn_in['ln1_scale'], 'L0_attn_ln1_bias': _L0_attn_in['ln1_bias'], 'L0_attn_W1': _L0_attn_in['W1'], 'L0_attn_b1': _L0_attn_in['b1'], 'L0_attn_W2': _L0_attn_in['W2'], 'L0_attn_b2': _L0_attn_in['b2'], 'L0_attn_ln2_scale': _L0_attn_in['ln2_scale'], 'L0_attn_ln2_bias': _L0_attn_in['ln2_bias'], 'L0_ffn_router_w': _L0_ffn_in['router_w'], 'L0_ffn_router_bias': _L0_ffn_in['router_bias'], 'L0_ffn_bank_mag': _L0_ffn_in['bank_mag'], 'L0_ffn_bank_freq': _L0_ffn_in['bank_freq'], 'L0_ffn_bank_phase': _L0_ffn_in['bank_phase'], 'L0_ffn_bank_down': _L0_ffn_in['bank_down'], 'L0_ffn_norm_w': _L0_ffn_in['norm_w'], 'L1_attn_w_qkv': _L1_attn_in['w_qkv'], 'L1_attn_w_proj': _L1_attn_in['w_proj'], 'L1_ffn_Wg': _L1_ffn_in['Wg'], 'L1_ffn_bg': _L1_ffn_in['bg'], 'L1_ffn_W1': _L1_ffn_in['W1'], 'L1_ffn_W2': _L1_ffn_in['W2']}
    _x0 = _d['L0_attn_x']
    _d['L0_attn_x'] = jax.random.normal(jax.random.fold_in(jax.random.key(seed), 1), (32, 256, 128), dtype=_x0.dtype)
    del _x0
    return _d

def reference(L0_attn_x, L0_attn_Wq, L0_attn_Wk, L0_attn_Wv, L0_attn_Wa, L0_attn_Wg, L0_attn_Wo, L0_attn_gn_scale, L0_attn_gn_bias, L0_attn_ln1_scale, L0_attn_ln1_bias, L0_attn_W1, L0_attn_b1, L0_attn_W2, L0_attn_b2, L0_attn_ln2_scale, L0_attn_ln2_bias, L0_ffn_router_w, L0_ffn_router_bias, L0_ffn_bank_mag, L0_ffn_bank_freq, L0_ffn_bank_phase, L0_ffn_bank_down, L0_ffn_norm_w, L1_attn_w_qkv, L1_attn_w_proj, L1_ffn_Wg, L1_ffn_bg, L1_ffn_W1, L1_ffn_W2):

    def _L0_attn_ref(x, Wq, Wk, Wv, Wa, Wg, Wo, gn_scale, gn_bias, ln1_scale, ln1_bias, W1, b1, W2, b2, ln2_scale, ln2_bias):
        import jax, jax.numpy as jnp
        import numpy as np
        from jax.lax import associative_scan
        B, S, D, F, G = (4, 512, 128, 512, 32)
        EPS = 1e-06

        def _gate_loop(k, v, q, a):
            kv = (k * v).astype(jnp.complex64)

            def op(e1, e2):
                a1, x1 = e1
                a2, x2 = e2
                return (a1 * a2, a2 * x1 + x2)
            _, h = associative_scan(op, (a, kv), axis=1)
            return q.astype(jnp.complex64) * h

        def _layernorm(x, scale, bias):
            mu = jnp.mean(x, axis=-1, keepdims=True)
            var = jnp.mean(jnp.square(x - mu), axis=-1, keepdims=True)
            return (x - mu) * jax.lax.rsqrt(var + EPS) * scale + bias

        def _groupnorm_complex(y, scale, bias):
            b, s, d = y.shape
            yr = y.reshape(b, s, G, d // G)
            mean = jnp.mean(yr, axis=(1, 3), keepdims=True)
            mean2 = jnp.mean(yr.real ** 2 + yr.imag ** 2, axis=(1, 3), keepdims=True)
            var = mean2 - (mean.real ** 2 + mean.imag ** 2)
            yn = (yr - mean) * jax.lax.rsqrt(var + EPS)
            return yn.reshape(b, s, d) * scale + bias
        q = x @ Wq
        k = x @ Wk
        v = x @ Wv
        a = x @ Wa
        a_real, a_imag = jnp.split(a, 2, axis=-1)
        a_c = a_real + 1j * a_imag
        mag = jnp.abs(a_c)
        phase = jnp.angle(a_c)
        a_c = jax.nn.sigmoid(mag) * jnp.exp(1j * phase)
        g = (x @ Wg).astype(jnp.complex64)
        y = _gate_loop(k, v, q, a_c)
        y = _groupnorm_complex(y, gn_scale, gn_bias)
        silu_g = g / (1.0 + jnp.exp(-g))
        y = y * silu_g
        y = (y @ Wo.astype(jnp.complex64)).real
        x = _layernorm(x + y, ln1_scale, ln1_bias)
        h = jax.nn.gelu(x @ W1 + b1)
        out = x + (h @ W2 + b2)
        return _layernorm(out, ln2_scale, ln2_bias)

    def _L0_ffn_ref(x, router_w, router_bias, bank_mag, bank_freq, bank_phase, bank_down, norm_w):
        import jax, jax.numpy as jnp
        import numpy as np
        TOPK = 2
        EPS = 1e-06
        b, t, d = x.shape
        scores = jnp.einsum('btd,nd->btn', x, router_w) + router_bias
        topv, topi = jax.lax.top_k(scores, TOPK)
        weights = jax.nn.softmax(topv, axis=-1)
        fx = x.reshape(b * t, d)
        mag = jnp.einsum('td,ndh->tnh', fx, bank_mag)
        freq = jnp.einsum('td,ndh->tnh', fx, bank_freq)
        hidden = jnp.tanh(mag) * jnp.cos(jax.nn.softplus(freq) + 0.1 + bank_phase[None, :, :])
        out_all = jnp.einsum('tnh,nhd->tnd', hidden, bank_down)
        ti = topi.reshape(b * t, TOPK)
        sel = jnp.take_along_axis(out_all, ti[:, :, None], axis=1)
        out = jnp.einsum('tkd,tk->td', sel, weights.reshape(b * t, TOPK)).reshape(b, t, d)
        out = out * jax.lax.rsqrt(jnp.mean(out * out, axis=-1, keepdims=True) + EPS) * norm_w
        return out

    def _L1_attn_ref(x, w_qkv, w_proj):
        import jax, jax.numpy as jnp
        import numpy as np
        B, T, DIM, H = (2, 256, 128, 16)
        HD = DIM // H

        def _custom_softmax(a):
            a = jnp.clip(a, -100.0, 100.0)
            m = jnp.max(a, axis=-1, keepdims=True)
            e = jnp.exp(a - m)
            p = e / (jnp.sum(e, axis=-1, keepdims=True) + 1e-06)
            p = p + 1e-08
            return p / jnp.sum(p, axis=-1, keepdims=True)
        b, t, c = x.shape
        scale = HD ** (-0.5)
        qkv = jnp.einsum('btc,oc->bto', x, w_qkv)
        qkv = qkv.reshape(b, t, 3, H, HD)
        q = jnp.transpose(qkv[:, :, 0], (0, 2, 1, 3))
        k = jnp.transpose(qkv[:, :, 1], (0, 2, 1, 3))
        v = jnp.transpose(qkv[:, :, 2], (0, 2, 1, 3))
        attn = jnp.einsum('bhqd,bhkd->bhqk', q, k) * scale
        causal = jnp.tril(jnp.ones((t, t), dtype=bool))
        attn = jnp.where(causal, attn, -jnp.inf)
        attn = _custom_softmax(attn)
        out = jnp.einsum('bhqk,bhkd->bhqd', attn, v)
        out = jnp.transpose(out, (0, 2, 1, 3)).reshape(b, t, c)
        return jnp.einsum('btc,oc->bto', out, w_proj)

    def _L1_ffn_ref(x, Wg, bg, W1, W2):
        import jax, jax.numpy as jnp
        import numpy as np
        E = 8
        K = 2
        R = 64
        ALPHA = 128.0
        SCALING = ALPHA / R
        orig_shape = x.shape
        D = orig_shape[-1]
        xf = x.reshape(-1, D)
        logits = xf @ Wg.T + bg
        top_gates, top_idx = jax.lax.top_k(logits, K)
        top_gates = jax.nn.softmax(top_gates, axis=-1)
        h = jax.nn.gelu(jnp.einsum('nd,erd->enr', xf, W1), approximate=False)
        eout = SCALING * jnp.einsum('enr,edr->ned', h, W2)
        sel = jnp.take_along_axis(eout, top_idx[:, :, None], axis=1)
        out = jnp.sum(top_gates[:, :, None] * sel, axis=1)
        return out.reshape(orig_shape)
    x = L0_attn_x
    x = x + 0.5 * _L0_ffn_ref(_layernorm(x, axis=-1), L0_ffn_router_w, L0_ffn_router_bias, L0_ffn_bank_mag, L0_ffn_bank_freq, L0_ffn_bank_phase, L0_ffn_bank_down, L0_ffn_norm_w)
    x = x + _L0_attn_ref(_layernorm(x, axis=-1), L0_attn_Wq, L0_attn_Wk, L0_attn_Wv, L0_attn_Wa, L0_attn_Wg, L0_attn_Wo, L0_attn_gn_scale, L0_attn_gn_bias, L0_attn_ln1_scale, L0_attn_ln1_bias, L0_attn_W1, L0_attn_b1, L0_attn_W2, L0_attn_b2, L0_attn_ln2_scale, L0_attn_ln2_bias)
    x = x + 0.5 * _L0_ffn_ref(_layernorm(x, axis=-1), L0_ffn_router_w, L0_ffn_router_bias, L0_ffn_bank_mag, L0_ffn_bank_freq, L0_ffn_bank_phase, L0_ffn_bank_down, L0_ffn_norm_w)
    x = x + 0.5 * _L1_ffn_ref(_layernorm(x, axis=-1), L1_ffn_Wg, L1_ffn_bg, L1_ffn_W1, L1_ffn_W2)
    x = x + _L1_attn_ref(_layernorm(x, axis=-1), L1_attn_w_qkv, L1_attn_w_proj)
    x = x + 0.5 * _L1_ffn_ref(_layernorm(x, axis=-1), L1_ffn_Wg, L1_ffn_bg, L1_ffn_W1, L1_ffn_W2)
    return x

_drawn_inputs = setup_inputs


def setup_inputs(seed=0):
    import zlib

    import numpy as np

    out = dict(_drawn_inputs(seed))
    spreads = {'L0_attn_gn_scale': (1.0, 0.2),
     'L0_attn_gn_bias': (0.0, 0.1),
     'L0_attn_ln1_scale': (1.0, 0.2),
     'L0_attn_ln1_bias': (0.0, 0.1),
     'L0_attn_ln2_scale': (1.0, 0.2),
     'L0_attn_ln2_bias': (0.0, 0.1),
     'L0_ffn_router_bias': (0.0, 0.1),
     'L0_ffn_norm_w': (1.0, 0.2),
     'L1_ffn_bg': (0.0, 0.1)}
    factors = {}
    for name, (base, spread) in spreads.items():
        noise = np.random.default_rng([zlib.crc32(name.encode()), seed]).standard_normal(out[name].shape)
        drawn = base * np.exp(spread * noise) if base else spread * noise
        out[name] = jnp.asarray(drawn.astype(out[name].dtype))
    for name, factor in factors.items():
        out[name] = (out[name] * factor).astype(out[name].dtype)
    return out
```

```python
from contextlib import ExitStack

import concourse.bass as bass
from concourse import mybir

F32 = mybir.dt.float32
BF16 = mybir.dt.bfloat16
I32 = mybir.dt.int32
U32 = mybir.dt.uint32
ALU = mybir.AluOpType
ACT = mybir.ActivationFunctionType
AX = mybir.AxisListType

P = 128
D = 128
B, T = 32, 256
N = B * T
TILES = N // P
GROUP = 4
GW = GROUP * D
GROUPS = TILES // GROUP
LN_EPS = 1e-5
EPS = 1e-6
MAGIC = 1.5 * 2.0 ** 23
PI = 3.141592653589793
TURN = 6.283185

E0, H0 = 16, 256
UNITS = 144
BATCH = 4
SLOTS = UNITS * P
E1, R1 = 8, 64
ER = E1 * R1
FF = 512
GN_GROUP = 4
HEADS, HD = 16, 8
VW = HD + 1
SEM0 = 120
NEG = -1e30


ALL = ("l0_ffn", "l0_attn", "l0_ffn", "l1_ffn", "l1_attn", "l1_ffn")


def macaron_kernel(nc, a, out, stages=ALL):
    ctx = ExitStack()
    names = [0]

    def uniq(n):
        names[0] += 1
        return f"{n}_{names[0]}"

    def dram(n, shape, dt=F32):
        return nc.dram_tensor(uniq(n), shape, dt, kind="Internal").ap()

    def chain(eng, sem, base=0):
        count = [0]

        def link(ins):
            count[0] += 1
            ins.then_inc(sem, 1)
            eng.wait_ge(sem, base + count[0])
        return link

    with ctx:
        def sb(n, shape, dt=F32):
            return ctx.enter_context(nc.sbuf_tensor(uniq(n), shape, dt))

        stage_sems = []

        def semaphore(n):
            stage_sems.append(nc.alloc_semaphore(name=uniq(n), num=SEM0 + len(stage_sems)))
            return stage_sems[-1]

        def gather_semaphore(n):
            return nc.alloc_semaphore(name=uniq(n))

        def end_stage():
            nc.all_engine_barrier(sems_to_clear=range(SEM0, SEM0 + len(stage_sems)))
            for s in stage_sems:
                nc.release_semaphore(s)
            stage_sems.clear()

        X = sb("X", [P, TILES * D])
        XN = sb("XN", [P, TILES * D])
        ident = sb("ident", [P, P])
        ident_b = sb("ident_b", [P, P], BF16)
        ones = sb("ones", [P, P])
        ones_b = sb("ones_b", [P, P], BF16)
        strict_b = sb("strict_b", [P, P], BF16)
        strict = sb("strict", [P, P])
        causal_b = sb("causal_b", [P, P], BF16)
        blockg = sb("blockg", [P, P])
        router_wT = sb("router_wT", [D, E0])
        gate_wT = sb("gate_wT", [D, E1])
        up1T = sb("up1T", [D, ER])
        down1T = sb("down1T", [P, ER])
        qkvT = sb("qkvT", [D, 3 * D])
        projT = sb("projT", [D, D])
        rbias = sb("rbias", [P, E0])
        gbias = sb("gbias", [P, E1])
        norm_w = sb("norm_w", [P, D])
        MV = sb("MV", [P, TILES * 2])
        MV2 = MV[:, :].rearrange("p (t k) -> p t k", k=2)
        headmask = sb("headmask", [P, GROUP])

        x_tiles = a["L0_attn_x"].rearrange("b t d -> (b t) d").rearrange("(t p) d -> p t d", p=P)
        out_tiles = out.rearrange("b t d -> (b t) d").rearrange("(t p) d -> p t d", p=P)
        X3 = X[:, :].rearrange("p (t d) -> p t d", d=D)

        def row_to_all(ap, n):
            return ap.rearrange("(o n) -> o n", o=1).broadcast_to([P, n])

        with ExitStack() as st:
            raw = {}
            for n, shape in (("rw", [E0, D]), ("gw", [E1, D]), ("w1", [P, 4, D]), ("w2", [D, ER]),
                             ("qkv", [P, 3, D]), ("proj", [D, D])):
                raw[n] = st.enter_context(nc.sbuf_tensor(uniq("raw_" + n), shape, F32))
            turned = [st.enter_context(nc.psum_tensor(uniq("turned"), [P, 512], F32)) for _ in range(4)]
            s_in = semaphore("s_in")
            s_const = semaphore("s_const")
            s_id = semaphore("s_id")
            s_turn = semaphore("s_turn")
            block = st.enter_context(nc.Block())
            loads = [
                (X3, x_tiles), (raw["rw"][:, :], a["L0_ffn_router_w"]), (raw["gw"][:, :], a["L1_ffn_Wg"]),
                (raw["w1"][:, :, :], a["L1_ffn_W1"].rearrange("e r d -> (e r) d").rearrange("(c p) d -> p c d", p=P)),
                (raw["w2"][:, :].rearrange("d (e r) -> d e r", r=R1), a["L1_ffn_W2"].rearrange("e d r -> d e r")),
                (raw["qkv"][:, :, :], a["L1_attn_w_qkv"].rearrange("(c p) d -> p c d", p=P)),
                (raw["proj"][:, :], a["L1_attn_w_proj"]),
                (rbias[:, :], row_to_all(a["L0_ffn_router_bias"], E0)),
                (gbias[:, :], row_to_all(a["L1_ffn_bg"], E1)),
                (norm_w[:, :], row_to_all(a["L0_ffn_norm_w"], D)),
            ]

            @block.sync
            def _(sp):
                for dst, src in loads:
                    sp.dma_start(dst, src).then_inc(s_in, 16)

            @block.gpsimd
            def _(pool):
                pool.memset(ident[:, :], 0.0)
                pool.memset(ones[:, :], 1.0)
                pool.memset(blockg[:, :], 1.0 / (GN_GROUP * T))
                pool.memset(causal_b[:, :], 0.0)
                pool.memset(headmask[:, :], 1.0)
                pool.memset(ones_b[:, :], 1.0).then_inc(s_const, 1)
                pool.wait_ge(s_const, 1)
                pool.affine_select(out=ident[:, :], in_=ident[:, :], compare_op=ALU.not_equal, fill=1.0,
                                   base=0, pattern=[[-1, P]], channel_multiplier=1)
                pool.affine_select(out=strict[:, :], in_=ones[:, :], compare_op=ALU.is_gt, fill=0.0,
                                   base=0, pattern=[[1, P]], channel_multiplier=-1)
                pool.affine_select(out=causal_b[:, :], in_=causal_b[:, :], compare_op=ALU.is_ge, fill=NEG,
                                   base=0, pattern=[[-1, P]], channel_multiplier=1)
                pool.affine_select(out=blockg[:, :].rearrange("p (g j) -> p g j", j=GN_GROUP),
                                   in_=blockg[:, :].rearrange("p (g j) -> p g j", j=GN_GROUP),
                                   compare_op=ALU.is_ge, fill=0.0, base=0,
                                   pattern=[[-GN_GROUP, P // GN_GROUP], [0, GN_GROUP]],
                                   channel_multiplier=1).then_inc(s_const, 1)
                pool.wait_ge(s_const, 2)
                pool.affine_select(out=blockg[:, :].rearrange("p (g j) -> p g j", j=GN_GROUP),
                                   in_=blockg[:, :].rearrange("p (g j) -> p g j", j=GN_GROUP),
                                   compare_op=ALU.is_ge, fill=0.0, base=GN_GROUP - 1,
                                   pattern=[[GN_GROUP, P // GN_GROUP], [0, GN_GROUP]],
                                   channel_multiplier=-1)
                pool.tensor_copy(ident_b[:, :], ident[:, :])
                pool.tensor_copy(strict_b[:, :], strict[:, :]).then_inc(s_id, 1)

            @block.vector
            def _(dve):
                dve.wait_ge(s_id, 1)
                dve.tensor_reduce(headmask[:, :], ident[:, :].rearrange("p (r j d) -> p j r d", j=GROUP, d=HD),
                                  AX.XY, ALU.add)

            turns = [(router_wT[:, :], raw["rw"][:, :], E0), (gate_wT[:, :], raw["gw"][:, :], E1),
                     (projT[:, :], raw["proj"][:, :], P)]
            turns += [(up1T[:, c * P:(c + 1) * P], raw["w1"][:, c, :], P) for c in range(4)]
            turns += [(down1T[:, c * P:(c + 1) * P], raw["w2"][:, c * P:(c + 1) * P], P) for c in range(4)]
            turns += [(qkvT[:, c * P:(c + 1) * P], raw["qkv"][:, c, :], P) for c in range(3)]

            @block.tensor
            def _(pe):
                pe.wait_ge(s_id, 1)
                pe.wait_ge(s_in, 16 * len(loads))
                for n, (dst, src, rows) in enumerate(turns):
                    o = turned[n // 4][:, (n % 4) * P:(n % 4) * P + rows]
                    pe.transpose(o, src, ident[0:rows, 0:rows]).then_inc(s_turn, 1)

            @block.scalar
            def _(act):
                for n, (dst, src, rows) in enumerate(turns):
                    act.wait_ge(s_turn, len(turns))
                    act.activation(dst, turned[n // 4][:, (n % 4) * P:(n % 4) * P + rows], ACT.Copy)

        def top2(dve, act_exp, link, SC, E, tmp, idx, big=3e38):
            m1, m2, k, oh1, oh2, sc2 = tmp
            v = lambda t: t[:, :].rearrange("p (t e) -> p t e", e=E)
            up = lambda t: t[:, :].unsqueeze(2).broadcast_to([P, TILES, E])
            for src, m, oh in ((SC, m1, oh1), (sc2, m2, oh2)):
                link(dve.tensor_reduce(m[:, :], v(src), AX.X, ALU.max))
                link(dve.tensor_tensor(v(oh), v(src), up(m), ALU.is_equal))
                link(dve.tensor_tensor(oh[:, :], oh[:, :], idx[:, :], ALU.mult))
                link(dve.tensor_reduce(k[:, :], v(oh), AX.X, ALU.max))
                link(dve.tensor_tensor(v(oh), v(idx), up(k), ALU.is_equal))
                if src is SC:
                    link(dve.scalar_tensor_tensor(sc2[:, :], oh[:, :], -big, SC[:, :], ALU.mult, ALU.add))

        def norm_stats(src, eps):
            with ExitStack() as st:
                stats = st.enter_context(nc.sbuf_tensor(uniq("stats"), [P, TILES * 6], F32))
                half = st.enter_context(nc.sbuf_tensor(uniq("half"), [P, TILES], F32))
                s_stat = semaphore("s_stat")
                s_var = semaphore("s_var")
                s_std = semaphore("s_std")
                block = st.enter_context(nc.Block())
                each = stats[:, :].rearrange("p (t k) -> p t k", k=6)

                @block.vector
                def _(dve):
                    with dve.Fori(0, TILES // 8) as i:
                        for j in range(8):
                            last = dve.bn_stats(stats[:, bass.ds(i * 48 + 6 * j, 6)], src[:, bass.ds(i * (8 * D) + j * D, D)])
                        last.then_inc(s_stat, 1)
                    link = chain(dve, s_stat, TILES // 8)
                    dve.wait_ge(s_stat, TILES // 8)
                    dve.tensor_tensor(MV2[:, :, 0], each[:, :, 1], each[:, :, 4], ALU.add)
                    dve.tensor_tensor(half[:, :], each[:, :, 1], each[:, :, 4], ALU.subtract)
                    link(dve.tensor_tensor(MV2[:, :, 1], each[:, :, 2], each[:, :, 5], ALU.add))
                    dve.tensor_scalar(MV2[:, :, 0], MV2[:, :, 0], 0.5, None, ALU.mult)
                    dve.tensor_scalar(MV2[:, :, 1], MV2[:, :, 1], 1.0 / D, eps, ALU.mult, ALU.add)
                    link(dve.scalar_tensor_tensor(half[:, :], half[:, :], 0.25, half[:, :], ALU.mult, ALU.mult))
                    dve.tensor_tensor(MV2[:, :, 1], MV2[:, :, 1], half[:, :], ALU.add).then_inc(s_var, 1)
                    dve.wait_ge(s_std, 1)
                    dve.reciprocal(MV2[:, :, 1], MV2[:, :, 1])

                @block.scalar
                def _(act):
                    act.wait_ge(s_var, 1)
                    act.activation(MV2[:, :, 1], MV2[:, :, 1], ACT.Sqrt).then_inc(s_std, 1)

        def norm_tiles(dve, dst, src, col, first, n=GROUP):
            for j in range(n):
                last = dve.tensor_scalar(dst(j), src[:, bass.ds(col + j * D, D)], MV[:, bass.ds(first + 2 * j, 1)],
                                         MV[:, bass.ds(first + 2 * j + 1, 1)], ALU.subtract, ALU.mult)
            return last

        def l0_ffn():
            norm_stats(X, LN_EPS)
            xs_sorted = dram("xs_sorted", [SLOTS, D])
            ys_sorted = dram("ys_sorted", [SLOTS, D])
            with ExitStack() as st:
                def sb(n, shape, dt=F32):
                    return st.enter_context(nc.sbuf_tensor(uniq(n), shape, dt))

                def sem(n):
                    return semaphore(n)

                MF = sb("MF", [P, E0 * 2 * H0])
                DN = sb("DN", [P, E0 * 2 * D])
                PH = sb("PH", [P, E0 * H0])
                slot1 = sb("slot1", [P, TILES], I32)
                slot2 = sb("slot2", [P, TILES], I32)
                w1 = sb("w1", [P, TILES])
                w2 = sb("w2", [P, TILES])
                unit_of = sb("unit_of", [P, UNITS], I32)
                s_weights = sem("s_weights")
                s_zero = sem("s_zero")

                with ExitStack() as st2:
                    def sb2(n, shape, dt=F32):
                        return st2.enter_context(nc.sbuf_tensor(uniq(n), shape, dt))

                    def sem2(n):
                        return semaphore(n)

                    SC = sb2("SC", [P, TILES * E0])
                    rb4 = rbias[:, :].unsqueeze(1).broadcast_to([P, GROUP, E0])
                    with ExitStack() as st3:
                        xs = st3.enter_context(nc.sbuf_tensor(uniq("xs"), [P, 2, GW], F32))
                        xsT = st3.enter_context(nc.sbuf_tensor(uniq("xsT"), [P, 2, GW], F32))
                        zero = st3.enter_context(nc.sbuf_tensor(uniq("zero"), [P, 2 * GW], F32))
                        pT = [st3.enter_context(nc.psum_tensor(uniq("pT"), [P, 512], F32)) for _ in range(2)]
                        pR = [st3.enter_context(nc.psum_tensor(uniq("pR"), [P, 512], F32)) for _ in range(2)]
                        S = {n: semaphore(n) for n in
                             ("xs", "turned", "xsT", "kept", "scores", "taken", "z")}
                        block = st3.enter_context(nc.Block())

                        @block.sync
                        def _(sp):
                            MFv = MF[:, :].rearrange("p (e k h) -> p e k h", k=2, h=H0)
                            sp.dma_start(MFv[:, :, 0, :], a["L0_ffn_bank_mag"].rearrange("e d h -> d e h")).then_inc(s_weights, 16)
                            sp.dma_start(MFv[:, :, 1, :], a["L0_ffn_bank_freq"].rearrange("e d h -> d e h")).then_inc(s_weights, 16)
                            sp.dma_start(DN[:, :].rearrange("p (e c d) -> p e c d", c=2, d=D),
                                         a["L0_ffn_bank_down"].rearrange("e (c p) d -> p e c d", p=P)).then_inc(s_weights, 16)
                            sp.dma_start(PH[:, :], row_to_all(a["L0_ffn_bank_phase"].rearrange("e h -> (e h)"), E0 * H0)).then_inc(s_weights, 16)
                            sp.wait_ge(S["z"], 1)
                            for u in range(0, UNITS, 8):
                                sp.dma_start(xs_sorted[u * P:(u + 8) * P, :].rearrange("(p t) d -> p (t d)", p=P),
                                             zero[:, :]).then_inc(s_zero, 16)
                            sp.wait_ge(s_weights, 64)
                            sp.wait_ge(s_zero, 16 * (UNITS // 8))

                        @block.gpsimd
                        def _(pool):
                            pool.memset(zero[:, :], 0.0).then_inc(S["z"], 1)
                            with pool.Fori(0, GROUPS // 2) as i:
                                for u in range(2):
                                    pool.wait_ge(S["xs"], i * 2 + u + 1)
                                    pool.tensor_copy(XN[:, bass.ds(i * (2 * GW) + u * GW, GW)], xs[:, u, :]).then_inc(S["kept"], 1)

                        @block.vector
                        def _(dve):
                            dve.sem_inc(S["taken"], 2)
                            dve.sem_inc(S["kept"], 2)
                            with dve.Fori(0, GROUPS // 2) as i:
                                for u in range(2):
                                    dve.wait_ge(S["kept"], i * 2 + u + 1)
                                    dve.wait_ge(S["turned"], i * 2 + u + 1)
                                    norm_tiles(dve, lambda j: xs[:, u, j * D:(j + 1) * D], X, i * (2 * GW) + u * GW,
                                               i * (4 * GROUP) + u * 2 * GROUP).then_inc(S["xs"], 1)
                                    dve.wait_ge(S["scores"], i * 2 + u + 1)
                                    dve.tensor_tensor(
                                        SC[:, bass.ds(i * (2 * GROUP * E0) + u * GROUP * E0, GROUP * E0)].rearrange("p (t e) -> p t e", e=E0),
                                        pR[u][:, 0:GROUP * E0].rearrange("p (t e) -> p t e", e=E0), rb4,
                                        ALU.add).then_inc(S["taken"], 1)

                        @block.tensor
                        def _(pe):
                            pe.sem_inc(S["turned"], 2)
                            with pe.Fori(0, GROUPS // 2) as i:
                                for u in range(2):
                                    pe.wait_ge(S["xs"], i * 2 + u + 1)
                                    pe.wait_ge(S["xsT"], i * 2 + u + 1)
                                    for j in range(GROUP):
                                        last = pe.transpose(pT[u][:, j * P:(j + 1) * P], xs[:, u, j * D:(j + 1) * D], ident[:, :])
                                    last.then_inc(S["turned"], 1)
                                    pe.wait_ge(S["xsT"], i * 2 + u + 3)
                                    pe.wait_ge(S["taken"], i * 2 + u + 1)
                                    for j in range(GROUP):
                                        last = pe.matmul(pR[u][:, j * E0:(j + 1) * E0], xsT[:, u, j * P:(j + 1) * P],
                                                         router_wT[:, :], start=True, stop=True)
                                    last.then_inc(S["scores"], 1)

                        @block.scalar
                        def _(act):
                            act.sem_inc(S["xsT"], 2)
                            with act.Fori(0, GROUPS // 2) as i:
                                for u in range(2):
                                    act.wait_ge(S["turned"], i * 2 + u + 3)
                                    act.wait_ge(S["taken"], i * 2 + u + 1)
                                    act.activation(xsT[:, u, :], pT[u][:, :], ACT.Copy).then_inc(S["xsT"], 1)

                    with ExitStack() as st3:
                        def sb3(n, shape, dt=F32):
                            return st3.enter_context(nc.sbuf_tensor(uniq(n), shape, dt))
                        idx = sb3("idx", [P, TILES * E0])
                        notfirst = sb3("notfirst", [P, TILES * E0])
                        unit_no = sb3("unit_no", [P, UNITS])
                        m1, m2, k = (sb3(n, [P, TILES]) for n in ("m1", "m2", "k"))
                        oh1, oh2, sc2 = (sb3(n, [P, TILES * E0]) for n in ("oh1", "oh2", "sc2"))
                        cnt = sb3("cnt", [P, TILES * E0], BF16)
                        tot = sb3("tot", [P, TILES * E0])
                        run = sb3("run", [P, TILES * E0])
                        slot = sb3("slot", [P, TILES * E0])
                        nt, ci, base = (sb3(n, [P, E0]) for n in ("nt", "ci", "base"))
                        cmp = sb3("cmp", [P, UNITS * E0])
                        unit_f = sb3("unit_f", [P, UNITS])
                        pE = [st3.enter_context(nc.psum_tensor(uniq("pE"), [P, 512], F32)) for _ in range(2)]
                        pS = [st3.enter_context(nc.psum_tensor(uniq("pS"), [P, 512], F32)) for _ in range(2)]
                        S = {n: semaphore(n) for n in ("c", "iota", "delta", "exp", "cnt", "sums")}
                        block = st3.enter_context(nc.Block())
                        te = lambda t: t[:, :].rearrange("p (t e) -> p t e", e=E0)
                        et = lambda t: t[:, :].rearrange("p (e t) -> p e t", t=TILES)
                        te_as_et = lambda t: t[:, :].rearrange("p (t e) -> p e t", e=E0)

                        @block.gpsimd
                        def _(pool):
                            pool.iota(te(idx), pattern=[[0, TILES], [-1, E0]], base=E0, channel_multiplier=0,
                                      allow_small_or_imprecise_dtypes=True)
                            pool.iota(unit_no[:, :], pattern=[[1, UNITS]], base=0, channel_multiplier=0,
                                      allow_small_or_imprecise_dtypes=True)
                            pool.memset(notfirst[:, :], 1.0).then_inc(S["iota"], 1)
                            pool.wait_ge(S["iota"], 1)
                            pool.memset(et(notfirst)[:, :, 0:1], 0.0).then_inc(S["iota"], 1)

                        @block.scalar
                        def _(act):
                            act.wait_ge(S["delta"], 1)
                            act.activation(w2[:, :], k[:, :], ACT.Exp).then_inc(S["exp"], 1)

                        @block.tensor
                        def _(pe):
                            pe.wait_ge(S["cnt"], 1)
                            for h in range(2):
                                pe.matmul(pE[h][:, :], strict_b[:, :], cnt[:, h * 512:(h + 1) * 512], start=True, stop=True)
                                last = pe.matmul(pS[h][:, :], ones_b[:, :], cnt[:, h * 512:(h + 1) * 512], start=True, stop=True)
                            last.then_inc(S["sums"], 1)

                        @block.vector
                        def _(dve):
                            link = chain(dve, S["c"])
                            dve.wait_ge(S["iota"], 2)
                            top2(dve, None, link, SC, E0, (m1, m2, k, oh1, oh2, sc2), idx)
                            dve.tensor_tensor(cnt[:, :], oh1[:, :], oh2[:, :], ALU.add).then_inc(S["cnt"], 1)
                            dve.tensor_tensor(k[:, :], m2[:, :], m1[:, :], ALU.subtract).then_inc(S["delta"], 1)
                            dve.wait_ge(S["exp"], 1)
                            link(dve.tensor_scalar(w1[:, :], w2[:, :], 1.0, None, ALU.add))
                            link(dve.reciprocal(w1[:, :], w1[:, :]))
                            link(dve.tensor_tensor(w2[:, :], w2[:, :], w1[:, :], ALU.mult))
                            dve.wait_ge(S["sums"], 1)
                            for h in range(2):
                                l = dve.tensor_copy(et(tot)[:, :, h * 32:(h + 1) * 32],
                                                    pS[h][:, :].rearrange("p (t e) -> p e t", e=E0))
                            link(l)
                            link(dve.tensor_tensor_scan(run[:, :], notfirst[:, :], tot[:, :], 0.0, ALU.mult, ALU.add))
                            link(dve.tensor_scalar(nt[:, :], et(run)[:, :, TILES - 1], 1.0 / P,
                                                   (P - 1.0) / P - 0.5 + 0.5 / P, ALU.mult, ALU.add))
                            link(dve.tensor_scalar(nt[:, :], nt[:, :], MAGIC, MAGIC, ALU.add, ALU.subtract))
                            link(dve.tensor_tensor_scan(ci[:, :], ones[:, 0:E0], nt[:, :], 0.0, ALU.mult, ALU.add))
                            link(dve.tensor_tensor(base[:, :], ci[:, :], nt[:, :], ALU.subtract))
                            link(dve.tensor_scalar(base[:, :], base[:, :], float(P), None, ALU.mult))
                            link(dve.tensor_tensor(run[:, :], run[:, :], tot[:, :], ALU.subtract))
                            link(dve.tensor_tensor(et(run), et(run), base[:, :].unsqueeze(2).broadcast_to([P, E0, TILES]), ALU.add))
                            for h in range(2):
                                l = dve.tensor_tensor(te_as_et(slot)[:, :, h * 32:(h + 1) * 32], et(run)[:, :, h * 32:(h + 1) * 32],
                                                      pE[h][:, :].rearrange("p (t e) -> p e t", e=E0), ALU.add)
                            link(l)
                            for oh, dst in ((oh1, slot1), (oh2, slot2)):
                                link(dve.tensor_tensor(oh[:, :], oh[:, :], slot[:, :], ALU.mult))
                                link(dve.tensor_reduce(k[:, :], te(oh), AX.X, ALU.add))
                                link(dve.tensor_copy(dst[:, :], k[:, :]))
                            cv = cmp[:, :].rearrange("p (u e) -> p u e", e=E0)
                            link(dve.tensor_tensor(cv, unit_no[:, :].unsqueeze(2).broadcast_to([P, UNITS, E0]),
                                                   ci[:, :].unsqueeze(1).broadcast_to([P, UNITS, E0]), ALU.is_ge))
                            link(dve.tensor_reduce(unit_f[:, :], cv, AX.X, ALU.add))
                            link(dve.tensor_scalar(unit_f[:, :], unit_f[:, :], float(E0 - 1), None, ALU.min))
                            link(dve.tensor_copy(unit_of[:, :], unit_f[:, :]))

                with ExitStack() as st3:
                    s_moved = gather_semaphore("s_moved")
                    block = st3.enter_context(nc.Block())

                    @block.gpsimd
                    def _(pool):
                        for t in range(TILES):
                            for s in (slot1, slot2):
                                pool.indirect_dma_start(
                                    out=xs_sorted, out_offset=bass.IndirectOffsetOnAxis(ap=s[:, t:t + 1].bitcast(U32), axis=0),
                                    in_=XN[:, t * D:(t + 1) * D], in_offset=None).then_inc(s_moved, 16)
                        pool.wait_ge(s_moved, 16 * 2 * TILES)

                with ExitStack() as st3:
                    def sb3(n, shape, dt=F32):
                        return st3.enter_context(nc.sbuf_tensor(uniq(n), shape, dt))
                    xg = sb3("xg", [P, 2, BATCH * D])
                    xgT = sb3("xgT", [P, BATCH * P])
                    th = sb3("th", [P, BATCH * H0])
                    fb = sb3("fb", [P, BATCH * H0])
                    nn = sb3("nn", [P, BATCH * H0])
                    hT = sb3("hT", [P, BATCH * 2 * P])
                    yo = sb3("yo", [P, 2, BATCH * D])
                    pMag = st3.enter_context(nc.psum_tensor(uniq("pMag"), [P, BATCH * H0], F32))
                    pFreq = st3.enter_context(nc.psum_tensor(uniq("pFreq"), [P, BATCH * H0], F32))
                    pT = st3.enter_context(nc.psum_tensor(uniq("pT"), [P, 512], F32))
                    pH = st3.enter_context(nc.psum_tensor(uniq("pH"), [P, 1024], F32))
                    pO = st3.enter_context(nc.psum_tensor(uniq("pO"), [P, 512], F32))
                    S = {n: semaphore(n) for n in
                         ("ph", "turned", "xgT", "mf", "low", "a", "d", "hid", "hTp", "hT", "o", "yo", "st0", "st1")}
                    S |= {n: gather_semaphore(n) for n in ("in0", "in1")}
                    block = st3.enter_context(nc.Block())
                    NB = UNITS // BATCH
                    bw = BATCH * H0

                    @block.gpsimd
                    def _(pool):
                        with pool.Fori(0, NB // 2) as i:
                            for u in range(2):
                                pool.wait_ge(S["turned"], i * 2 + u + 1)
                                pool.dma_start(xg[:, u, :].rearrange("p (t d) -> p t d", d=D),
                                             xs_sorted[bass.ds(i * (2 * BATCH * P) + u * BATCH * P, BATCH * P), :]
                                             .rearrange("(t p) d -> p t d", p=P)).then_inc(S[f"in{u}"], 16)

                    @block.sync
                    def _(sp):
                        with sp.Fori(0, NB // 2) as i:
                            for u in range(2):
                                sp.wait_ge(S["yo"], i * 2 + u + 3)
                                sp.dma_start(ys_sorted[bass.ds(i * (2 * BATCH * P) + u * BATCH * P, BATCH * P), :]
                                               .rearrange("(t p) d -> p t d", p=P),
                                               yo[:, u, :].rearrange("p (t d) -> p t d", d=D)).then_inc(S[f"st{u}"], 16)
                        for u in range(2):
                            sp.wait_ge(S[f"st{u}"], 16 * (NB // 2 + 1))

                    @block.tensor
                    def _(pe):
                        pe.sem_inc(S["turned"], 2)
                        with pe.Fori(0, NB // 2) as i:
                            for u in range(2):
                                n = i * 2 + u
                                pe.wait_ge(S[f"in{u}"], i * 16 + 16)
                                pe.wait_ge(S["xgT"], n + 1)
                                for j in range(BATCH):
                                    l = pe.transpose(pT[:, j * P:(j + 1) * P], xg[:, u, j * D:(j + 1) * D], ident[:, :])
                                l.then_inc(S["turned"], 1)
                                pe.wait_ge(S["xgT"], n + 2)
                                pe.wait_ge(S["hid"], n + 1)
                                ex = []
                                for j in range(BATCH):
                                    e = pe.value_load(unit_of[0:1, bass.ds(i * (2 * BATCH) + u * BATCH + j, 1)], min_val=0, max_val=E0 - 1)
                                    ex.append(e)
                                    pe.matmul(pMag[:, j * H0:(j + 1) * H0], xgT[:, j * P:(j + 1) * P],
                                              MF[:, bass.ds(e * (2 * H0), H0)], start=True, stop=True)
                                    l = pe.matmul(pFreq[:, j * H0:(j + 1) * H0], xgT[:, j * P:(j + 1) * P],
                                                  MF[:, bass.ds(e * (2 * H0) + H0, H0)], start=True, stop=True)
                                l.then_inc(S["mf"], 1)
                                pe.wait_ge(S["hid"], n + 2)
                                for j in range(BATCH):
                                    for c in range(2):
                                        l = pe.transpose(pH[:, (2 * j + c) * P:(2 * j + c + 1) * P],
                                                         th[:, j * H0 + c * P:j * H0 + (c + 1) * P], ident[:, :])
                                l.then_inc(S["hTp"], 1)
                                pe.wait_ge(S["hT"], n + 1)
                                pe.wait_ge(S["yo"], n + 2)
                                for j in range(BATCH):
                                    for c in range(2):
                                        l = pe.matmul(pO[:, j * D:(j + 1) * D], hT[:, (2 * j + c) * P:(2 * j + c + 1) * P],
                                                      DN[:, bass.ds(ex[j] * (2 * D) + c * D, D)], start=(c == 0), stop=(c == 1))
                                l.then_inc(S["o"], 1)

                    @block.scalar
                    def _(act):
                        act.sem_inc(S["xgT"], 1)
                        with act.Fori(0, NB // 2) as i:
                            for u in range(2):
                                n = i * 2 + u
                                act.wait_ge(S["turned"], n + 3)
                                act.activation(xgT[:, :], pT[:, :], ACT.Copy).then_inc(S["xgT"], 1)
                                act.preload_act_table_set("natural_log_exp_and_others")
                                act.wait_ge(S["low"], n + 1)
                                act.activation(fb[:, :], fb[:, :], ACT.Exp).then_inc(S["a"], 1)
                                act.wait_ge(S["a"], i * 4 + 2 * u + 1)
                                act.activation(fb[:, :], fb[:, :], ACT.Ln, bias=1.0).then_inc(S["a"], 1)
                                act.preload_act_table_set("silu_and_others")
                                act.activation(th[:, :], pMag[:, :], ACT.Tanh)
                                act.wait_ge(S["d"], i * 8 + u * 4 + 4)
                                act.activation(fb[:, :], fb[:, :], ACT.Sin, scale=-TURN).then_inc(S["ph"], 1)
                                act.wait_ge(S["hTp"], n + 1)
                                act.activation(hT[:, :], pH[:, :], ACT.Copy).then_inc(S["hT"], 1)

                    @block.vector
                    def _(dve):
                        dve.sem_inc(S["hid"], 1)
                        dve.sem_inc(S["yo"], 2)
                        dve.sem_inc(S["st0"], 16)
                        dve.sem_inc(S["st1"], 16)
                        dve.tensor_scalar(PH[:, :], PH[:, :], 0.1 + PI / 2, 1.0 / (2 * PI), ALU.add, ALU.mult).then_inc(s_zero, 1)
                        dve.wait_ge(s_zero, 16 * (UNITS // 8) + 1)
                        with dve.Fori(0, NB // 2) as i:
                            for u in range(2):
                                n = i * 2 + u
                                link = chain(dve, S["d"], i * 8 + u * 4)
                                dve.wait_ge(S["mf"], n + 1)
                                dve.tensor_scalar(fb[:, :], pFreq[:, :], 40.0, None, ALU.min).then_inc(S["low"], 1)
                                dve.wait_ge(S["a"], i * 4 + 2 * u + 2)
                                link(dve.tensor_tensor(fb[:, :], fb[:, :], pFreq[:, :], ALU.max))
                                for j in range(BATCH):
                                    e = dve.value_load(unit_of[0:1, bass.ds(i * (2 * BATCH) + u * BATCH + j, 1)], min_val=0, max_val=E0 - 1)
                                    l = dve.scalar_tensor_tensor(fb[:, j * H0:(j + 1) * H0], fb[:, j * H0:(j + 1) * H0],
                                                                 1.0 / (2 * PI), PH[:, bass.ds(e * H0, H0)], ALU.mult, ALU.add)
                                link(l)
                                link(dve.tensor_scalar(nn[:, :], fb[:, :], MAGIC, None, ALU.add))
                                link(dve.scalar_tensor_tensor(fb[:, :], nn[:, :], MAGIC, fb[:, :], ALU.subtract, ALU.subtract))
                                dve.wait_ge(S["ph"], n + 1)
                                dve.tensor_tensor(th[:, :], th[:, :], fb[:, :], ALU.mult).then_inc(S["hid"], 1)
                                dve.wait_ge(S["o"], n + 1)
                                dve.wait_ge(S[f"st{u}"], i * 16 + 16)
                                dve.tensor_copy(yo[:, u, :], pO[:, :]).then_inc(S["yo"], 1)

                with ExitStack() as st3:
                    def sb3(n, shape, dt=F32):
                        return st3.enter_context(nc.sbuf_tensor(uniq(n), shape, dt))
                    G = 8
                    R = TILES // G
                    y1 = sb3("y1", [P, 2, G * D])
                    y2 = sb3("y2", [P, 2, G * D])
                    sq = sb3("sq", [P, G * D])
                    ms = sb3("ms", [P, 2, G])
                    S = {n: semaphore(n) for n in ("ms", "rms", "c", "x")}
                    S |= {n: gather_semaphore(n) for n in ("g0", "g1")}
                    block = st3.enter_context(nc.Block())

                    @block.gpsimd
                    def _(pool):
                        def gather(r):
                            if r >= 2:
                                pool.wait_ge(S["x"], r - 1)
                            for g in range(G):
                                t = r * G + g
                                for s, y in ((slot1, y1), (slot2, y2)):
                                    pool.indirect_dma_start(
                                        out=y[:, r % 2, g * D:(g + 1) * D], out_offset=None, in_=ys_sorted,
                                        in_offset=bass.IndirectOffsetOnAxis(ap=s[:, t:t + 1].bitcast(U32), axis=0)).then_inc(S[f"g{r % 2}"], 16)

                        gather(0)
                        for r in range(R):
                            if r + 1 < R:
                                gather(r + 1)

                    @block.scalar
                    def _(act):
                        for r in range(R):
                            act.wait_ge(S["ms"], r + 1)
                            act.activation(ms[:, r % 2, :], ms[:, r % 2, :], ACT.Sqrt).then_inc(S["rms"], 1)

                    @block.vector
                    def _(dve):
                        link = chain(dve, S["c"])
                        v = lambda t: t.rearrange("p (t d) -> p t d", d=D)
                        for r in range(R):
                            dve.wait_ge(S[f"g{r % 2}"], 16 * 2 * G * (r // 2 + 1))
                            wb = lambda w: w[:, r * G:(r + 1) * G].unsqueeze(2).broadcast_to([P, G, D])
                            b1, b2 = y1[:, r % 2, :], y2[:, r % 2, :]
                            link(dve.tensor_tensor(v(b1), v(b1), wb(w1), ALU.mult))
                            link(dve.tensor_tensor(v(b2), v(b2), wb(w2), ALU.mult))
                            link(dve.tensor_tensor(b1, b1, b2, ALU.add))
                            link(dve.tensor_tensor(sq[:, :], b1, b1, ALU.mult))
                            link(dve.tensor_reduce(ms[:, r % 2, :], v(sq[:, :]), AX.X, ALU.add))
                            dve.tensor_scalar(ms[:, r % 2, :], ms[:, r % 2, :], 1.0 / D, EPS, ALU.mult, ALU.add).then_inc(S["ms"], 1)
                            dve.wait_ge(S["rms"], r + 1)
                            link(dve.reciprocal(ms[:, r % 2, :], ms[:, r % 2, :]))
                            link(dve.tensor_tensor(v(b1), v(b1), ms[:, r % 2, :].unsqueeze(2).broadcast_to([P, G, D]), ALU.mult))
                            link(dve.tensor_tensor(v(b1), v(b1), norm_w[:, :].unsqueeze(1).broadcast_to([P, G, D]), ALU.mult))
                            xr = X[:, r * G * D:(r + 1) * G * D]
                            dve.scalar_tensor_tensor(xr, b1, 0.5, xr, ALU.mult, ALU.add).then_inc(S["x"], 1)

        def l1_ffn():
            norm_stats(X, LN_EPS)
            XNT = XN
            with ExitStack() as st:
                SC = st.enter_context(nc.sbuf_tensor(uniq("SC"), [P, TILES * E1], F32))
                gb4 = gbias[:, :].unsqueeze(1).broadcast_to([P, GROUP, E1])
                with ExitStack() as st3:
                    xs = st3.enter_context(nc.sbuf_tensor(uniq("xs"), [P, 2, GW], F32))
                    xsT = st3.enter_context(nc.sbuf_tensor(uniq("xsT"), [P, 2, GW], F32))
                    pT = [st3.enter_context(nc.psum_tensor(uniq("pT"), [P, 512], F32)) for _ in range(2)]
                    pR = [st3.enter_context(nc.psum_tensor(uniq("pR"), [P, 512], F32)) for _ in range(2)]
                    S = {n: semaphore(n) for n in ("xs", "turned", "xsT", "kept", "scores", "taken")}
                    block = st3.enter_context(nc.Block())

                    @block.gpsimd
                    def _(pool):
                        pool.sem_inc(S["kept"], 2)
                        with pool.Fori(0, GROUPS // 2) as i:
                            for u in range(2):
                                pool.wait_ge(S["xsT"], i * 2 + u + 3)
                                pool.tensor_copy(XNT[:, bass.ds(i * (2 * GW) + u * GW, GW)], xsT[:, u, :]).then_inc(S["kept"], 1)

                    @block.vector
                    def _(dve):
                        dve.sem_inc(S["taken"], 2)
                        with dve.Fori(0, GROUPS // 2) as i:
                            for u in range(2):
                                dve.wait_ge(S["turned"], i * 2 + u + 1)
                                norm_tiles(dve, lambda j: xs[:, u, j * D:(j + 1) * D], X, i * (2 * GW) + u * GW,
                                           i * (4 * GROUP) + u * 2 * GROUP).then_inc(S["xs"], 1)
                                dve.wait_ge(S["scores"], i * 2 + u + 1)
                                dve.tensor_tensor(
                                    SC[:, bass.ds(i * (2 * GROUP * E1) + u * GROUP * E1, GROUP * E1)].rearrange("p (t e) -> p t e", e=E1),
                                    pR[u][:, 0:GROUP * E1].rearrange("p (t e) -> p t e", e=E1), gb4,
                                    ALU.add).then_inc(S["taken"], 1)

                    @block.tensor
                    def _(pe):
                        pe.sem_inc(S["turned"], 2)
                        with pe.Fori(0, GROUPS // 2) as i:
                            for u in range(2):
                                pe.wait_ge(S["xs"], i * 2 + u + 1)
                                pe.wait_ge(S["xsT"], i * 2 + u + 1)
                                for j in range(GROUP):
                                    last = pe.transpose(pT[u][:, j * P:(j + 1) * P], xs[:, u, j * D:(j + 1) * D], ident[:, :])
                                last.then_inc(S["turned"], 1)
                                pe.wait_ge(S["xsT"], i * 2 + u + 3)
                                pe.wait_ge(S["taken"], i * 2 + u + 1)
                                for j in range(GROUP):
                                    last = pe.matmul(pR[u][:, j * E1:(j + 1) * E1], xsT[:, u, j * P:(j + 1) * P],
                                                     gate_wT[:, :], start=True, stop=True)
                                last.then_inc(S["scores"], 1)

                    @block.scalar
                    def _(act):
                        act.sem_inc(S["xsT"], 2)
                        with act.Fori(0, GROUPS // 2) as i:
                            for u in range(2):
                                act.wait_ge(S["turned"], i * 2 + u + 3)
                                act.wait_ge(S["taken"], i * 2 + u + 1)
                                act.wait_ge(S["kept"], i * 2 + u + 1)
                                act.activation(xsT[:, u, :], pT[u][:, :], ACT.Copy).then_inc(S["xsT"], 1)

                with ExitStack() as st3:
                    def sb3(n, shape, dt=F32):
                        return st3.enter_context(nc.sbuf_tensor(uniq(n), shape, dt))
                    idx = sb3("idx", [P, TILES * E1])
                    m1, m2, k, w1, w2 = (sb3(n, [P, TILES]) for n in ("m1", "m2", "k", "w1", "w2"))
                    oh1, oh2, sc2 = (sb3(n, [P, TILES * E1]) for n in ("oh1", "oh2", "sc2"))
                    S = {n: semaphore(n) for n in ("c", "iota", "delta", "exp")}
                    block = st3.enter_context(nc.Block())
                    te = lambda t: t[:, :].rearrange("p (t e) -> p t e", e=E1)

                    @block.gpsimd
                    def _(pool):
                        pool.iota(te(idx), pattern=[[0, TILES], [-1, E1]], base=E1, channel_multiplier=0,
                                  allow_small_or_imprecise_dtypes=True).then_inc(S["iota"], 1)

                    @block.scalar
                    def _(act):
                        act.wait_ge(S["delta"], 1)
                        act.activation(w2[:, :], k[:, :], ACT.Exp).then_inc(S["exp"], 1)

                    @block.vector
                    def _(dve):
                        link = chain(dve, S["c"])
                        dve.wait_ge(S["iota"], 1)
                        top2(dve, None, link, SC, E1, (m1, m2, k, oh1, oh2, sc2), idx)
                        dve.tensor_tensor(k[:, :], m2[:, :], m1[:, :], ALU.subtract).then_inc(S["delta"], 1)
                        dve.wait_ge(S["exp"], 1)
                        link(dve.tensor_scalar(w1[:, :], w2[:, :], 1.0, None, ALU.add))
                        link(dve.reciprocal(w1[:, :], w1[:, :]))
                        link(dve.tensor_tensor(w2[:, :], w2[:, :], w1[:, :], ALU.mult))
                        up = lambda t: t[:, :].unsqueeze(2).broadcast_to([P, TILES, E1])
                        link(dve.tensor_tensor(te(oh1), te(oh1), up(w1), ALU.mult))
                        link(dve.tensor_tensor(te(oh2), te(oh2), up(w2), ALU.mult))
                        dve.tensor_tensor(SC[:, :], oh1[:, :], oh2[:, :], ALU.add)

                with ExitStack() as st3:
                    def sb3(n, shape, dt=F32):
                        return st3.enter_context(nc.sbuf_tensor(uniq(n), shape, dt))
                    CH = ER // P
                    gates = sb3("gates", [P, 2, GROUP * ER])
                    hid = sb3("hid", [P, 2, GW])
                    gated = sb3("gated", [P, 4, GW])
                    pU, pG, pO = ([st3.enter_context(nc.psum_tensor(uniq(n), [P, 512], F32)) for _ in range(2)] for n in ("pU", "pG", "pO"))
                    S = {n: semaphore(n) for n in ("gates", "up", "gelu", "gated", "out", "taken")}
                    block = st3.enter_context(nc.Block())
                    UN = 2
                    LAG = 2
                    KS = UN * CH

                    @block.gpsimd
                    def _(pool):
                        with pool.Fori(0, GROUPS // UN) as i:
                            for u in range(UN):
                                pool.wait_ge(S["up"], i * KS + u * CH + CH)
                                g1 = SC[:, bass.ds(i * (UN * GROUP * E1) + u * GROUP * E1, GROUP * E1)]
                                pool.tensor_copy(gates[:, u, :].rearrange("p (e r) -> p e r", r=R1),
                                                 g1.unsqueeze(2).broadcast_to([P, GROUP * E1, R1])).then_inc(S["gates"], 1)

                    @block.tensor
                    def _(pe):
                        pe.sem_inc(S["up"], 2 * CH)
                        pe.sem_inc(S["out"], 4)
                        with pe.Fori(0, GROUPS // UN) as i:
                            def up(kk):
                                g, c = kk // CH, kk % CH
                                if c == 0:
                                    pe.wait_ge(S["gates"], i * UN + g + 1)
                                pe.wait_ge(S["gated"], i * KS + kk + 1)
                                pe.matmul(pU[kk % 2][:, :], up1T[:, c * P:(c + 1) * P],
                                          XNT[:, bass.ds(i * (UN * GW) + g * GW, GW)], start=True, stop=True)
                                for j in range(GROUP):
                                    gs = gates[:, g, j * ER + c * P:j * ER + (c + 1) * P]
                                    last = pe.transpose(pG[kk % 2][:, j * P:(j + 1) * P], gs, ident[:, :])
                                last.then_inc(S["up"], 1)

                            def down(kk):
                                g, c = kk // CH, kk % CH
                                pe.wait_ge(S["gated"], i * KS + kk + 3)
                                if c == 0:
                                    pe.wait_ge(S["taken"], i * UN + g + 1)
                                for j in range(GROUP):
                                    last = pe.matmul(pO[g % 2][:, j * D:(j + 1) * D], gated[:, kk % 4, j * P:(j + 1) * P],
                                                     down1T[:, c * P:(c + 1) * P], start=(c == 0 and j == 0),
                                                     stop=(c == CH - 1), skip_group_check=True)
                                last.then_inc(S["out"], 1)

                            for kk in range(KS + LAG):
                                if kk < KS:
                                    up(kk)
                                if kk >= LAG:
                                    down(kk - LAG)

                    @block.scalar
                    def _(act):
                        act.preload_act_table_set("gelu_and_others")
                        with act.Fori(0, GROUPS // UN) as i:
                            for kk in range(KS):
                                act.wait_ge(S["up"], i * KS + kk + 2 * CH + 1)
                                act.wait_ge(S["gated"], i * KS + kk + 1)
                                act.activation(hid[:, kk % 2, :], pU[kk % 2][:, :], ACT.Gelu).then_inc(S["gelu"], 1)

                    @block.vector
                    def _(dve):
                        dve.sem_inc(S["gated"], 2)
                        dve.sem_inc(S["taken"], 2)
                        with dve.Fori(0, GROUPS // UN) as i:
                            def onto_x(g):
                                dve.wait_ge(S["out"], i * KS + (g + 1) * CH + 4)
                                xv = X[:, bass.ds(i * (UN * GW) + g * GW, GW)]
                                dve.tensor_tensor(xv, xv, pO[g % 2][:, :], ALU.add).then_inc(S["taken"], 1)
                            for kk in range(KS):
                                dve.wait_ge(S["gelu"], i * KS + kk + 1)
                                dve.wait_ge(S["out"], i * KS + kk + 1)
                                dve.tensor_tensor(gated[:, kk % 4, :], hid[:, kk % 2, :], pG[kk % 2][:, :], ALU.mult).then_inc(S["gated"], 1)
                                if kk >= CH + LAG and (kk - LAG) % CH == 0:
                                    onto_x((kk - LAG) // CH - 1)
                            onto_x(UN - 1)

        def l0_attn():
            norm_stats(X, LN_EPS)
            W = 2 * T
            with ExitStack() as st:
                def sb3(n, shape, dt=F32):
                    return st.enter_context(nc.sbuf_tensor(uniq(n), shape, dt))
                wp = sb3("wp", [D, 6 * D])
                wo = sb3("wo", [D, D])
                wf1 = sb3("wf1", [D, FF])
                wf2 = sb3("wf2", [P, 4 * D])
                cols = sb3("cols", [P, 2])
                b1c = sb3("b1c", [P, 4])
                rows = {n: sb3(n, [P, D]) for n in ("ln1_scale", "ln1_bias", "b2", "ln2_scale", "ln2_bias")}
                first = sb3("first", [P, W])
                halfpi = sb3("halfpi", [P, 1])
                with ExitStack() as st3:
                    def t(n, shape=None, dt=F32):
                        return st3.enter_context(nc.sbuf_tensor(uniq(n), shape or [P, W], dt))
                    xs, xT, q, k, g, ar, ai, s1, s2, kv = (t(n) for n in ("xs", "xT", "q", "k", "g", "ar", "ai", "s1", "s2", "kv"))
                    den, tt, hx, hy, ph, r, sg, th, sn, cs = (t(n) for n in ("den", "tt", "hx", "hy", "ph", "r", "sg", "th", "sn", "cs"))
                    ur, ui, yr, yi, ta, aar, aai = (t(n) for n in ("ur", "ui", "yr", "yi", "ta", "aar", "aai"))
                    sums = t("sums", [P, 8])
                    mean = t("mean", [P, 8])
                    gn = t("gn", [P, 6])
                    pT, pq, pk, pv, par, pai, pg, pW = (st3.enter_context(nc.psum_tensor(uniq("p"), [P, 512], F32)) for _ in range(8))
                    S = {n: semaphore(n) for n in
                         ("w", "fi", "xs", "kept", "turned", "xT", "proj", "copied", "d", "mag2", "mag", "ang", "at", "turns", "trig",
                          "y", "sq", "sums", "mean", "var", "std", "z", "wo")}
                    block = st3.enter_context(nc.Block())
                    col = lambda ap: ap.rearrange("(p o) -> p o", o=1)
                    loads = [(wp[:, n * D:(n + 1) * D], a["L0_attn_" + w]) for n, w in enumerate(("Wq", "Wk", "Wv"))]
                    loads += [(wp[:, 3 * D:5 * D], a["L0_attn_Wa"]), (wp[:, 5 * D:6 * D], a["L0_attn_Wg"]), (wo[:, :], a["L0_attn_Wo"]),
                              (wf1[:, :], a["L0_attn_W1"]),
                              (wf2[:, :].rearrange("p (c d) -> p c d", d=D), a["L0_attn_W2"].rearrange("(c p) d -> p c d", p=P)),
                              (cols[:, 0:1], col(a["L0_attn_gn_scale"])), (cols[:, 1:2], col(a["L0_attn_gn_bias"])),
                              (b1c[:, :], a["L0_attn_b1"].rearrange("(c p) -> p c", p=P))]
                    loads += [(rows[n][:, :], row_to_all(a["L0_attn_" + n], D)) for n in rows]

                    @block.sync
                    def _(sp):
                        with nc.allow_non_contiguous_dma(reason="a few columns of 4 bytes"):
                            for dst, src in loads:
                                sp.dma_start(dst, src).then_inc(S["w"], 16)

                    @block.gpsimd
                    def _(pool):
                        pool.memset(halfpi[:, :], PI / 2)
                        pool.memset(first[:, :], 1.0).then_inc(S["fi"], 1)
                        pool.wait_ge(S["fi"], 1)
                        pool.memset(first[:, 0:W:T], 0.0).then_inc(S["fi"], 1)
                        with pool.Fori(0, GROUPS) as i:
                            pool.wait_ge(S["xs"], i + 1)
                            pool.tensor_copy(XN[:, bass.ds(i * GW, GW)], xs[:, :]).then_inc(S["kept"], 1)

                    @block.tensor
                    def _(pe):
                        pe.wait_ge(S["w"], 16 * len(loads))
                        with pe.Fori(0, GROUPS) as i:
                            pe.wait_ge(S["xs"], i + 1)
                            for j in range(GROUP):
                                last = pe.transpose(pT[:, j * P:(j + 1) * P], xs[:, j * D:(j + 1) * D], ident[:, :])
                            last.then_inc(S["turned"], 1)
                            pe.wait_ge(S["xT"], i + 1)
                            for n, p in enumerate((pq, pk, pv, par, pai, pg)):
                                last = pe.matmul(p[:, :], wp[:, n * D:(n + 1) * D], xT[:, :], start=True, stop=True)
                            last.then_inc(S["proj"], 1)
                            pe.wait_ge(S["sq"], i + 1)
                            pe.wait_ge(S["y"], i + 1)
                            pe.matmul(pT[:, 0:8], blockg[:, :], sums[:, :], start=True, stop=True).then_inc(S["mean"], 1)
                            pe.wait_ge(S["z"], i + 1)
                            for j in range(GROUP):
                                last = pe.matmul(pW[:, j * D:(j + 1) * D], yr[:, j * P:(j + 1) * P], wo[:, :], start=True, stop=True)
                            last.then_inc(S["wo"], 1)

                    @block.scalar
                    def _(act):
                        act.wait_ge(S["fi"], 2)
                        with act.Fori(0, GROUPS) as i:
                            act.wait_ge(S["turned"], i + 1)
                            act.activation(xT[:, :], pT[:, :], ACT.Copy).then_inc(S["xT"], 1)
                            act.wait_ge(S["proj"], i + 1)
                            act.activation(s1[:, :], par[:, :], ACT.Square)
                            act.activation(s2[:, :], pai[:, :], ACT.Square).then_inc(S["copied"], 1)
                            act.activation(aar[:, :], par[:, :], ACT.Abs)
                            act.activation(aai[:, :], pai[:, :], ACT.Abs)
                            for dst, p in ((ar, par), (ai, pai), (k, pk), (q, pq), (g, pg)):
                                last = act.activation(dst[:, :], p[:, :], ACT.Copy)
                            last.then_inc(S["copied"], 1)
                            act.preload_act_table_set("sqrt_and_others")
                            act.wait_ge(S["mag2"], i + 1)
                            act.activation(s1[:, :], s1[:, :], ACT.Sqrt).then_inc(S["mag"], 1)
                            act.preload_act_table_set("sigmoid_and_others")
                            act.wait_ge(S["mag"], i + 1)
                            act.wait_ge(S["copied"], i * 2 + 2)
                            act.activation(r[:, :], s1[:, :], ACT.Sigmoid)
                            act.activation(sg[:, :], g[:, :], ACT.Sigmoid)
                            act.wait_ge(S["ang"], i + 1)
                            act.activation(tt[:, :], tt[:, :], ACT.Arctan).then_inc(S["at"], 1)
                            act.preload_act_table_set("trig_and_small")
                            act.wait_ge(S["turns"], i + 1)
                            act.activation(sn[:, :], th[:, :], ACT.Sin, scale=TURN)
                            act.activation(cs[:, :], ph[:, :], ACT.Sin, scale=-TURN, bias=halfpi[:, 0:1]).then_inc(S["trig"], 1)
                            act.wait_ge(S["y"], i + 1)
                            for n, (y, junk) in enumerate(((yr, s2), (yi, aai))):
                                for h in range(2):
                                    last = act.activation(junk[:, h * T:(h + 1) * T], y[:, h * T:(h + 1) * T], ACT.Square,
                                                          accum_out=sums[:, 4 + 2 * n + h:5 + 2 * n + h])
                            last.then_inc(S["sq"], 1)
                            act.preload_act_table_set("sqrt_and_others")
                            act.wait_ge(S["var"], i + 1)
                            act.activation(gn[:, 0:2], gn[:, 0:2], ACT.Sqrt).then_inc(S["std"], 1)

                    @block.vector
                    def _(dve):
                        dve.wait_ge(S["w"], 16 * len(loads))
                        dve.wait_ge(S["fi"], 2)
                        STEPS = 24
                        with dve.Fori(0, GROUPS) as i:
                            count = [0]

                            def link(ins):
                                count[0] += 1
                                ins.then_inc(S["d"], 1)
                                dve.wait_ge(S["d"], i * STEPS + count[0])
                            f = lambda x: x[:, :]
                            norm_tiles(dve, lambda j: xs[:, j * D:(j + 1) * D], X, i * GW, i * (2 * GROUP)).then_inc(S["xs"], 1)
                            dve.wait_ge(S["copied"], i * 2 + 1)
                            dve.scalar_tensor_tensor(f(s1), f(s1), 1e-36, f(s2), ALU.add, ALU.add).then_inc(S["mag2"], 1)
                            dve.wait_ge(S["copied"], i * 2 + 2)
                            dve.tensor_scalar(f(hx), f(ar), 0.0, 0.5, ALU.is_ge, ALU.subtract)
                            dve.tensor_scalar(f(hy), f(ai), 0.0, 0.5, ALU.is_ge, ALU.subtract)
                            dve.tensor_tensor(f(kv), f(k), pv[:, :], ALU.mult)
                            dve.wait_ge(S["mag"], i + 1)
                            link(dve.tensor_tensor(f(den), f(aar), f(s1), ALU.add))
                            link(dve.reciprocal(f(den), f(den)))
                            dve.tensor_tensor(f(tt), f(aai), f(den), ALU.mult).then_inc(S["ang"], 1)
                            dve.wait_ge(S["at"], i + 1)
                            link(dve.tensor_scalar(f(tt), f(tt), 4.0 / PI, -1.0, ALU.mult, ALU.add))
                            link(dve.tensor_tensor(f(tt), f(tt), f(hx), ALU.mult))
                            link(dve.scalar_tensor_tensor(f(tt), f(tt), 0.5, f(hy), ALU.add, ALU.mult))
                            link(dve.tensor_tensor_scan(f(th), f(first), f(tt), 0.0, ALU.mult, ALU.add))
                            link(dve.tensor_scalar(f(ta), f(th), MAGIC, MAGIC, ALU.add, ALU.subtract))
                            link(dve.tensor_tensor(f(th), f(th), f(ta), ALU.subtract))
                            link(dve.tensor_scalar(f(ph), f(th), -1.0, None, ALU.mult))
                            dve.tensor_tensor(f(ph), f(ph), f(th), ALU.max).then_inc(S["turns"], 1)
                            dve.wait_ge(S["trig"], i + 1)
                            link(dve.tensor_tensor(f(r), f(r), f(first), ALU.mult))
                            dve.tensor_tensor(f(ar), f(kv), f(cs), ALU.mult)
                            link(dve.scalar_tensor_tensor(f(ai), f(kv), -1.0, f(sn), ALU.mult, ALU.mult))
                            dve.tensor_tensor_scan(f(ur), f(r), f(ar), 0.0, ALU.mult, ALU.add)
                            dve.tensor_tensor_scan(f(ui), f(r), f(ai), 0.0, ALU.mult, ALU.add)
                            dve.tensor_tensor(f(cs), f(cs), f(q), ALU.mult)
                            link(dve.tensor_tensor(f(sn), f(sn), f(q), ALU.mult))
                            dve.tensor_tensor(f(yr), f(cs), f(ur), ALU.mult)
                            dve.tensor_tensor(f(yi), f(cs), f(ui), ALU.mult)
                            dve.tensor_tensor(f(ta), f(sn), f(ui), ALU.mult)
                            link(dve.tensor_tensor(f(ar), f(sn), f(ur), ALU.mult))
                            dve.tensor_tensor(f(yr), f(yr), f(ta), ALU.subtract)
                            link(dve.tensor_tensor(f(yi), f(yi), f(ar), ALU.add))
                            seq = lambda x: x[:, :].rearrange("p (s t) -> p s t", s=2)
                            dve.tensor_reduce(sums[:, 0:2], seq(yr), AX.X, ALU.add)
                            dve.tensor_reduce(sums[:, 2:4], seq(yi), AX.X, ALU.add).then_inc(S["y"], 1)
                            link(dve.tensor_tensor(f(g), f(g), f(sg), ALU.mult))
                            dve.wait_ge(S["mean"], i + 1)
                            link(dve.tensor_copy(mean[:, :], pT[:, 0:8]))
                            link(dve.tensor_tensor(gn[:, 2:6], mean[:, 0:4], mean[:, 0:4], ALU.mult))
                            link(dve.tensor_tensor(gn[:, 2:6], mean[:, 4:8], gn[:, 2:6], ALU.subtract))
                            dve.scalar_tensor_tensor(gn[:, 0:2], gn[:, 2:4], EPS, gn[:, 4:6], ALU.add, ALU.add).then_inc(S["var"], 1)
                            dve.wait_ge(S["std"], i + 1)
                            link(dve.reciprocal(gn[:, 0:2], gn[:, 0:2]))
                            link(dve.tensor_scalar(gn[:, 0:2], gn[:, 0:2], cols[:, 0:1], None, ALU.mult))
                            link(dve.tensor_tensor(gn[:, 2:4], mean[:, 0:2], gn[:, 0:2], ALU.mult))
                            link(dve.tensor_scalar(gn[:, 2:4], gn[:, 2:4], -1.0, cols[:, 1:2], ALU.mult, ALU.add))
                            for h in range(2):
                                l = dve.tensor_scalar(yr[:, h * T:(h + 1) * T], yr[:, h * T:(h + 1) * T], gn[:, h:h + 1],
                                                      gn[:, 2 + h:3 + h], ALU.mult, ALU.add)
                            link(l)
                            dve.tensor_tensor(f(yr), f(yr), f(g), ALU.mult).then_inc(S["z"], 1)
                            dve.wait_ge(S["wo"], i + 1)
                            dve.wait_ge(S["kept"], i + 1)
                            xv = XN[:, bass.ds(i * GW, GW)]
                            link(dve.tensor_tensor(xv, xv, pW[:, :], ALU.add))
                            assert count[0] == STEPS

                norm_stats(XN, EPS)
                with ExitStack() as st3:
                    def t(n, shape=None, dt=F32):
                        return st3.enter_context(nc.sbuf_tensor(uniq(n), shape or [P, W], dt))
                    x1 = t("x1", [P, 2, W])
                    x1T = t("x1T", [P, 2, W])
                    hid = t("hid", [P, 4, W])
                    pT, pU, pO = ([st3.enter_context(nc.psum_tensor(uniq(n), [P, 512], F32)) for _ in range(2)] for n in ("pT", "pU", "pO"))
                    S = {n: semaphore(n) for n in ("d", "x1", "turned", "x1T", "up", "gelu", "down")}
                    block = st3.enter_context(nc.Block())
                    over = lambda n: rows[n][:, :].unsqueeze(1).broadcast_to([P, GROUP, D])

                    @block.vector
                    def _(dve):
                        def normed(c, base, g, u):
                            v = x1[:, u, :].rearrange("p (t d) -> p t d", d=D)
                            ln = chain(dve, S["d"], base)
                            ln(norm_tiles(dve, lambda j: x1[:, u, j * D:(j + 1) * D], XN, c, g))
                            ln(dve.tensor_tensor(v, v, over("ln1_scale"), ALU.mult))
                            dve.tensor_tensor(v, v, over("ln1_bias"), ALU.add).then_inc(S["x1"], 1)

                        def finish(i, base, c, u):
                            v = x1[:, u, :].rearrange("p (t d) -> p t d", d=D)
                            ln = chain(dve, S["d"], base)
                            dve.wait_ge(S["down"], i * 8 + 4 * u + 8)
                            ln(dve.tensor_tensor(v, v, over("b2"), ALU.add))
                            ln(dve.tensor_tensor(XN[:, bass.ds(c, GW)], x1[:, u, :], pO[u][:, :], ALU.add))

                        with dve.Fori(0, GROUPS // 2) as i:
                            normed(i * (2 * GW), i * 8, i * (4 * GROUP), 0)
                            normed(i * (2 * GW) + GW, i * 8 + 2, i * (4 * GROUP) + 2 * GROUP, 1)
                            finish(i, i * 8 + 4, i * (2 * GW), 0)
                            finish(i, i * 8 + 6, i * (2 * GW) + GW, 1)

                    @block.tensor
                    def _(pe):
                        pe.sem_inc(S["down"], 4)
                        with pe.Fori(0, GROUPS // 2) as i:
                            for u in range(2):
                                pe.wait_ge(S["x1"], i * 2 + u + 1)
                                for j in range(GROUP):
                                    last = pe.transpose(pT[u][:, j * P:(j + 1) * P], x1[:, u, j * D:(j + 1) * D], ident[:, :])
                                last.then_inc(S["turned"], 1)
                            KS = 8

                            def up(kk):
                                g, c = kk // 4, kk % 4
                                if c == 0:
                                    pe.wait_ge(S["x1T"], i * 2 + g + 1)
                                pe.wait_ge(S["gelu"], i * KS + kk + 1)
                                pe.matmul(pU[kk % 2][:, :], wf1[:, c * P:(c + 1) * P], x1T[:, g, :], start=True, stop=True).then_inc(S["up"], 1)

                            def down(kk):
                                g, c = kk // 4, kk % 4
                                pe.wait_ge(S["gelu"], i * KS + kk + 3)
                                for j in range(GROUP):
                                    last = pe.matmul(pO[g][:, j * D:(j + 1) * D], hid[:, c, j * P:(j + 1) * P],
                                                     wf2[:, c * D:(c + 1) * D], start=(c == 0 and j == 0), stop=(c == 3),
                                                     skip_group_check=True)
                                last.then_inc(S["down"], 1)
                            for kk in range(KS + 1):
                                if kk < KS:
                                    up(kk)
                                if kk >= 1:
                                    down(kk - 1)

                    @block.scalar
                    def _(act):
                        act.sem_inc(S["gelu"], 2)
                        act.preload_act_table_set("gelu_apprx_tanh_and_others")
                        with act.Fori(0, GROUPS // 2) as i:
                            for u in range(2):
                                act.wait_ge(S["turned"], i * 2 + u + 1)
                                act.activation(x1T[:, u, :], pT[u][:, :], ACT.Copy).then_inc(S["x1T"], 1)
                            for kk in range(8):
                                act.wait_ge(S["up"], i * 8 + kk + 1)
                                act.wait_ge(S["down"], i * 8 + kk + 1)
                                act.activation(hid[:, kk % 4, :], pU[kk % 2][:, :], ACT.Gelu_apprx_tanh,
                                               bias=b1c[:, kk % 4:kk % 4 + 1]).then_inc(S["gelu"], 1)

                norm_stats(XN, EPS)
                with ExitStack() as st3:
                    ys = st3.enter_context(nc.sbuf_tensor(uniq("ys"), [P, 2, GW], F32))
                    S = {n: semaphore(n) for n in ("n", "scaled", "biased", "d")}
                    block = st3.enter_context(nc.Block())

                    @block.vector
                    def _(dve):
                        with dve.Fori(0, GROUPS // 2) as i:
                            link = chain(dve, S["d"], i * 8)
                            for u in range(2):
                                c = i * (2 * GW) + u * GW
                                v = ys[:, u, :].rearrange("p (t d) -> p t d", d=D)
                                over = lambda n: rows[n][:, :].unsqueeze(1).broadcast_to([P, GROUP, D])
                                link(norm_tiles(dve, lambda j: ys[:, u, j * D:(j + 1) * D], XN, c, i * (4 * GROUP) + u * 2 * GROUP))
                                link(dve.tensor_tensor(v, v, over("ln2_scale"), ALU.mult))
                                link(dve.tensor_tensor(v, v, over("ln2_bias"), ALU.add))
                                link(dve.tensor_tensor(X[:, bass.ds(c, GW)], X[:, bass.ds(c, GW)], ys[:, u, :], ALU.add))

        def l1_attn():
            norm_stats(X, LN_EPS)
            SCALE = float(HD) ** -0.5
            QT = T // P
            units = [(0, h, 4) for h in range(0, HEADS, 4)] + [(1, h, 2) for h in range(0, HEADS, 2)]
            NU = len(units)
            with ExitStack() as st3:
                def t(n, shape, dt=F32):
                    return st3.enter_context(nc.sbuf_tensor(uniq(n), shape, dt))
                xs = t("xs", [P, QT * D])
                xT = t("xT", [P, T])
                kS = t("kS", [P, T])
                Qm = t("Qm", [P, 4, T])
                hm = t("hm", [P, 4])
                Vx = t("Vx", [P, QT, HEADS, VW])
                dif = t("dif", [P, 3, 512])
                ET = t("ET", [P, 3, 512])
                mx = t("mx", [P, 2, 4])
                MC = t("MC", [P, QT, HEADS])
                O = t("O", [P, QT, HEADS, VW])
                Vall = t("Vall", [P, HEADS * VW])
                rs = t("rs", [P, QT, HEADS])
                att = t("att", [P, QT * D])
                attT = t("attT", [P, T])
                low = t("low", [P, HEADS])
                neg100 = t("neg100", [P, 1])
                mask2 = t("mask2", [P, T], BF16)
                pS, pX = ([st3.enter_context(nc.psum_tensor(uniq(n), [P, 512], F32)) for _ in range(2)] for n in ("pS", "pX"))
                pO, pA, pB, pT = (st3.enter_context(nc.psum_tensor(uniq(n), [P, 512], F32)) for n in ("pO", "pA", "pB", "pT"))
                S = {n: semaphore(n) for n in
                     ("c0", "xs", "turned", "xT", "qk", "v", "q", "vx", "s", "max", "mc", "dif", "min", "xp", "exp", "pv", "low", "d", "att", "attT", "attTs", "out", "x")}
                block = st3.enter_context(nc.Block())
                VN = HEADS * VW

                @block.gpsimd
                def _(pool):
                    pool.memset(neg100[:, :], -100.0)
                    pool.memset(Vx[:, :, :, :], 1.0)
                    pool.memset(mask2[:, 0:P], 0.0)
                    pool.tensor_copy(mask2[:, P:T], causal_b[:, :])
                    pool.tensor_scalar(hm[:, :], headmask[:, :], SCALE, None, ALU.mult).then_inc(S["c0"], 1)
                @block.tensor
                def _(pe):
                    pe.wait_ge(S["c0"], 1)
                    with pe.Fori(0, B) as b:
                        pe.wait_ge(S["xs"], b + 1)
                        for j in range(QT):
                            last = pe.transpose(pT[:, j * P:(j + 1) * P], xs[:, j * D:(j + 1) * D], ident[:, :])
                        last.then_inc(S["turned"], 1)
                        pe.wait_ge(S["xT"], b + 1)
                        pe.matmul(pA[:, 0:T], qkvT[:, 0:D], xT[:, :], start=True, stop=True)
                        pe.matmul(pA[:, T:2 * T], qkvT[:, D:2 * D], xT[:, :], start=True, stop=True).then_inc(S["qk"], 1)
                        for j in range(QT):
                            last = pe.matmul(pB[:, j * D:(j + 1) * D], xT[:, j * P:(j + 1) * P], qkvT[:, 2 * D:3 * D], start=True, stop=True)
                        last.then_inc(S["v"], 1)
                        pe.wait_ge(S["vx"], b + 1)
                        vrow = lambda j: Vx[:, j, :, :].rearrange("p h w -> p (h w)")
                        pe.matmul(pO[:, 2 * VN:3 * VN], ones[:, :], vrow(1), start=True, stop=True)
                        pe.matmul(pB[:, 2 * D:2 * D + VN], ones[:, :], vrow(0), start=True, stop=False)
                        pe.matmul(pB[:, 2 * D:2 * D + VN], ones[:, :], vrow(1), start=False, stop=True)
                        pe.wait_ge(S["q"], b + 1)

                        def scores(n):
                            qt, h0, nh = units[n]
                            K = P * (qt + 1)
                            pe.wait_ge(S["dif"], b * NU + n + 1)
                            rhs = mask2[:, T - K:T].unsqueeze(1).broadcast_to([P, nh, K])
                            pe.matmul(pS[n % 2][:, :], ident_b[:, :], rhs, start=True, stop=False, skip_group_check=True)
                            for m in range(nh):
                                h = h0 + m
                                r0 = 32 * (h // 4)
                                last = pe.matmul(pS[n % 2][:, m * K:(m + 1) * K], Qm[r0:r0 + 32, h % 4, qt * P:(qt + 1) * P],
                                                 kS[r0:r0 + 32, 0:K], start=False, stop=(m == nh - 1), skip_group_check=True)
                            last.then_inc(S["s"], 1)

                        def turn(n):
                            pe.wait_ge(S["min"], b * NU + n + 1)
                            pe.wait_ge(S["exp"], b * NU + n + 1)
                            for m in range(4):
                                last = pe.transpose(pX[n % 2][:, m * P:(m + 1) * P], dif[:, n % 3, m * P:(m + 1) * P], ident[:, :])
                            last.then_inc(S["xp"], 1)

                        def values(n):
                            qt, h0, nh = units[n]
                            pe.wait_ge(S["exp"], b * NU + n + 3)
                            for m in range(nh):
                                h = h0 + m
                                for kt in range(qt + 1):
                                    last = pe.matmul(pO[:, qt * VN + h * VW:qt * VN + (h + 1) * VW],
                                                     ET[:, n % 3, (m * (qt + 1) + kt) * P:(m * (qt + 1) + kt + 1) * P],
                                                     Vx[:, kt, h, :], start=(kt == 0), stop=(kt == qt))
                            last.then_inc(S["pv"], 1)
                        for n in range(NU + 4):
                            if n < NU:
                                scores(n)
                            if 2 <= n < NU + 2:
                                turn(n - 2)
                            if n >= 4:
                                values(n - 4)
                        pe.wait_ge(S["att"], b + 1)
                        for j in range(QT):
                            last = pe.transpose(pT[:, j * P:(j + 1) * P], att[:, j * D:(j + 1) * D], ident[:, :])
                        last.then_inc(S["attT"], 1)
                        pe.wait_ge(S["attTs"], b + 1)
                        for j in range(QT):
                            last = pe.matmul(pB[:, j * D:(j + 1) * D], attT[:, j * P:(j + 1) * P], projT[:, :], start=True, stop=True)
                        last.then_inc(S["out"], 1)

                @block.scalar
                def _(act):
                    act.sem_inc(S["exp"], 2)
                    act.preload_act_table_set("exp_and_others")
                    act.wait_ge(S["c0"], 1)
                    with act.Fori(0, B) as b:
                        act.wait_ge(S["turned"], b + 1)
                        act.activation(xT[:, :], pT[:, 0:T], ACT.Copy).then_inc(S["xT"], 1)
                        act.wait_ge(S["qk"], b + 1)
                        act.activation(kS[:, :], pA[:, T:2 * T], ACT.Copy)
                        for j in range(4):
                            last = act.activation(Qm[:, j, :], pA[:, 0:T], ACT.Copy, scale=hm[:, j:j + 1])
                        last.then_inc(S["q"], 1)
                        for n in range(NU):
                            act.wait_ge(S["xp"], b * NU + n + 4)
                            act.wait_ge(S["pv"], b * NU + n + 1)
                            act.activation(ET[:, n % 3, :], pX[n % 2][:, :], ACT.Exp).then_inc(S["exp"], 1)
                        act.wait_ge(S["mc"], b + 1)
                        act.activation(low[:, :], MC[:, 0, :], ACT.Exp, scale=-1.0, bias=neg100[:, 0:1]).then_inc(S["low"], 1)
                        act.wait_ge(S["attT"], b + 1)
                        act.activation(attT[:, :], pT[:, 0:T], ACT.Copy).then_inc(S["attTs"], 1)

                @block.vector
                def _(dve):
                    dve.sem_inc(S["dif"], 2)
                    dve.sem_inc(S["xp"], 3)
                    dve.wait_ge(S["c0"], 1)
                    dve.sem_inc(S["pv"], 3)
                    STEPS = 8 + 2 * NU
                    with dve.Fori(0, B) as b:
                        link = chain(dve, S["d"], b * STEPS)
                        norm_tiles(dve, lambda j: xs[:, j * D:(j + 1) * D], X, b * (QT * D), b * (2 * QT), QT).then_inc(S["xs"], 1)
                        dve.wait_ge(S["v"], b + 1)
                        dve.tensor_copy(Vx[:, :, :, 0:HD], pB[:, 0:2 * D].rearrange("p (k h d) -> p k h d", k=QT, d=HD)).then_inc(S["vx"], 1)
                        for n, (qt, h0, nh) in enumerate(units):
                            dve.wait_ge(S["s"], b * NU + n + 1)
                            sc = pS[n % 2][:, :].rearrange("p (h k) -> p h k", h=nh)
                            link(dve.tensor_reduce(mx[:, n % 2, 0:nh], sc, AX.X, ALU.max))
                            link(dve.tensor_scalar(MC[:, qt, h0:h0 + nh], mx[:, n % 2, 0:nh], -100.0, 100.0, ALU.max, ALU.min))
                            dve.wait_ge(S["xp"], b * NU + n + 1)
                            dve.scalar_tensor_tensor(dif[:, n % 3, :].rearrange("p (h k) -> p h k", h=nh), sc, -100.0,
                                                     MC[:, qt, h0:h0 + nh].unsqueeze(2).broadcast_to([P, nh, P * (qt + 1)]),
                                                     ALU.max, ALU.subtract).then_inc(S["dif"], 1)
                            dve.wait_ge(S["dif"], b * NU + n + 3)
                            dve.tensor_scalar(dif[:, n % 3, :], dif[:, n % 3, :], 0.0, None, ALU.min).then_inc(S["min"], 1)
                        dve.sem_inc(S["mc"], 1)
                        dve.wait_ge(S["low"], b + 1)
                        dve.wait_ge(S["pv"], b * NU + NU + 3)
                        Of = lambda j: O[:, j, :, :].rearrange("p h w -> p (h w)")
                        hw = lambda ap: ap.rearrange("p (h w) -> p h w", w=VW)
                        link(dve.tensor_tensor(O[:, 0, :, :], hw(pO[:, 2 * VN:3 * VN]), low[:, :].unsqueeze(2).broadcast_to([P, HEADS, VW]), ALU.mult))
                        dve.tensor_tensor(Of(0), Of(0), pO[:, 0:VN], ALU.add)
                        dve.tensor_scalar(Vall[:, :], pB[:, 2 * D:2 * D + VN], 1e-8, None, ALU.mult)
                        link(dve.tensor_copy(Of(1), pO[:, VN:2 * VN]))
                        link(dve.tensor_scalar(rs[:, :, :], O[:, :, :, HD], 1e-6, None, ALU.add))
                        link(dve.reciprocal(rs[:, :, :], rs[:, :, :]))
                        for j in range(QT):
                            l = dve.tensor_tensor(O[:, j, :, :], O[:, j, :, :], rs[:, j, :].unsqueeze(2).broadcast_to([P, HEADS, VW]), ALU.mult)
                        link(l)
                        for j in range(QT):
                            l = dve.tensor_tensor(Of(j), Of(j), Vall[:, :], ALU.add)
                        link(l)
                        link(dve.reciprocal(rs[:, :, :], O[:, :, :, HD]))
                        for j in range(QT):
                            l = dve.tensor_tensor(att[:, j * D:(j + 1) * D].rearrange("p (h d) -> p h d", d=HD), O[:, j, :, 0:HD],
                                                  rs[:, j, :].unsqueeze(2).broadcast_to([P, HEADS, HD]), ALU.mult)
                        l.then_inc(S["att"], 1)
                        dve.wait_ge(S["out"], b + 1)
                        xv = X[:, bass.ds(b * (QT * D), QT * D)]
                        link(dve.tensor_tensor(xv, xv, pB[:, 0:2 * D], ALU.add))

        table = {"l0_ffn": l0_ffn, "l1_ffn": l1_ffn, "l0_attn": l0_attn, "l1_attn": l1_attn}
        end_stage()
        for s in stages:
            table[s]()
            end_stage()


        with ExitStack() as st:
            s_out = semaphore("s_out")
            block = st.enter_context(nc.Block())

            @block.sync
            def _(sp):
                sp.dma_start(out_tiles, X3).then_inc(s_out, 16)
                sp.wait_ge(s_out, 16)

_INS = ['L0_attn_x', 'L0_attn_Wq', 'L0_attn_Wk', 'L0_attn_Wv', 'L0_attn_Wa', 'L0_attn_Wg', 'L0_attn_Wo',
        'L0_attn_gn_scale', 'L0_attn_gn_bias', 'L0_attn_ln1_scale', 'L0_attn_ln1_bias', 'L0_attn_W1',
        'L0_attn_b1', 'L0_attn_W2', 'L0_attn_b2', 'L0_attn_ln2_scale', 'L0_attn_ln2_bias',
        'L0_ffn_router_w', 'L0_ffn_router_bias', 'L0_ffn_bank_mag', 'L0_ffn_bank_freq', 'L0_ffn_bank_phase',
        'L0_ffn_bank_down', 'L0_ffn_norm_w', 'L1_attn_w_qkv', 'L1_attn_w_proj', 'L1_ffn_Wg', 'L1_ffn_bg',
        'L1_ffn_W1', 'L1_ffn_W2']


def kernel(**inputs):
    import numpy as _np
    import concourse.bacc as _bacc
    from concourse import mybir as _mybir
    from concourse.bass_utils import run_bass_kernel_spmd as _run

    nc = _bacc.Bacc("TRN2", target_bir_lowering=False, num_devices=1)
    arrays, args = {}, {}
    for name in _INS:
        v = _np.ascontiguousarray(inputs[name])
        arrays[f"in_{name}_dram"] = v
        args[name] = nc.dram_tensor(f"in_{name}_dram", v.shape, _mybir.dt.from_np(v.dtype), kind="ExternalInput").ap()
    out = nc.dram_tensor("out_0_dram", (B, T, D), _mybir.dt.from_np(_np.dtype("float32")), kind="ExternalOutput").ap()
    macaron_kernel(nc, args, out)
    r = _run(nc, [arrays], core_ids=[0])
    return r.results[0]["out_0_dram"]
```

```python
from contextlib import ExitStack

import concourse.bass as bass
from concourse import mybir

F32 = mybir.dt.float32
BF16 = mybir.dt.bfloat16
I32 = mybir.dt.int32
U32 = mybir.dt.uint32
ALU = mybir.AluOpType
ACT = mybir.ActivationFunctionType
AX = mybir.AxisListType

P = 128
D = 128
B, T = 32, 256
N = B * T
TILES = N // P
GROUP = 4
GW = GROUP * D
GROUPS = TILES // GROUP
LN_EPS = 1e-5
EPS = 1e-6
MAGIC = 1.5 * 2.0 ** 23
PI = 3.141592653589793
TURN = 6.283185

E0, H0 = 16, 256
UNITS = 144
BATCH = 4
NBATCH = UNITS // BATCH
PADDED = UNITS + 2 * BATCH
SLOTS = PADDED * P
E1, R1 = 8, 64
ER = E1 * R1
FF = 512
GN_GROUP = 4
HEADS, HD = 16, 8
VW = HD + 1
SEM0 = 120
NEG = -1e30


ALL = ("l0_ffn", "l0_attn", "l0_ffn", "l1_ffn", "l1_attn", "l1_ffn")


def macaron_kernel(nc, a, out, stages=ALL):
    ctx = ExitStack()
    names = [0]

    def uniq(n):
        names[0] += 1
        return f"{n}_{names[0]}"

    def dram(n, shape, dt=F32):
        return nc.dram_tensor(uniq(n), shape, dt, kind="Internal").ap()

    def chain(eng, sem, base=0):
        count = [0]

        def link(ins):
            count[0] += 1
            ins.then_inc(sem, 1)
            eng.wait_ge(sem, base + count[0])
        return link

    with ctx:
        def sb(n, shape, dt=F32):
            return ctx.enter_context(nc.sbuf_tensor(uniq(n), shape, dt))

        stage_sems = []

        def semaphore(n):
            stage_sems.append(nc.alloc_semaphore(name=uniq(n), num=SEM0 + len(stage_sems)))
            return stage_sems[-1]

        def gather_semaphore(n):
            return nc.alloc_semaphore(name=uniq(n))

        def end_stage():
            nc.all_engine_barrier(sems_to_clear=range(SEM0, SEM0 + len(stage_sems)))
            for s in stage_sems:
                nc.release_semaphore(s)
            stage_sems.clear()

        X = sb("X", [P, TILES * D])
        XN = sb("XN", [P, TILES * D])
        ident = sb("ident", [P, P])
        ident_b = sb("ident_b", [P, P], BF16)
        ones = sb("ones", [P, P])
        ones_b = sb("ones_b", [P, P], BF16)
        strict_b = sb("strict_b", [P, P], BF16)
        strict = sb("strict", [P, P])
        causal_b = sb("causal_b", [P, P], BF16)
        blockg = sb("blockg", [P, P])
        router_wT = sb("router_wT", [D, E0])
        gate_wT = sb("gate_wT", [D, E1])
        up1T = sb("up1T", [D, ER])
        down1T = sb("down1T", [P, ER])
        qkvT = sb("qkvT", [D, 3 * D])
        projT = sb("projT", [D, D])
        rbias = sb("rbias", [P, E0])
        gbias = sb("gbias", [P, E1])
        norm_w = sb("norm_w", [P, D])
        MV = sb("MV", [P, TILES * 2])
        MV2 = MV[:, :].rearrange("p (t k) -> p t k", k=2)
        headmask = sb("headmask", [P, GROUP])

        x_tiles = a["L0_attn_x"].rearrange("b t d -> (b t) d").rearrange("(t p) d -> p t d", p=P)
        out_tiles = out.rearrange("b t d -> (b t) d").rearrange("(t p) d -> p t d", p=P)
        X3 = X[:, :].rearrange("p (t d) -> p t d", d=D)

        def row_to_all(ap, n):
            return ap.rearrange("(o n) -> o n", o=1).broadcast_to([P, n])

        with ExitStack() as st:
            raw = {}
            for n, shape in (("rw", [E0, D]), ("gw", [E1, D]), ("w1", [P, 4, D]), ("w2", [D, ER]),
                             ("qkv", [P, 3, D]), ("proj", [D, D])):
                raw[n] = st.enter_context(nc.sbuf_tensor(uniq("raw_" + n), shape, F32))
            turned = [st.enter_context(nc.psum_tensor(uniq("turned"), [P, 512], F32)) for _ in range(4)]
            s_in = semaphore("s_in")
            s_const = semaphore("s_const")
            s_id = semaphore("s_id")
            s_turn = semaphore("s_turn")
            block = st.enter_context(nc.Block())
            loads = [
                (X3, x_tiles), (raw["rw"][:, :], a["L0_ffn_router_w"]), (raw["gw"][:, :], a["L1_ffn_Wg"]),
                (raw["w1"][:, :, :], a["L1_ffn_W1"].rearrange("e r d -> (e r) d").rearrange("(c p) d -> p c d", p=P)),
                (raw["w2"][:, :].rearrange("d (e r) -> d e r", r=R1), a["L1_ffn_W2"].rearrange("e d r -> d e r")),
                (raw["qkv"][:, :, :], a["L1_attn_w_qkv"].rearrange("(c p) d -> p c d", p=P)),
                (raw["proj"][:, :], a["L1_attn_w_proj"]),
                (rbias[:, :], row_to_all(a["L0_ffn_router_bias"], E0)),
                (gbias[:, :], row_to_all(a["L1_ffn_bg"], E1)),
                (norm_w[:, :], row_to_all(a["L0_ffn_norm_w"], D)),
            ]

            @block.sync
            def _(sp):
                for dst, src in loads:
                    sp.dma_start(dst, src).then_inc(s_in, 16)

            @block.gpsimd
            def _(pool):
                pool.memset(ident[:, :], 0.0)
                pool.memset(ones[:, :], 1.0)
                pool.memset(blockg[:, :], 1.0 / (GN_GROUP * T))
                pool.memset(causal_b[:, :], 0.0)
                pool.memset(headmask[:, :], 1.0)
                pool.memset(ones_b[:, :], 1.0).then_inc(s_const, 1)
                pool.wait_ge(s_const, 1)
                pool.affine_select(out=ident[:, :], in_=ident[:, :], compare_op=ALU.not_equal, fill=1.0,
                                   base=0, pattern=[[-1, P]], channel_multiplier=1)
                pool.affine_select(out=strict[:, :], in_=ones[:, :], compare_op=ALU.is_gt, fill=0.0,
                                   base=0, pattern=[[1, P]], channel_multiplier=-1)
                pool.affine_select(out=causal_b[:, :], in_=causal_b[:, :], compare_op=ALU.is_ge, fill=NEG,
                                   base=0, pattern=[[-1, P]], channel_multiplier=1)
                pool.affine_select(out=blockg[:, :].rearrange("p (g j) -> p g j", j=GN_GROUP),
                                   in_=blockg[:, :].rearrange("p (g j) -> p g j", j=GN_GROUP),
                                   compare_op=ALU.is_ge, fill=0.0, base=0,
                                   pattern=[[-GN_GROUP, P // GN_GROUP], [0, GN_GROUP]],
                                   channel_multiplier=1).then_inc(s_const, 1)
                pool.wait_ge(s_const, 2)
                pool.affine_select(out=blockg[:, :].rearrange("p (g j) -> p g j", j=GN_GROUP),
                                   in_=blockg[:, :].rearrange("p (g j) -> p g j", j=GN_GROUP),
                                   compare_op=ALU.is_ge, fill=0.0, base=GN_GROUP - 1,
                                   pattern=[[GN_GROUP, P // GN_GROUP], [0, GN_GROUP]],
                                   channel_multiplier=-1)
                pool.tensor_copy(ident_b[:, :], ident[:, :])
                pool.tensor_copy(strict_b[:, :], strict[:, :]).then_inc(s_id, 1)

            @block.vector
            def _(dve):
                dve.wait_ge(s_id, 1)
                dve.tensor_reduce(headmask[:, :], ident[:, :].rearrange("p (r j d) -> p j r d", j=GROUP, d=HD),
                                  AX.XY, ALU.add)

            turns = [(router_wT[:, :], raw["rw"][:, :], E0), (gate_wT[:, :], raw["gw"][:, :], E1),
                     (projT[:, :], raw["proj"][:, :], P)]
            turns += [(up1T[:, c * P:(c + 1) * P], raw["w1"][:, c, :], P) for c in range(4)]
            turns += [(down1T[:, c * P:(c + 1) * P], raw["w2"][:, c * P:(c + 1) * P], P) for c in range(4)]
            turns += [(qkvT[:, c * P:(c + 1) * P], raw["qkv"][:, c, :], P) for c in range(3)]

            @block.tensor
            def _(pe):
                pe.wait_ge(s_id, 1)
                pe.wait_ge(s_in, 16 * len(loads))
                for n, (dst, src, rows) in enumerate(turns):
                    o = turned[n // 4][:, (n % 4) * P:(n % 4) * P + rows]
                    pe.transpose(o, src, ident[0:rows, 0:rows]).then_inc(s_turn, 1)

            @block.scalar
            def _(act):
                for n, (dst, src, rows) in enumerate(turns):
                    act.wait_ge(s_turn, len(turns))
                    act.activation(dst, turned[n // 4][:, (n % 4) * P:(n % 4) * P + rows], ACT.Copy)

        def top2(dve, act_exp, link, SC, E, tmp, idx, big=3e38):
            m1, m2, k, oh1, oh2, sc2 = tmp
            v = lambda t: t[:, :].rearrange("p (t e) -> p t e", e=E)
            up = lambda t: t[:, :].unsqueeze(2).broadcast_to([P, TILES, E])
            for src, m, oh in ((SC, m1, oh1), (sc2, m2, oh2)):
                link(dve.tensor_reduce(m[:, :], v(src), AX.X, ALU.max))
                link(dve.tensor_tensor(v(oh), v(src), up(m), ALU.is_equal))
                link(dve.tensor_tensor(oh[:, :], oh[:, :], idx[:, :], ALU.mult))
                link(dve.tensor_reduce(k[:, :], v(oh), AX.X, ALU.max))
                link(dve.tensor_tensor(v(oh), v(idx), up(k), ALU.is_equal))
                if src is SC:
                    link(dve.scalar_tensor_tensor(sc2[:, :], oh[:, :], -big, SC[:, :], ALU.mult, ALU.add))

        def norm_stats(src, eps):
            with ExitStack() as st:
                stats = st.enter_context(nc.sbuf_tensor(uniq("stats"), [P, TILES * 6], F32))
                half = st.enter_context(nc.sbuf_tensor(uniq("half"), [P, TILES], F32))
                s_stat = semaphore("s_stat")
                s_var = semaphore("s_var")
                s_std = semaphore("s_std")
                block = st.enter_context(nc.Block())
                each = stats[:, :].rearrange("p (t k) -> p t k", k=6)

                @block.vector
                def _(dve):
                    with dve.Fori(0, TILES // 8) as i:
                        for j in range(8):
                            last = dve.bn_stats(stats[:, bass.ds(i * 48 + 6 * j, 6)], src[:, bass.ds(i * (8 * D) + j * D, D)])
                        last.then_inc(s_stat, 1)
                    link = chain(dve, s_stat, TILES // 8)
                    dve.wait_ge(s_stat, TILES // 8)
                    dve.tensor_tensor(MV2[:, :, 0], each[:, :, 1], each[:, :, 4], ALU.add)
                    dve.tensor_tensor(half[:, :], each[:, :, 1], each[:, :, 4], ALU.subtract)
                    link(dve.tensor_tensor(MV2[:, :, 1], each[:, :, 2], each[:, :, 5], ALU.add))
                    dve.tensor_scalar(MV2[:, :, 0], MV2[:, :, 0], 0.5, None, ALU.mult)
                    dve.tensor_scalar(MV2[:, :, 1], MV2[:, :, 1], 1.0 / D, eps, ALU.mult, ALU.add)
                    link(dve.scalar_tensor_tensor(half[:, :], half[:, :], 0.25, half[:, :], ALU.mult, ALU.mult))
                    dve.tensor_tensor(MV2[:, :, 1], MV2[:, :, 1], half[:, :], ALU.add).then_inc(s_var, 1)
                    dve.wait_ge(s_std, 1)
                    dve.reciprocal(MV2[:, :, 1], MV2[:, :, 1])

                @block.scalar
                def _(act):
                    act.wait_ge(s_var, 1)
                    act.activation(MV2[:, :, 1], MV2[:, :, 1], ACT.Sqrt).then_inc(s_std, 1)

        def norm_tiles(dve, dst, src, col, first, n=GROUP):
            for j in range(n):
                last = dve.tensor_scalar(dst(j), src[:, bass.ds(col + j * D, D)], MV[:, bass.ds(first + 2 * j, 1)],
                                         MV[:, bass.ds(first + 2 * j + 1, 1)], ALU.subtract, ALU.mult)
            return last

        def l0_ffn():
            norm_stats(X, LN_EPS)
            xs_sorted = dram("xs_sorted", [SLOTS, D])
            ys_sorted = dram("ys_sorted", [UNITS * P, D])
            with ExitStack() as st:
                def sb(n, shape, dt=F32):
                    return st.enter_context(nc.sbuf_tensor(uniq(n), shape, dt))

                def sem(n):
                    return semaphore(n)

                MF = sb("MF", [P, E0 * 2 * H0])
                DN = sb("DN", [P, E0 * 2 * D])
                PH = sb("PH", [P, E0 * H0])
                slot1 = sb("slot1", [P, TILES], I32)
                slot2 = sb("slot2", [P, TILES], I32)
                w1 = sb("w1", [P, TILES])
                w2 = sb("w2", [P, TILES])
                unit_of = sb("unit_of", [P, PADDED], I32)
                s_weights = sem("s_weights")
                s_zero = sem("s_zero")

                with ExitStack() as st2:
                    def sb2(n, shape, dt=F32):
                        return st2.enter_context(nc.sbuf_tensor(uniq(n), shape, dt))

                    def sem2(n):
                        return semaphore(n)

                    SC = sb2("SC", [P, TILES * E0])
                    rb4 = rbias[:, :].unsqueeze(1).broadcast_to([P, GROUP, E0])
                    with ExitStack() as st3:
                        xs = st3.enter_context(nc.sbuf_tensor(uniq("xs"), [P, 2, GW], F32))
                        xsT = st3.enter_context(nc.sbuf_tensor(uniq("xsT"), [P, 2, GW], F32))
                        zero = st3.enter_context(nc.sbuf_tensor(uniq("zero"), [P, 2 * GW], F32))
                        pT = [st3.enter_context(nc.psum_tensor(uniq("pT"), [P, 512], F32)) for _ in range(2)]
                        pR = [st3.enter_context(nc.psum_tensor(uniq("pR"), [P, 512], F32)) for _ in range(2)]
                        S = {n: semaphore(n) for n in
                             ("xs", "turned", "xsT", "kept", "scores", "taken", "z")}
                        block = st3.enter_context(nc.Block())

                        @block.sync
                        def _(sp):
                            MFv = MF[:, :].rearrange("p (e k h) -> p e k h", k=2, h=H0)
                            sp.dma_start(MFv[:, :, 0, :], a["L0_ffn_bank_mag"].rearrange("e d h -> d e h")).then_inc(s_weights, 16)
                            sp.dma_start(MFv[:, :, 1, :], a["L0_ffn_bank_freq"].rearrange("e d h -> d e h")).then_inc(s_weights, 16)
                            sp.dma_start(DN[:, :].rearrange("p (e c d) -> p e c d", c=2, d=D),
                                         a["L0_ffn_bank_down"].rearrange("e (c p) d -> p e c d", p=P)).then_inc(s_weights, 16)
                            sp.dma_start(PH[:, :], row_to_all(a["L0_ffn_bank_phase"].rearrange("e h -> (e h)"), E0 * H0)).then_inc(s_weights, 16)
                            sp.wait_ge(S["z"], 1)
                            for u in range(0, PADDED, 8):
                                sp.dma_start(xs_sorted[u * P:(u + 8) * P, :].rearrange("(p t) d -> p (t d)", p=P),
                                             zero[:, :]).then_inc(s_zero, 16)
                            sp.wait_ge(s_weights, 64)
                            sp.wait_ge(s_zero, 16 * (PADDED // 8))

                        @block.gpsimd
                        def _(pool):
                            pool.memset(zero[:, :], 0.0).then_inc(S["z"], 1)
                            with pool.Fori(0, GROUPS // 2) as i:
                                for u in range(2):
                                    pool.wait_ge(S["xs"], i * 2 + u + 1)
                                    pool.tensor_copy(XN[:, bass.ds(i * (2 * GW) + u * GW, GW)], xs[:, u, :]).then_inc(S["kept"], 1)

                        @block.vector
                        def _(dve):
                            dve.sem_inc(S["taken"], 2)
                            dve.sem_inc(S["kept"], 2)
                            with dve.Fori(0, GROUPS // 2) as i:
                                for u in range(2):
                                    dve.wait_ge(S["kept"], i * 2 + u + 1)
                                    dve.wait_ge(S["turned"], i * 2 + u + 1)
                                    norm_tiles(dve, lambda j: xs[:, u, j * D:(j + 1) * D], X, i * (2 * GW) + u * GW,
                                               i * (4 * GROUP) + u * 2 * GROUP).then_inc(S["xs"], 1)
                                    dve.wait_ge(S["scores"], i * 2 + u + 1)
                                    dve.tensor_tensor(
                                        SC[:, bass.ds(i * (2 * GROUP * E0) + u * GROUP * E0, GROUP * E0)].rearrange("p (t e) -> p t e", e=E0),
                                        pR[u][:, 0:GROUP * E0].rearrange("p (t e) -> p t e", e=E0), rb4,
                                        ALU.add).then_inc(S["taken"], 1)

                        @block.tensor
                        def _(pe):
                            pe.sem_inc(S["turned"], 2)
                            with pe.Fori(0, GROUPS // 2) as i:
                                for u in range(2):
                                    pe.wait_ge(S["xs"], i * 2 + u + 1)
                                    pe.wait_ge(S["xsT"], i * 2 + u + 1)
                                    for j in range(GROUP):
                                        last = pe.transpose(pT[u][:, j * P:(j + 1) * P], xs[:, u, j * D:(j + 1) * D], ident[:, :])
                                    last.then_inc(S["turned"], 1)
                                    pe.wait_ge(S["xsT"], i * 2 + u + 3)
                                    pe.wait_ge(S["taken"], i * 2 + u + 1)
                                    for j in range(GROUP):
                                        last = pe.matmul(pR[u][:, j * E0:(j + 1) * E0], xsT[:, u, j * P:(j + 1) * P],
                                                         router_wT[:, :], start=True, stop=True)
                                    last.then_inc(S["scores"], 1)

                        @block.scalar
                        def _(act):
                            act.sem_inc(S["xsT"], 2)
                            with act.Fori(0, GROUPS // 2) as i:
                                for u in range(2):
                                    act.wait_ge(S["turned"], i * 2 + u + 3)
                                    act.wait_ge(S["taken"], i * 2 + u + 1)
                                    act.activation(xsT[:, u, :], pT[u][:, :], ACT.Copy).then_inc(S["xsT"], 1)

                    with ExitStack() as st3:
                        def sb3(n, shape, dt=F32):
                            return st3.enter_context(nc.sbuf_tensor(uniq(n), shape, dt))
                        idx = sb3("idx", [P, TILES * E0])
                        notfirst = sb3("notfirst", [P, TILES * E0])
                        unit_no = sb3("unit_no", [P, PADDED])
                        m1, m2, k = (sb3(n, [P, TILES]) for n in ("m1", "m2", "k"))
                        oh1, oh2, sc2 = (sb3(n, [P, TILES * E0]) for n in ("oh1", "oh2", "sc2"))
                        cnt = sb3("cnt", [P, TILES * E0], BF16)
                        tot = sb3("tot", [P, TILES * E0])
                        run = sb3("run", [P, TILES * E0])
                        slot = sb3("slot", [P, TILES * E0])
                        nt, ci, base = (sb3(n, [P, E0]) for n in ("nt", "ci", "base"))
                        cmp = sb3("cmp", [P, PADDED * E0])
                        unit_f = sb3("unit_f", [P, PADDED])
                        pE = [st3.enter_context(nc.psum_tensor(uniq("pE"), [P, 512], F32)) for _ in range(2)]
                        pS = [st3.enter_context(nc.psum_tensor(uniq("pS"), [P, 512], F32)) for _ in range(2)]
                        S = {n: semaphore(n) for n in ("c", "iota", "delta", "exp", "cnt", "sums")}
                        block = st3.enter_context(nc.Block())
                        te = lambda t: t[:, :].rearrange("p (t e) -> p t e", e=E0)
                        et = lambda t: t[:, :].rearrange("p (e t) -> p e t", t=TILES)
                        te_as_et = lambda t: t[:, :].rearrange("p (t e) -> p e t", e=E0)

                        @block.gpsimd
                        def _(pool):
                            pool.iota(te(idx), pattern=[[0, TILES], [-1, E0]], base=E0, channel_multiplier=0,
                                      allow_small_or_imprecise_dtypes=True)
                            pool.iota(unit_no[:, :], pattern=[[1, PADDED]], base=0, channel_multiplier=0,
                                      allow_small_or_imprecise_dtypes=True)
                            pool.memset(notfirst[:, :], 1.0).then_inc(S["iota"], 1)
                            pool.wait_ge(S["iota"], 1)
                            pool.memset(et(notfirst)[:, :, 0:1], 0.0).then_inc(S["iota"], 1)

                        @block.scalar
                        def _(act):
                            act.wait_ge(S["delta"], 1)
                            act.activation(w2[:, :], k[:, :], ACT.Exp).then_inc(S["exp"], 1)

                        @block.tensor
                        def _(pe):
                            pe.wait_ge(S["cnt"], 1)
                            for h in range(2):
                                pe.matmul(pE[h][:, :], strict_b[:, :], cnt[:, h * 512:(h + 1) * 512], start=True, stop=True)
                                last = pe.matmul(pS[h][:, :], ones_b[:, :], cnt[:, h * 512:(h + 1) * 512], start=True, stop=True)
                            last.then_inc(S["sums"], 1)

                        @block.vector
                        def _(dve):
                            link = chain(dve, S["c"])
                            dve.wait_ge(S["iota"], 2)
                            top2(dve, None, link, SC, E0, (m1, m2, k, oh1, oh2, sc2), idx)
                            dve.tensor_tensor(cnt[:, :], oh1[:, :], oh2[:, :], ALU.add).then_inc(S["cnt"], 1)
                            dve.tensor_tensor(k[:, :], m2[:, :], m1[:, :], ALU.subtract).then_inc(S["delta"], 1)
                            dve.wait_ge(S["exp"], 1)
                            link(dve.tensor_scalar(w1[:, :], w2[:, :], 1.0, None, ALU.add))
                            link(dve.reciprocal(w1[:, :], w1[:, :]))
                            link(dve.tensor_tensor(w2[:, :], w2[:, :], w1[:, :], ALU.mult))
                            dve.wait_ge(S["sums"], 1)
                            for h in range(2):
                                l = dve.tensor_copy(et(tot)[:, :, h * 32:(h + 1) * 32],
                                                    pS[h][:, :].rearrange("p (t e) -> p e t", e=E0))
                            link(l)
                            link(dve.tensor_tensor_scan(run[:, :], notfirst[:, :], tot[:, :], 0.0, ALU.mult, ALU.add))
                            link(dve.tensor_scalar(nt[:, :], et(run)[:, :, TILES - 1], 1.0 / P,
                                                   (P - 1.0) / P - 0.5 + 0.5 / P, ALU.mult, ALU.add))
                            link(dve.tensor_scalar(nt[:, :], nt[:, :], MAGIC, MAGIC, ALU.add, ALU.subtract))
                            link(dve.tensor_tensor_scan(ci[:, :], ones[:, 0:E0], nt[:, :], 0.0, ALU.mult, ALU.add))
                            link(dve.tensor_tensor(base[:, :], ci[:, :], nt[:, :], ALU.subtract))
                            link(dve.tensor_scalar(base[:, :], base[:, :], float(P), None, ALU.mult))
                            link(dve.tensor_tensor(run[:, :], run[:, :], tot[:, :], ALU.subtract))
                            link(dve.tensor_tensor(et(run), et(run), base[:, :].unsqueeze(2).broadcast_to([P, E0, TILES]), ALU.add))
                            for h in range(2):
                                l = dve.tensor_tensor(te_as_et(slot)[:, :, h * 32:(h + 1) * 32], et(run)[:, :, h * 32:(h + 1) * 32],
                                                      pE[h][:, :].rearrange("p (t e) -> p e t", e=E0), ALU.add)
                            link(l)
                            for oh, dst in ((oh1, slot1), (oh2, slot2)):
                                link(dve.tensor_tensor(oh[:, :], oh[:, :], slot[:, :], ALU.mult))
                                link(dve.tensor_reduce(k[:, :], te(oh), AX.X, ALU.add))
                                link(dve.tensor_copy(dst[:, :], k[:, :]))
                            cv = cmp[:, :].rearrange("p (u e) -> p u e", e=E0)
                            link(dve.tensor_tensor(cv, unit_no[:, :].unsqueeze(2).broadcast_to([P, PADDED, E0]),
                                                   ci[:, :].unsqueeze(1).broadcast_to([P, PADDED, E0]), ALU.is_ge))
                            link(dve.tensor_reduce(unit_f[:, :], cv, AX.X, ALU.add))
                            link(dve.tensor_scalar(unit_f[:, :], unit_f[:, :], float(E0 - 1), None, ALU.min))
                            link(dve.tensor_copy(unit_of[:, :], unit_f[:, :]))

                with ExitStack() as st3:
                    s_moved = gather_semaphore("s_moved")
                    block = st3.enter_context(nc.Block())

                    @block.gpsimd
                    def _(pool):
                        for t in range(TILES):
                            for s in (slot1, slot2):
                                pool.indirect_dma_start(
                                    out=xs_sorted, out_offset=bass.IndirectOffsetOnAxis(ap=s[:, t:t + 1].bitcast(U32), axis=0),
                                    in_=XN[:, t * D:(t + 1) * D], in_offset=None).then_inc(s_moved, 16)
                        pool.wait_ge(s_moved, 16 * 2 * TILES)

                with ExitStack() as st3:
                    def sb3(n, shape, dt=F32):
                        return st3.enter_context(nc.sbuf_tensor(uniq(n), shape, dt))
                    BW = BATCH * H0
                    tanhs = [XN[:, k * BW:(k + 1) * BW] for k in range(4)]
                    freqs = [XN[:, (4 + k) * BW:(5 + k) * BW] for k in range(4)]
                    xg = sb3("xg", [P, 4, BATCH * D])
                    xgT = sb3("xgT", [P, 2, BATCH * P])
                    fb = sb3("fb", [P, 2, BW])
                    turns = sb3("turns", [P, 2, BW])
                    hT = sb3("hT", [P, 2, BW])
                    yo = sb3("yo", [P, 2, BATCH * D])
                    pMag = st3.enter_context(nc.psum_tensor(uniq("pMag"), [P, BW], F32))
                    pFreq = st3.enter_context(nc.psum_tensor(uniq("pFreq"), [P, BW], F32))
                    pT = st3.enter_context(nc.psum_tensor(uniq("pT"), [P, 512], F32))
                    pH = st3.enter_context(nc.psum_tensor(uniq("pH"), [P, BW], F32))
                    pO = st3.enter_context(nc.psum_tensor(uniq("pO"), [P, 512], F32))
                    S = {n: semaphore(n) for n in
                         ("turned", "xgT", "up", "front", "low", "exp", "ln", "d", "angle", "sin", "hid", "hTp", "hT",
                          "down", "yo", "st0", "st1", "phase")}
                    S |= {n: gather_semaphore(n) for n in ("in0", "in1", "in2", "in3")}
                    block = st3.enter_context(nc.Block())
                    PAIRS = NBATCH // 2
                    LOOPS = (PAIRS - 2) // 2
                    assert NBATCH == 2 * PAIRS and PAIRS == 2 * LOOPS + 2

                    def load(pool, row, slot):
                        pool.dma_start(xg[:, slot, :].rearrange("p (t d) -> p t d", d=D),
                                       xs_sorted[bass.ds(row, BATCH * P), :].rearrange("(t p) d -> p t d", p=P)
                                       ).then_inc(S[f"in{slot}"], 16)

                    @block.gpsimd
                    def _(pool):
                        for n in range(4):
                            load(pool, n * BATCH * P, n)
                        with pool.Fori(0, (NBATCH - 4) // 4) as i:
                            for k in range(4):
                                pool.wait_ge(S["turned"], i * 4 + k + 1)
                                load(pool, i * (4 * BATCH * P) + (k + 4) * BATCH * P, k)
                        for k in range(2):
                            pool.wait_ge(S["turned"], NBATCH - 4 + k + 1)
                            load(pool, (NBATCH + k) * BATCH * P, k)

                    @block.sync
                    def _(sp):
                        with sp.Fori(0, NBATCH // 4) as i:
                            for k in range(4):
                                sp.wait_ge(S["yo"], i * 4 + k + 2)
                                sp.dma_start(ys_sorted[bass.ds(i * (4 * BATCH * P) + k * BATCH * P, BATCH * P), :]
                                             .rearrange("(t p) d -> p t d", p=P),
                                             yo[:, k % 2, :].rearrange("p (t d) -> p t d", d=D)).then_inc(S[f"st{k % 2}"], 16)
                        for u in range(2):
                            sp.wait_ge(S[f"st{u}"], 16 * (NBATCH // 2 + 1))

                    @block.tensor
                    def _(pe):
                        def experts(b):
                            return [pe.value_load(unit_of[0:1, bass.ds(b * BATCH + j, 1)], min_val=0, max_val=E0 - 1)
                                    for j in range(BATCH)]

                        def turn(b, slot, loads):
                            pe.wait_ge(S[f"in{slot}"], loads)
                            pe.wait_ge(S["xgT"], b + 1)
                            for j in range(BATCH):
                                last = pe.transpose(pT[:, j * P:(j + 1) * P], xg[:, slot, j * D:(j + 1) * D], ident[:, :])
                            last.then_inc(S["turned"], 1)

                        def up(b, slot):
                            es = experts(b)
                            pe.wait_ge(S["xgT"], b + 2)
                            pe.wait_ge(S["front"], b + 1)
                            for j, e in enumerate(es):
                                lhs = xgT[:, slot % 2, j * P:(j + 1) * P]
                                pe.matmul(pFreq[:, j * H0:(j + 1) * H0], lhs, MF[:, bass.ds(e * (2 * H0) + H0, H0)], start=True, stop=True)
                                last = pe.matmul(pMag[:, j * H0:(j + 1) * H0], lhs, MF[:, bass.ds(e * (2 * H0), H0)], start=True, stop=True)
                            last.then_inc(S["up"], 1)

                        def turn_hidden(b, slot):
                            pe.wait_ge(S["hid"], b + 1)
                            pe.wait_ge(S["hT"], b + 1)
                            for j in range(2 * BATCH):
                                last = pe.transpose(pH[:, j * P:(j + 1) * P], tanhs[slot][:, j * P:(j + 1) * P], ident[:, :])
                            last.then_inc(S["hTp"], 1)

                        def down(b, slot):
                            es = experts(b)
                            pe.wait_ge(S["hT"], b + 2)
                            pe.wait_ge(S["yo"], b + 1)
                            for j, e in enumerate(es):
                                for c in range(2):
                                    last = pe.matmul(pO[:, j * D:(j + 1) * D], hT[:, slot % 2, (2 * j + c) * P:(2 * j + c + 1) * P],
                                                     DN[:, bass.ds(e * (2 * D) + c * D, D)], start=(c == 0), stop=(c == 1))
                            last.then_inc(S["down"], 1)

                        def step(b, k, loads, before=True, after=True):
                            c = (k + 2) % 4
                            if before:
                                turn_hidden(b - 2, c)
                            if after:
                                up(b + 2, c)
                            if before:
                                down(b - 2, c)
                                turn_hidden(b - 1, c + 1)
                            if after:
                                turn(b + 4, k, loads)
                                up(b + 3, c + 1)
                            if before:
                                down(b - 1, c + 1)
                            if after:
                                turn(b + 5, k + 1, loads)

                        turn(0, 0, 16)
                        up(0, 0)
                        turn(1, 1, 16)
                        turn_next = lambda n: turn(n, n, 16)
                        up(1, 1)
                        turn_next(2)
                        turn_next(3)
                        step(0, 0, 32, before=False)
                        with pe.Fori(0, LOOPS) as i:
                            step(i * 4 + 2, 2, i * 16 + 32)
                            step(i * 4 + 4, 0, i * 16 + 48)
                        step(NBATCH - 2, 2, 0, after=False)
                        step(NBATCH, 0, 0, after=False)

                    @block.scalar
                    def _(act):
                        act.sem_inc(S["xgT"], 1)
                        act.sem_inc(S["front"], 1)
                        act.sem_inc(S["hT"], 1)

                        def turned(b, slot):
                            act.wait_ge(S["turned"], b + 1)
                            act.activation(xgT[:, slot % 2, :], pT[:, :], ACT.Copy).then_inc(S["xgT"], 1)

                        def front(b, slot):
                            act.wait_ge(S["up"], b + 1)
                            act.wait_ge(S["hTp"], b + 1)
                            act.activation(freqs[slot], pFreq[:, :], ACT.Copy)
                            act.activation(tanhs[slot], pMag[:, :], ACT.Tanh).then_inc(S["front"], 1)

                        def hidden_turned(b, slot):
                            act.wait_ge(S["hTp"], b + 5)
                            act.wait_ge(S["down"], b + 1)
                            act.activation(hT[:, slot % 2, :], pH[:, :], ACT.Copy).then_inc(S["hT"], 1)

                        def exp(b, slot):
                            act.wait_ge(S["low"], b + 1)
                            act.activation(fb[:, slot % 2, :], fb[:, slot % 2, :], ACT.Exp).then_inc(S["exp"], 1)

                        def ln(b, slot):
                            act.wait_ge(S["exp"], b + 1)
                            act.activation(fb[:, slot % 2, :], fb[:, slot % 2, :], ACT.Ln, bias=1.0).then_inc(S["ln"], 1)

                        def sin(b, slot):
                            act.wait_ge(S["angle"], b + 1)
                            act.activation(turns[:, slot % 2, :], turns[:, slot % 2, :], ACT.Sin, scale=-TURN).then_inc(S["sin"], 1)

                        def step(b, k, before=True, after=True):
                            c = (k + 2) % 4
                            act.preload_act_table_set("natural_log_exp_and_others")
                            exp(b, k)
                            if before:
                                hidden_turned(b - 2, c)
                            exp(b + 1, k + 1)
                            ln(b, k)
                            ln(b + 1, k + 1)
                            if before:
                                hidden_turned(b - 1, c + 1)
                            act.preload_act_table_set("silu_and_others")
                            if after:
                                front(b + 2, c)
                                turned(b + 4, k)
                            sin(b, k)
                            if after:
                                front(b + 3, c + 1)
                                turned(b + 5, k + 1)
                            sin(b + 1, k + 1)

                        act.preload_act_table_set("silu_and_others")
                        turned(0, 0)
                        turned(1, 1)
                        front(0, 0)
                        turned(2, 2)
                        front(1, 1)
                        turned(3, 3)
                        step(0, 0, before=False)
                        with act.Fori(0, LOOPS) as i:
                            step(i * 4 + 2, 2)
                            step(i * 4 + 4, 0)
                        step(NBATCH - 2, 2, after=False)
                        hidden_turned(NBATCH - 2, 2)
                        hidden_turned(NBATCH - 1, 3)

                    @block.vector
                    def _(dve):
                        dve.sem_inc(S["yo"], 1)
                        dve.sem_inc(S["st0"], 16)
                        dve.sem_inc(S["st1"], 16)
                        dve.sem_inc(S["hTp"], 4)
                        dve.sem_inc(S["down"], 2)
                        dve.tensor_scalar(PH[:, :], PH[:, :], 0.1 + PI / 2, 1.0 / (2 * PI), ALU.add, ALU.mult).then_inc(S["phase"], 1)
                        dve.wait_ge(S["phase"], 1)

                        def low(b, slot):
                            dve.wait_ge(S["front"], b + 2)
                            dve.wait_ge(S["angle"], b - 1)
                            dve.tensor_scalar(fb[:, slot % 2, :], freqs[slot], 40.0, None, ALU.min).then_inc(S["low"], 1)

                        def angle(b, slot, link):
                            u = slot % 2
                            es = [dve.value_load(unit_of[0:1, bass.ds(b * BATCH + j, 1)], min_val=0, max_val=E0 - 1)
                                  for j in range(BATCH)]
                            dve.wait_ge(S["ln"], b + 1)
                            link(dve.tensor_tensor(fb[:, u, :], fb[:, u, :], freqs[slot], ALU.max))
                            for j, e in enumerate(es):
                                last = dve.scalar_tensor_tensor(fb[:, u, j * H0:(j + 1) * H0], fb[:, u, j * H0:(j + 1) * H0],
                                                                1.0 / (2 * PI), PH[:, bass.ds(e * H0, H0)], ALU.mult, ALU.add)
                            link(last)
                            link(dve.tensor_scalar(turns[:, u, :], fb[:, u, :], MAGIC, None, ALU.add))
                            dve.scalar_tensor_tensor(turns[:, u, :], turns[:, u, :], MAGIC, fb[:, u, :],
                                                     ALU.subtract, ALU.subtract).then_inc(S["angle"], 1)

                        def hidden(b, slot):
                            dve.wait_ge(S["sin"], b + 1)
                            dve.tensor_tensor(tanhs[slot], tanhs[slot], turns[:, slot % 2, :], ALU.mult).then_inc(S["hid"], 1)

                        def store(b, slot, stored):
                            dve.wait_ge(S["down"], b + 3)
                            dve.wait_ge(S[f"st{slot % 2}"], stored)
                            dve.tensor_copy(yo[:, slot % 2, :], pO[:, :]).then_inc(S["yo"], 1)

                        def step(b, k, stored, link, before=True, after=True):
                            c = (k + 2) % 4
                            if before:
                                hidden(b - 1, c + 1)
                            angle(b, k, link)
                            if before:
                                store(b - 2, c, stored)
                            angle(b + 1, k + 1, link)
                            if after:
                                low(b + 2, c)
                            hidden(b, k)
                            if before:
                                store(b - 1, c + 1, stored)
                            if after:
                                low(b + 3, c + 1)

                        def first_low(b):
                            dve.wait_ge(S["front"], b + 2)
                            dve.tensor_scalar(fb[:, b % 2, :], freqs[b], 40.0, None, ALU.min).then_inc(S["low"], 1)

                        first_low(0)
                        first_low(1)
                        link = chain(dve, S["d"])
                        step(0, 0, 0, link, before=False)
                        with dve.Fori(0, LOOPS) as i:
                            link = chain(dve, S["d"], i * 12 + 6)
                            step(i * 4 + 2, 2, i * 32 + 16, link)
                            step(i * 4 + 4, 0, i * 32 + 32, link)
                        link = chain(dve, S["d"], LOOPS * 12 + 6)
                        step(NBATCH - 2, 2, 16 * (PAIRS - 1), link, after=False)
                        hidden(NBATCH - 1, 3)
                        store(NBATCH - 2, 2, 16 * PAIRS)
                        store(NBATCH - 1, 3, 16 * PAIRS)

                with ExitStack() as st3:
                    def sb3(n, shape, dt=F32):
                        return st3.enter_context(nc.sbuf_tensor(uniq(n), shape, dt))
                    G = 8
                    R = TILES // G
                    y1 = sb3("y1", [P, 2, G * D])
                    y2 = sb3("y2", [P, 2, G * D])
                    sq = sb3("sq", [P, G * D])
                    ms = sb3("ms", [P, 2, G])
                    S = {n: semaphore(n) for n in ("ms", "rms", "c", "x")}
                    S |= {n: gather_semaphore(n) for n in ("g0", "g1")}
                    block = st3.enter_context(nc.Block())

                    @block.gpsimd
                    def _(pool):
                        def gather(r):
                            if r >= 2:
                                pool.wait_ge(S["x"], r - 1)
                            for g in range(G):
                                t = r * G + g
                                for s, y in ((slot1, y1), (slot2, y2)):
                                    pool.indirect_dma_start(
                                        out=y[:, r % 2, g * D:(g + 1) * D], out_offset=None, in_=ys_sorted,
                                        in_offset=bass.IndirectOffsetOnAxis(ap=s[:, t:t + 1].bitcast(U32), axis=0)).then_inc(S[f"g{r % 2}"], 16)

                        gather(0)
                        for r in range(R):
                            if r + 1 < R:
                                gather(r + 1)

                    @block.scalar
                    def _(act):
                        for r in range(R):
                            act.wait_ge(S["ms"], r + 1)
                            act.activation(ms[:, r % 2, :], ms[:, r % 2, :], ACT.Sqrt).then_inc(S["rms"], 1)

                    @block.vector
                    def _(dve):
                        link = chain(dve, S["c"])
                        v = lambda t: t.rearrange("p (t d) -> p t d", d=D)
                        for r in range(R):
                            dve.wait_ge(S[f"g{r % 2}"], 16 * 2 * G * (r // 2 + 1))
                            wb = lambda w: w[:, r * G:(r + 1) * G].unsqueeze(2).broadcast_to([P, G, D])
                            b1, b2 = y1[:, r % 2, :], y2[:, r % 2, :]
                            link(dve.tensor_tensor(v(b1), v(b1), wb(w1), ALU.mult))
                            link(dve.tensor_tensor(v(b2), v(b2), wb(w2), ALU.mult))
                            link(dve.tensor_tensor(b1, b1, b2, ALU.add))
                            link(dve.tensor_tensor(sq[:, :], b1, b1, ALU.mult))
                            link(dve.tensor_reduce(ms[:, r % 2, :], v(sq[:, :]), AX.X, ALU.add))
                            dve.tensor_scalar(ms[:, r % 2, :], ms[:, r % 2, :], 1.0 / D, EPS, ALU.mult, ALU.add).then_inc(S["ms"], 1)
                            dve.wait_ge(S["rms"], r + 1)
                            link(dve.reciprocal(ms[:, r % 2, :], ms[:, r % 2, :]))
                            link(dve.tensor_tensor(v(b1), v(b1), ms[:, r % 2, :].unsqueeze(2).broadcast_to([P, G, D]), ALU.mult))
                            link(dve.tensor_tensor(v(b1), v(b1), norm_w[:, :].unsqueeze(1).broadcast_to([P, G, D]), ALU.mult))
                            xr = X[:, r * G * D:(r + 1) * G * D]
                            dve.scalar_tensor_tensor(xr, b1, 0.5, xr, ALU.mult, ALU.add).then_inc(S["x"], 1)

        def l1_ffn():
            norm_stats(X, LN_EPS)
            XNT = XN
            with ExitStack() as st:
                SC = st.enter_context(nc.sbuf_tensor(uniq("SC"), [P, TILES * E1], F32))
                GA = st.enter_context(nc.sbuf_tensor(uniq("GA"), [P, (TILES + GROUP) * E1], F32))
                gb4 = gbias[:, :].unsqueeze(1).broadcast_to([P, GROUP, E1])
                with ExitStack() as st3:
                    xs = st3.enter_context(nc.sbuf_tensor(uniq("xs"), [P, 2, GW], F32))
                    xsT = st3.enter_context(nc.sbuf_tensor(uniq("xsT"), [P, 2, GW], F32))
                    pT = [st3.enter_context(nc.psum_tensor(uniq("pT"), [P, 512], F32)) for _ in range(2)]
                    pR = [st3.enter_context(nc.psum_tensor(uniq("pR"), [P, 512], F32)) for _ in range(2)]
                    S = {n: semaphore(n) for n in ("xs", "turned", "xsT", "kept", "scores", "taken")}
                    block = st3.enter_context(nc.Block())

                    @block.gpsimd
                    def _(pool):
                        pool.sem_inc(S["kept"], 2)
                        with pool.Fori(0, GROUPS // 2) as i:
                            for u in range(2):
                                pool.wait_ge(S["xsT"], i * 2 + u + 3)
                                pool.tensor_copy(XNT[:, bass.ds(i * (2 * GW) + u * GW, GW)], xsT[:, u, :]).then_inc(S["kept"], 1)

                    @block.vector
                    def _(dve):
                        dve.sem_inc(S["taken"], 2)
                        with dve.Fori(0, GROUPS // 2) as i:
                            for u in range(2):
                                dve.wait_ge(S["turned"], i * 2 + u + 1)
                                norm_tiles(dve, lambda j: xs[:, u, j * D:(j + 1) * D], X, i * (2 * GW) + u * GW,
                                           i * (4 * GROUP) + u * 2 * GROUP).then_inc(S["xs"], 1)
                                dve.wait_ge(S["scores"], i * 2 + u + 1)
                                dve.tensor_tensor(
                                    SC[:, bass.ds(i * (2 * GROUP * E1) + u * GROUP * E1, GROUP * E1)].rearrange("p (t e) -> p t e", e=E1),
                                    pR[u][:, 0:GROUP * E1].rearrange("p (t e) -> p t e", e=E1), gb4,
                                    ALU.add).then_inc(S["taken"], 1)

                    @block.tensor
                    def _(pe):
                        pe.sem_inc(S["turned"], 2)
                        with pe.Fori(0, GROUPS // 2) as i:
                            for u in range(2):
                                pe.wait_ge(S["xs"], i * 2 + u + 1)
                                pe.wait_ge(S["xsT"], i * 2 + u + 1)
                                for j in range(GROUP):
                                    last = pe.transpose(pT[u][:, j * P:(j + 1) * P], xs[:, u, j * D:(j + 1) * D], ident[:, :])
                                last.then_inc(S["turned"], 1)
                                pe.wait_ge(S["xsT"], i * 2 + u + 3)
                                pe.wait_ge(S["taken"], i * 2 + u + 1)
                                for j in range(GROUP):
                                    last = pe.matmul(pR[u][:, j * E1:(j + 1) * E1], xsT[:, u, j * P:(j + 1) * P],
                                                     gate_wT[:, :], start=True, stop=True)
                                last.then_inc(S["scores"], 1)

                    @block.scalar
                    def _(act):
                        act.sem_inc(S["xsT"], 2)
                        with act.Fori(0, GROUPS // 2) as i:
                            for u in range(2):
                                act.wait_ge(S["turned"], i * 2 + u + 3)
                                act.wait_ge(S["taken"], i * 2 + u + 1)
                                act.wait_ge(S["kept"], i * 2 + u + 1)
                                act.activation(xsT[:, u, :], pT[u][:, :], ACT.Copy).then_inc(S["xsT"], 1)

                with ExitStack() as st3:
                    def sb3(n, shape, dt=F32):
                        return st3.enter_context(nc.sbuf_tensor(uniq(n), shape, dt))
                    idx = sb3("idx", [P, TILES * E1])
                    m1, m2, k, w1, w2 = (sb3(n, [P, TILES]) for n in ("m1", "m2", "k", "w1", "w2"))
                    oh1, oh2, sc2 = (sb3(n, [P, TILES * E1]) for n in ("oh1", "oh2", "sc2"))
                    S = {n: semaphore(n) for n in ("c", "iota", "delta", "exp")}
                    block = st3.enter_context(nc.Block())
                    te = lambda t: t[:, :].rearrange("p (t e) -> p t e", e=E1)

                    @block.gpsimd
                    def _(pool):
                        pool.memset(GA[:, TILES * E1:], 0.0)
                        pool.iota(te(idx), pattern=[[0, TILES], [-1, E1]], base=E1, channel_multiplier=0,
                                  allow_small_or_imprecise_dtypes=True).then_inc(S["iota"], 1)

                    @block.scalar
                    def _(act):
                        act.wait_ge(S["delta"], 1)
                        act.activation(w2[:, :], k[:, :], ACT.Exp).then_inc(S["exp"], 1)

                    @block.vector
                    def _(dve):
                        link = chain(dve, S["c"])
                        dve.wait_ge(S["iota"], 1)
                        top2(dve, None, link, SC, E1, (m1, m2, k, oh1, oh2, sc2), idx)
                        dve.tensor_tensor(k[:, :], m2[:, :], m1[:, :], ALU.subtract).then_inc(S["delta"], 1)
                        dve.wait_ge(S["exp"], 1)
                        link(dve.tensor_scalar(w1[:, :], w2[:, :], 1.0, None, ALU.add))
                        link(dve.reciprocal(w1[:, :], w1[:, :]))
                        link(dve.tensor_tensor(w2[:, :], w2[:, :], w1[:, :], ALU.mult))
                        up = lambda t: t[:, :].unsqueeze(2).broadcast_to([P, TILES, E1])
                        link(dve.tensor_tensor(te(oh1), te(oh1), up(w1), ALU.mult))
                        link(dve.tensor_tensor(te(oh2), te(oh2), up(w2), ALU.mult))
                        dve.tensor_tensor(GA[:, 0:TILES * E1], oh1[:, :], oh2[:, :], ALU.add)

                with ExitStack() as st3:
                    def sb3(n, shape, dt=F32):
                        return st3.enter_context(nc.sbuf_tensor(uniq(n), shape, dt))
                    CH = ER // P
                    gates = sb3("gates", [P, 2, GROUP * ER])
                    hid = sb3("hid", [P, 2, GW])
                    gated = sb3("gated", [P, 4, GW])
                    pU, pG, pO = ([st3.enter_context(nc.psum_tensor(uniq(n), [P, 512], F32)) for _ in range(2)] for n in ("pU", "pG", "pO"))
                    S = {n: semaphore(n) for n in ("gates", "up", "gelu", "gated", "out", "taken")}
                    block = st3.enter_context(nc.Block())
                    UN = 2
                    LAG = 2
                    KS = UN * CH

                    @block.tensor
                    def _(pe):
                        pe.sem_inc(S["up"], 2 * CH)
                        pe.sem_inc(S["out"], 4)
                        with pe.Fori(0, GROUPS // UN) as i:
                            def up(kk):
                                g, c = kk // CH, kk % CH
                                if c == 0:
                                    pe.wait_ge(S["gates"], i * UN + g + 1)
                                pe.wait_ge(S["gated"], i * KS + kk + 1)
                                pe.matmul(pU[kk % 2][:, :], up1T[:, c * P:(c + 1) * P],
                                          XNT[:, bass.ds(i * (UN * GW) + g * GW, GW)], start=True, stop=True)
                                for j in range(GROUP):
                                    gs = gates[:, g, j * ER + c * P:j * ER + (c + 1) * P]
                                    last = pe.transpose(pG[kk % 2][:, j * P:(j + 1) * P], gs, ident[:, :])
                                last.then_inc(S["up"], 1)

                            def down(kk):
                                g, c = kk // CH, kk % CH
                                pe.wait_ge(S["gated"], i * KS + kk + 3)
                                if c == 0:
                                    pe.wait_ge(S["taken"], i * UN + g + 1)
                                for j in range(GROUP):
                                    last = pe.matmul(pO[g % 2][:, j * D:(j + 1) * D], gated[:, kk % 4, j * P:(j + 1) * P],
                                                     down1T[:, c * P:(c + 1) * P], start=(c == 0 and j == 0),
                                                     stop=(c == CH - 1), skip_group_check=True)
                                last.then_inc(S["out"], 1)

                            for kk in range(KS + LAG):
                                if kk < KS:
                                    up(kk)
                                if kk >= LAG:
                                    down(kk - LAG)

                    @block.scalar
                    def _(act):
                        act.preload_act_table_set("gelu_and_others")
                        def expand(group, u, cols):
                            act.wait_ge(S["up"], group * CH + CH)
                            act.activation(gates[:, u, :].rearrange("p (e r) -> p e r", r=R1),
                                           GA[:, bass.ds(cols, GROUP * E1)].unsqueeze(2).broadcast_to([P, GROUP * E1, R1]),
                                           ACT.Copy).then_inc(S["gates"], 1)

                        expand(0, 0, 0)
                        with act.Fori(0, GROUPS // UN) as i:
                            for kk in range(KS):
                                act.wait_ge(S["up"], i * KS + kk + 2 * CH + 1)
                                act.wait_ge(S["gated"], i * KS + kk + 1)
                                act.activation(hid[:, kk % 2, :], pU[kk % 2][:, :], ACT.Gelu).then_inc(S["gelu"], 1)
                                if kk % CH == 1:
                                    g = kk // CH + 1
                                    expand(i * UN + g, g % 2, i * (UN * GROUP * E1) + g * GROUP * E1)

                    @block.vector
                    def _(dve):
                        dve.sem_inc(S["gated"], 2)
                        dve.sem_inc(S["taken"], 2)
                        with dve.Fori(0, GROUPS // UN) as i:
                            def onto_x(g):
                                dve.wait_ge(S["out"], i * KS + (g + 1) * CH + 4)
                                xv = X[:, bass.ds(i * (UN * GW) + g * GW, GW)]
                                dve.tensor_tensor(xv, xv, pO[g % 2][:, :], ALU.add).then_inc(S["taken"], 1)
                            for kk in range(KS):
                                dve.wait_ge(S["gelu"], i * KS + kk + 1)
                                dve.wait_ge(S["out"], i * KS + kk + 1)
                                dve.tensor_tensor(gated[:, kk % 4, :], hid[:, kk % 2, :], pG[kk % 2][:, :], ALU.mult).then_inc(S["gated"], 1)
                                if kk >= CH + LAG and (kk - LAG) % CH == 0:
                                    onto_x((kk - LAG) // CH - 1)
                            onto_x(UN - 1)

        def l0_attn():
            norm_stats(X, LN_EPS)
            W = 2 * T
            with ExitStack() as st:
                def sb3(n, shape, dt=F32):
                    return st.enter_context(nc.sbuf_tensor(uniq(n), shape, dt))
                wp = sb3("wp", [D, 6 * D])
                wo = sb3("wo", [D, D])
                wf1 = sb3("wf1", [D, FF])
                wf2 = sb3("wf2", [P, 4 * D])
                cols = sb3("cols", [P, 2])
                b1c = sb3("b1c", [P, 4])
                rows = {n: sb3(n, [P, D]) for n in ("ln1_scale", "ln1_bias", "b2", "ln2_scale", "ln2_bias")}
                first = sb3("first", [P, W])
                halfpi = sb3("halfpi", [P, 1])
                with ExitStack() as st3:
                    def t(n, shape=None, dt=F32):
                        return st3.enter_context(nc.sbuf_tensor(uniq(n), shape or [P, W], dt))
                    xs, xT, q, k, g, ar, ai, s1, s2, kv = (t(n) for n in ("xs", "xT", "q", "k", "g", "ar", "ai", "s1", "s2", "kv"))
                    den, tt, hx, hy, ph, r, sg, th, sn, cs = (t(n) for n in ("den", "tt", "hx", "hy", "ph", "r", "sg", "th", "sn", "cs"))
                    ur, ui, yr, yi, ta, aar, aai = (t(n) for n in ("ur", "ui", "yr", "yi", "ta", "aar", "aai"))
                    sums = t("sums", [P, 8])
                    mean = t("mean", [P, 8])
                    gn = t("gn", [P, 6])
                    pT, pq, pk, pv, par, pai, pg, pW = (st3.enter_context(nc.psum_tensor(uniq("p"), [P, 512], F32)) for _ in range(8))
                    S = {n: semaphore(n) for n in
                         ("w", "fi", "xs", "kept", "turned", "xT", "proj", "copied", "d", "mag2", "mag", "ang", "at", "turns", "trig",
                          "y", "sq", "sums", "mean", "var", "std", "z", "wo")}
                    block = st3.enter_context(nc.Block())
                    col = lambda ap: ap.rearrange("(p o) -> p o", o=1)
                    loads = [(wp[:, n * D:(n + 1) * D], a["L0_attn_" + w]) for n, w in enumerate(("Wq", "Wk", "Wv"))]
                    loads += [(wp[:, 3 * D:5 * D], a["L0_attn_Wa"]), (wp[:, 5 * D:6 * D], a["L0_attn_Wg"]), (wo[:, :], a["L0_attn_Wo"]),
                              (wf1[:, :], a["L0_attn_W1"]),
                              (wf2[:, :].rearrange("p (c d) -> p c d", d=D), a["L0_attn_W2"].rearrange("(c p) d -> p c d", p=P)),
                              (cols[:, 0:1], col(a["L0_attn_gn_scale"])), (cols[:, 1:2], col(a["L0_attn_gn_bias"])),
                              (b1c[:, :], a["L0_attn_b1"].rearrange("(c p) -> p c", p=P))]
                    loads += [(rows[n][:, :], row_to_all(a["L0_attn_" + n], D)) for n in rows]

                    @block.sync
                    def _(sp):
                        with nc.allow_non_contiguous_dma(reason="a few columns of 4 bytes"):
                            for dst, src in loads:
                                sp.dma_start(dst, src).then_inc(S["w"], 16)

                    @block.gpsimd
                    def _(pool):
                        pool.memset(halfpi[:, :], PI / 2)
                        pool.memset(first[:, :], 1.0).then_inc(S["fi"], 1)
                        pool.wait_ge(S["fi"], 1)
                        pool.memset(first[:, 0:W:T], 0.0).then_inc(S["fi"], 1)
                        with pool.Fori(0, GROUPS) as i:
                            pool.wait_ge(S["xs"], i + 1)
                            pool.tensor_copy(XN[:, bass.ds(i * GW, GW)], xs[:, :]).then_inc(S["kept"], 1)

                    @block.tensor
                    def _(pe):
                        pe.wait_ge(S["w"], 16 * len(loads))
                        with pe.Fori(0, GROUPS) as i:
                            pe.wait_ge(S["xs"], i + 1)
                            for j in range(GROUP):
                                last = pe.transpose(pT[:, j * P:(j + 1) * P], xs[:, j * D:(j + 1) * D], ident[:, :])
                            last.then_inc(S["turned"], 1)
                            pe.wait_ge(S["xT"], i + 1)
                            for n, p in enumerate((pq, pk, pv, par, pai, pg)):
                                last = pe.matmul(p[:, :], wp[:, n * D:(n + 1) * D], xT[:, :], start=True, stop=True)
                            last.then_inc(S["proj"], 1)
                            pe.wait_ge(S["sq"], i + 1)
                            pe.wait_ge(S["y"], i + 1)
                            pe.matmul(pT[:, 0:8], blockg[:, :], sums[:, :], start=True, stop=True).then_inc(S["mean"], 1)
                            pe.wait_ge(S["z"], i + 1)
                            for j in range(GROUP):
                                last = pe.matmul(pW[:, j * D:(j + 1) * D], yr[:, j * P:(j + 1) * P], wo[:, :], start=True, stop=True)
                            last.then_inc(S["wo"], 1)

                    @block.scalar
                    def _(act):
                        act.wait_ge(S["fi"], 2)
                        with act.Fori(0, GROUPS) as i:
                            act.wait_ge(S["turned"], i + 1)
                            act.activation(xT[:, :], pT[:, :], ACT.Copy).then_inc(S["xT"], 1)
                            act.wait_ge(S["proj"], i + 1)
                            act.activation(s1[:, :], par[:, :], ACT.Square)
                            act.activation(s2[:, :], pai[:, :], ACT.Square).then_inc(S["copied"], 1)
                            act.activation(aar[:, :], par[:, :], ACT.Abs)
                            act.activation(aai[:, :], pai[:, :], ACT.Abs)
                            for dst, p in ((ar, par), (ai, pai), (k, pk), (q, pq), (g, pg)):
                                last = act.activation(dst[:, :], p[:, :], ACT.Copy)
                            last.then_inc(S["copied"], 1)
                            act.preload_act_table_set("sqrt_and_others")
                            act.wait_ge(S["mag2"], i + 1)
                            act.activation(s1[:, :], s1[:, :], ACT.Sqrt).then_inc(S["mag"], 1)
                            act.preload_act_table_set("sigmoid_and_others")
                            act.wait_ge(S["mag"], i + 1)
                            act.wait_ge(S["copied"], i * 2 + 2)
                            act.activation(r[:, :], s1[:, :], ACT.Sigmoid)
                            act.activation(sg[:, :], g[:, :], ACT.Sigmoid)
                            act.wait_ge(S["ang"], i + 1)
                            act.activation(tt[:, :], tt[:, :], ACT.Arctan).then_inc(S["at"], 1)
                            act.preload_act_table_set("trig_and_small")
                            act.wait_ge(S["turns"], i + 1)
                            act.activation(sn[:, :], th[:, :], ACT.Sin, scale=TURN)
                            act.activation(cs[:, :], ph[:, :], ACT.Sin, scale=-TURN, bias=halfpi[:, 0:1]).then_inc(S["trig"], 1)
                            act.wait_ge(S["y"], i + 1)
                            for n, (y, junk) in enumerate(((yr, s2), (yi, aai))):
                                for h in range(2):
                                    last = act.activation(junk[:, h * T:(h + 1) * T], y[:, h * T:(h + 1) * T], ACT.Square,
                                                          accum_out=sums[:, 4 + 2 * n + h:5 + 2 * n + h])
                            last.then_inc(S["sq"], 1)
                            act.preload_act_table_set("sqrt_and_others")
                            act.wait_ge(S["var"], i + 1)
                            act.activation(gn[:, 0:2], gn[:, 0:2], ACT.Sqrt).then_inc(S["std"], 1)

                    @block.vector
                    def _(dve):
                        dve.wait_ge(S["w"], 16 * len(loads))
                        dve.wait_ge(S["fi"], 2)
                        STEPS = 24
                        with dve.Fori(0, GROUPS) as i:
                            count = [0]

                            def link(ins):
                                count[0] += 1
                                ins.then_inc(S["d"], 1)
                                dve.wait_ge(S["d"], i * STEPS + count[0])
                            f = lambda x: x[:, :]
                            norm_tiles(dve, lambda j: xs[:, j * D:(j + 1) * D], X, i * GW, i * (2 * GROUP)).then_inc(S["xs"], 1)
                            dve.wait_ge(S["copied"], i * 2 + 1)
                            dve.scalar_tensor_tensor(f(s1), f(s1), 1e-36, f(s2), ALU.add, ALU.add).then_inc(S["mag2"], 1)
                            dve.wait_ge(S["copied"], i * 2 + 2)
                            dve.tensor_scalar(f(hx), f(ar), 0.0, 0.5, ALU.is_ge, ALU.subtract)
                            dve.tensor_scalar(f(hy), f(ai), 0.0, 0.5, ALU.is_ge, ALU.subtract)
                            dve.tensor_tensor(f(kv), f(k), pv[:, :], ALU.mult)
                            dve.wait_ge(S["mag"], i + 1)
                            link(dve.tensor_tensor(f(den), f(aar), f(s1), ALU.add))
                            link(dve.reciprocal(f(den), f(den)))
                            dve.tensor_tensor(f(tt), f(aai), f(den), ALU.mult).then_inc(S["ang"], 1)
                            dve.wait_ge(S["at"], i + 1)
                            link(dve.tensor_scalar(f(tt), f(tt), 4.0 / PI, -1.0, ALU.mult, ALU.add))
                            link(dve.tensor_tensor(f(tt), f(tt), f(hx), ALU.mult))
                            link(dve.scalar_tensor_tensor(f(tt), f(tt), 0.5, f(hy), ALU.add, ALU.mult))
                            link(dve.tensor_tensor_scan(f(th), f(first), f(tt), 0.0, ALU.mult, ALU.add))
                            link(dve.tensor_scalar(f(ta), f(th), MAGIC, MAGIC, ALU.add, ALU.subtract))
                            link(dve.tensor_tensor(f(th), f(th), f(ta), ALU.subtract))
                            link(dve.tensor_scalar(f(ph), f(th), -1.0, None, ALU.mult))
                            dve.tensor_tensor(f(ph), f(ph), f(th), ALU.max).then_inc(S["turns"], 1)
                            dve.wait_ge(S["trig"], i + 1)
                            link(dve.tensor_tensor(f(r), f(r), f(first), ALU.mult))
                            dve.tensor_tensor(f(ar), f(kv), f(cs), ALU.mult)
                            link(dve.scalar_tensor_tensor(f(ai), f(kv), -1.0, f(sn), ALU.mult, ALU.mult))
                            dve.tensor_tensor_scan(f(ur), f(r), f(ar), 0.0, ALU.mult, ALU.add)
                            dve.tensor_tensor_scan(f(ui), f(r), f(ai), 0.0, ALU.mult, ALU.add)
                            dve.tensor_tensor(f(cs), f(cs), f(q), ALU.mult)
                            link(dve.tensor_tensor(f(sn), f(sn), f(q), ALU.mult))
                            dve.tensor_tensor(f(yr), f(cs), f(ur), ALU.mult)
                            dve.tensor_tensor(f(yi), f(cs), f(ui), ALU.mult)
                            dve.tensor_tensor(f(ta), f(sn), f(ui), ALU.mult)
                            link(dve.tensor_tensor(f(ar), f(sn), f(ur), ALU.mult))
                            dve.tensor_tensor(f(yr), f(yr), f(ta), ALU.subtract)
                            link(dve.tensor_tensor(f(yi), f(yi), f(ar), ALU.add))
                            seq = lambda x: x[:, :].rearrange("p (s t) -> p s t", s=2)
                            dve.tensor_reduce(sums[:, 0:2], seq(yr), AX.X, ALU.add)
                            dve.tensor_reduce(sums[:, 2:4], seq(yi), AX.X, ALU.add).then_inc(S["y"], 1)
                            link(dve.tensor_tensor(f(g), f(g), f(sg), ALU.mult))
                            dve.wait_ge(S["mean"], i + 1)
                            link(dve.tensor_copy(mean[:, :], pT[:, 0:8]))
                            link(dve.tensor_tensor(gn[:, 2:6], mean[:, 0:4], mean[:, 0:4], ALU.mult))
                            link(dve.tensor_tensor(gn[:, 2:6], mean[:, 4:8], gn[:, 2:6], ALU.subtract))
                            dve.scalar_tensor_tensor(gn[:, 0:2], gn[:, 2:4], EPS, gn[:, 4:6], ALU.add, ALU.add).then_inc(S["var"], 1)
                            dve.wait_ge(S["std"], i + 1)
                            link(dve.reciprocal(gn[:, 0:2], gn[:, 0:2]))
                            link(dve.tensor_scalar(gn[:, 0:2], gn[:, 0:2], cols[:, 0:1], None, ALU.mult))
                            link(dve.tensor_tensor(gn[:, 2:4], mean[:, 0:2], gn[:, 0:2], ALU.mult))
                            link(dve.tensor_scalar(gn[:, 2:4], gn[:, 2:4], -1.0, cols[:, 1:2], ALU.mult, ALU.add))
                            for h in range(2):
                                l = dve.tensor_scalar(yr[:, h * T:(h + 1) * T], yr[:, h * T:(h + 1) * T], gn[:, h:h + 1],
                                                      gn[:, 2 + h:3 + h], ALU.mult, ALU.add)
                            link(l)
                            dve.tensor_tensor(f(yr), f(yr), f(g), ALU.mult).then_inc(S["z"], 1)
                            dve.wait_ge(S["wo"], i + 1)
                            dve.wait_ge(S["kept"], i + 1)
                            xv = XN[:, bass.ds(i * GW, GW)]
                            link(dve.tensor_tensor(xv, xv, pW[:, :], ALU.add))
                            assert count[0] == STEPS

                norm_stats(XN, EPS)
                with ExitStack() as st3:
                    def t(n, shape=None, dt=F32):
                        return st3.enter_context(nc.sbuf_tensor(uniq(n), shape or [P, W], dt))
                    x1 = t("x1", [P, 2, W])
                    x1T = t("x1T", [P, 2, W])
                    hid = t("hid", [P, 4, W])
                    pT, pU, pO = ([st3.enter_context(nc.psum_tensor(uniq(n), [P, 512], F32)) for _ in range(2)] for n in ("pT", "pU", "pO"))
                    S = {n: semaphore(n) for n in ("d", "x1", "turned", "x1T", "up", "gelu", "down")}
                    block = st3.enter_context(nc.Block())
                    over = lambda n: rows[n][:, :].unsqueeze(1).broadcast_to([P, GROUP, D])

                    @block.vector
                    def _(dve):
                        def normed(c, base, g, u):
                            v = x1[:, u, :].rearrange("p (t d) -> p t d", d=D)
                            ln = chain(dve, S["d"], base)
                            ln(norm_tiles(dve, lambda j: x1[:, u, j * D:(j + 1) * D], XN, c, g))
                            ln(dve.tensor_tensor(v, v, over("ln1_scale"), ALU.mult))
                            dve.tensor_tensor(v, v, over("ln1_bias"), ALU.add).then_inc(S["x1"], 1)

                        def finish(i, base, c, u):
                            v = x1[:, u, :].rearrange("p (t d) -> p t d", d=D)
                            ln = chain(dve, S["d"], base)
                            dve.wait_ge(S["down"], i * 8 + 4 * u + 8)
                            ln(dve.tensor_tensor(v, v, over("b2"), ALU.add))
                            ln(dve.tensor_tensor(XN[:, bass.ds(c, GW)], x1[:, u, :], pO[u][:, :], ALU.add))

                        with dve.Fori(0, GROUPS // 2) as i:
                            normed(i * (2 * GW), i * 8, i * (4 * GROUP), 0)
                            normed(i * (2 * GW) + GW, i * 8 + 2, i * (4 * GROUP) + 2 * GROUP, 1)
                            finish(i, i * 8 + 4, i * (2 * GW), 0)
                            finish(i, i * 8 + 6, i * (2 * GW) + GW, 1)

                    @block.tensor
                    def _(pe):
                        pe.sem_inc(S["down"], 4)
                        with pe.Fori(0, GROUPS // 2) as i:
                            for u in range(2):
                                pe.wait_ge(S["x1"], i * 2 + u + 1)
                                for j in range(GROUP):
                                    last = pe.transpose(pT[u][:, j * P:(j + 1) * P], x1[:, u, j * D:(j + 1) * D], ident[:, :])
                                last.then_inc(S["turned"], 1)
                            KS = 8

                            def up(kk):
                                g, c = kk // 4, kk % 4
                                if c == 0:
                                    pe.wait_ge(S["x1T"], i * 2 + g + 1)
                                pe.wait_ge(S["gelu"], i * KS + kk + 1)
                                pe.matmul(pU[kk % 2][:, :], wf1[:, c * P:(c + 1) * P], x1T[:, g, :], start=True, stop=True).then_inc(S["up"], 1)

                            def down(kk):
                                g, c = kk // 4, kk % 4
                                pe.wait_ge(S["gelu"], i * KS + kk + 3)
                                for j in range(GROUP):
                                    last = pe.matmul(pO[g][:, j * D:(j + 1) * D], hid[:, c, j * P:(j + 1) * P],
                                                     wf2[:, c * D:(c + 1) * D], start=(c == 0 and j == 0), stop=(c == 3),
                                                     skip_group_check=True)
                                last.then_inc(S["down"], 1)
                            for kk in range(KS + 1):
                                if kk < KS:
                                    up(kk)
                                if kk >= 1:
                                    down(kk - 1)

                    @block.scalar
                    def _(act):
                        act.sem_inc(S["gelu"], 2)
                        act.preload_act_table_set("gelu_apprx_tanh_and_others")
                        with act.Fori(0, GROUPS // 2) as i:
                            for u in range(2):
                                act.wait_ge(S["turned"], i * 2 + u + 1)
                                act.activation(x1T[:, u, :], pT[u][:, :], ACT.Copy).then_inc(S["x1T"], 1)
                            for kk in range(8):
                                act.wait_ge(S["up"], i * 8 + kk + 1)
                                act.wait_ge(S["down"], i * 8 + kk + 1)
                                act.activation(hid[:, kk % 4, :], pU[kk % 2][:, :], ACT.Gelu_apprx_tanh,
                                               bias=b1c[:, kk % 4:kk % 4 + 1]).then_inc(S["gelu"], 1)

                norm_stats(XN, EPS)
                with ExitStack() as st3:
                    ys = st3.enter_context(nc.sbuf_tensor(uniq("ys"), [P, 2, GW], F32))
                    S = {n: semaphore(n) for n in ("n", "scaled", "biased", "d")}
                    block = st3.enter_context(nc.Block())

                    @block.vector
                    def _(dve):
                        with dve.Fori(0, GROUPS // 2) as i:
                            link = chain(dve, S["d"], i * 8)
                            for u in range(2):
                                c = i * (2 * GW) + u * GW
                                v = ys[:, u, :].rearrange("p (t d) -> p t d", d=D)
                                over = lambda n: rows[n][:, :].unsqueeze(1).broadcast_to([P, GROUP, D])
                                link(norm_tiles(dve, lambda j: ys[:, u, j * D:(j + 1) * D], XN, c, i * (4 * GROUP) + u * 2 * GROUP))
                                link(dve.tensor_tensor(v, v, over("ln2_scale"), ALU.mult))
                                link(dve.tensor_tensor(v, v, over("ln2_bias"), ALU.add))
                                link(dve.tensor_tensor(X[:, bass.ds(c, GW)], X[:, bass.ds(c, GW)], ys[:, u, :], ALU.add))

        def l1_attn():
            norm_stats(X, LN_EPS)
            SCALE = float(HD) ** -0.5
            QT = T // P
            units = [(0, h, 4) for h in range(0, HEADS, 4)] + [(1, h, 2) for h in range(0, HEADS, 2)]
            NU = len(units)
            with ExitStack() as st3:
                def t(n, shape, dt=F32):
                    return st3.enter_context(nc.sbuf_tensor(uniq(n), shape, dt))
                VN = HEADS * VW
                CW = 32
                HG = P // CW
                xs = t("xs", [P, QT * D])
                xT = t("xT", [P, T])
                kS = t("kS", [P, 2, T])
                Qm = XN[:, :].rearrange("p (u h t) -> p u h t", u=2, h=HEADS)
                hm = t("hm", [P, HEADS])
                Vx = t("Vx", [P, 2, QT, HEADS, CW])
                Vsum = t("Vsum", [P, 2 * VN])
                OT = t("OT", [P, QT, 512])
                dif = t("dif", [P, 3, 512])
                ET = t("ET", [P, 3, 512])
                mx = t("mx", [P, 2, 4])
                MC = t("MC", [P, QT, HEADS])
                O = t("O", [P, QT, HEADS, VW])
                rs = t("rs", [P, QT, HEADS])
                att = t("att", [P, QT * D])
                attT = t("attT", [P, T])
                low = t("low", [P, 2, HEADS])
                neg100 = t("neg100", [P, 1])
                mask2 = t("mask2", [P, T], BF16)
                pS, pX, pOT = ([st3.enter_context(nc.psum_tensor(uniq(n), [P, 512], F32)) for _ in range(2)] for n in ("pS", "pX", "pOT"))
                pA, pB = (st3.enter_context(nc.psum_tensor(uniq(n), [P, 512], F32)) for n in ("pA", "pB"))
                S = {n: semaphore(n) for n in
                     ("c0", "mask", "xs", "turned", "xT", "qk", "v", "q", "vx", "vsums", "vkept", "ot0", "ot1", "oturned0", "oturned1", "s", "dif", "xp", "relu", "exp", "pv",
                      "low", "d", "att", "attT", "attTs", "out", "x")}
                block = st3.enter_context(nc.Block())

                @block.gpsimd
                def _(pool):
                    pool.memset(neg100[:, :], -100.0)
                    pool.memset(Vx[:, :, :, :, :], 1.0)
                    pool.memset(mask2[:, 0:P], 0.0)
                    pool.tensor_copy(mask2[:, P:T], causal_b[:, :])
                    link = chain(pool, S["mask"])
                    link(pool.memset(hm[:, :], SCALE))
                    link(pool.affine_select(out=hm[:, :], in_=hm[:, :], compare_op=ALU.is_ge, fill=0.0, base=0,
                                            pattern=[[-HD, HEADS]], channel_multiplier=1))
                    pool.affine_select(out=hm[:, :], in_=hm[:, :], compare_op=ALU.is_ge, fill=0.0, base=HD - 1,
                                       pattern=[[HD, HEADS]], channel_multiplier=-1).then_inc(S["c0"], 1)

                @block.tensor
                def _(pe):
                    def rows_turned(b):
                        pe.wait_ge(S["xs"], b + 1)
                        pe.wait_ge(S["x"], b + 1)
                        for j in range(QT):
                            last = pe.transpose(pA[:, j * P:(j + 1) * P], xs[:, j * D:(j + 1) * D], ident[:, :])
                        last.then_inc(S["turned"], 1)

                    def qkv(b):
                        pe.wait_ge(S["xT"], b + 1)
                        pe.matmul(pA[:, 0:T], qkvT[:, 0:D], xT[:, :], start=True, stop=True)
                        pe.matmul(pA[:, T:2 * T], qkvT[:, D:2 * D], xT[:, :], start=True, stop=True).then_inc(S["qk"], 1)
                        pe.wait_ge(S["vkept"], b + 1)
                        for j in range(QT):
                            last = pe.matmul(pB[:, j * D:(j + 1) * D], xT[:, j * P:(j + 1) * P], qkvT[:, 2 * D:3 * D], start=True, stop=True)
                        last.then_inc(S["v"], 1)

                    def value_sums(b, par):
                        vrow = lambda j: Vx[:, par, j, :, 0:VW]
                        pe.matmul(pB[:, 0:VN], ones[:, :], vrow(0), start=True, stop=False)
                        pe.matmul(pB[:, 0:VN], ones[:, :], vrow(1), start=False, stop=True)
                        pe.matmul(pB[:, VN:2 * VN], ones[:, :], vrow(1), start=True, stop=True).then_inc(S["vsums"], 1)

                    def scores(g, n, par):
                        qt, h0, nh = units[n]
                        K = P * (qt + 1)
                        pe.wait_ge(S["dif"], g + 1)
                        rhs = mask2[:, T - K:T].unsqueeze(1).broadcast_to([P, nh, K])
                        pe.matmul(pS[n % 2][:, :], ident_b[:, :], rhs, start=True, stop=False, skip_group_check=True)
                        for m in range(nh):
                            last = pe.matmul(pS[n % 2][:, m * K:(m + 1) * K], Qm[:, par, h0 + m, qt * P:(qt + 1) * P],
                                             kS[:, par, 0:K], start=False, stop=(m == nh - 1), skip_group_check=True)
                        last.then_inc(S["s"], 1)

                    def turn(g, n):
                        pe.wait_ge(S["dif"], g + 3)
                        pe.wait_ge(S["exp"], g + 1)
                        for m in range(4):
                            last = pe.transpose(pX[n % 2][:, m * P:(m + 1) * P], dif[:, n % 3, m * P:(m + 1) * P], ident[:, :])
                        last.then_inc(S["xp"], 1)

                    def values(g, b, n, par):
                        qt, h0, nh = units[n]
                        pe.wait_ge(S["exp"], g + 3)
                        if n == 0:
                            pe.wait_ge(S["ot0"], b + 1)
                        if n == HEADS // 4:
                            pe.wait_ge(S["ot1"], b + 1)
                        for kt in range(qt + 1):
                            for m in range(nh):
                                h = h0 + m
                                c0 = CW * (h % HG)
                                last = pe.matmul(pOT[qt][c0:c0 + CW, (h // HG) * P:(h // HG + 1) * P], Vx[:, par, kt, h, :],
                                                 ET[:, n % 3, (m * (qt + 1) + kt) * P:(m * (qt + 1) + kt + 1) * P],
                                                 start=(kt == 0), stop=(kt == qt), tile_position=(0, c0), skip_group_check=True)
                        last.then_inc(S["pv"], 1)

                    def sums_turned(b, after):
                        pe.wait_ge(S["ot0"], b + 2)
                        if after:
                            pe.wait_ge(S["q"], b + 3)
                        else:
                            pe.wait_ge(S["x"], b + 3)
                        for j in range(4):
                            last = pe.transpose(pA[:, j * P:(j + 1) * P], OT[:, 0, j * P:(j + 1) * P], ident[:, :])
                        last.then_inc(S["oturned0"], 1)
                        pe.wait_ge(S["ot1"], b + 2)
                        if after:
                            pe.wait_ge(S["vx"], b + 3)
                        else:
                            pe.wait_ge(S["vkept"], b + 3)
                        for j in range(4):
                            last = pe.transpose(pB[:, j * P:(j + 1) * P], OT[:, 1, j * P:(j + 1) * P], ident[:, :])
                        last.then_inc(S["oturned1"], 1)

                    def attended_turned(b):
                        pe.wait_ge(S["att"], b + 1)
                        for j in range(QT):
                            last = pe.transpose(pA[:, j * P:(j + 1) * P], att[:, j * D:(j + 1) * D], ident[:, :])
                        last.then_inc(S["attT"], 1)

                    def project(b):
                        pe.wait_ge(S["attTs"], b + 1)
                        for j in range(QT):
                            last = pe.matmul(pA[:, T + j * D:T + (j + 1) * D], attT[:, j * P:(j + 1) * P], projT[:, :], start=True, stop=True)
                        last.then_inc(S["out"], 1)

                    def slot(b, par, n, before, after):
                        g = b * NU + n
                        scores(g, n, par)
                        if before and n == 1:
                            value_sums(b - 1, 1 - par)
                        if after and n == 2:
                            rows_turned(b + 1)
                        if before and n == 6:
                            sums_turned(b - 1, after)
                        if before and n == 9:
                            attended_turned(b - 1)
                        if n >= 2 or before:
                            turn(g - 2, (n - 2) % NU)
                        if n >= 4:
                            values(g - 4, b, n - 4, par)
                        elif before:
                            values(g - 4, b - 1, n - 4 + NU, 1 - par)
                        if after and n == 3:
                            qkv(b + 1)
                        if before and n == 10:
                            project(b - 1)

                    pe.wait_ge(S["c0"], 1)
                    rows_turned(0)
                    qkv(0)
                    pe.wait_ge(S["q"], 1)
                    pe.wait_ge(S["vx"], 1)
                    for n in range(NU):
                        slot(0, 0, n, False, True)
                    with pe.Fori(0, (B - 2) // 2) as i:
                        for par in (1, 0):
                            for n in range(NU):
                                slot(i * 2 + (2 - par), par, n, True, True)
                    for n in range(NU):
                        slot(B - 1, 1, n, True, False)
                    for n in range(2):
                        turn(B * NU + n - 2, n - 2 + NU)
                        values(B * NU + n - 4, B - 1, n - 4 + NU, 1)
                    for n in range(2, 4):
                        values(B * NU + n - 4, B - 1, n - 4 + NU, 1)
                    value_sums(B - 1, 1)
                    sums_turned(B - 1, False)
                    attended_turned(B - 1)
                    project(B - 1)

                @block.scalar
                def _(act):
                    act.sem_inc(S["exp"], 2)
                    act.sem_inc(S["vkept"], 2)
                    act.sem_inc(S["ot0"], 1)
                    act.sem_inc(S["ot1"], 1)
                    act.preload_act_table_set("exp_and_others")
                    act.wait_ge(S["c0"], 1)

                    def rows_turned(b):
                        act.wait_ge(S["turned"], b + 1)
                        act.activation(xT[:, :], pA[:, 0:T], ACT.Copy).then_inc(S["xT"], 1)

                    def keys(b, par):
                        act.wait_ge(S["qk"], b + 1)
                        act.activation(kS[:, par, :], pA[:, T:2 * T], ACT.Copy)

                    def queries(h0, h1, par):
                        for h in range(h0, h1):
                            last = act.activation(Qm[:, par, h, :], pA[:, 0:T], ACT.Copy, scale=hm[:, h:h + 1])
                        if h1 == HEADS:
                            last.then_inc(S["q"], 1)

                    def v_rows(b, par):
                        act.wait_ge(S["v"], b + 1)
                        act.activation(Vx[:, par, :, :, 0:HD], pB[:, 0:2 * D].rearrange("p (k h d) -> p k h d", k=QT, d=HD),
                                       ACT.Copy).then_inc(S["vx"], 1)

                    def keep_sums(b):
                        act.wait_ge(S["vsums"], b + 1)
                        act.activation(Vsum[:, 0:VN], pB[:, 0:VN], ACT.Copy, scale=1e-8)
                        act.activation(Vsum[:, VN:], pB[:, VN:2 * VN], ACT.Copy).then_inc(S["vkept"], 1)

                    def keep_values(b, qt):
                        act.wait_ge(S["pv"], b * NU + 3 + (HEADS // 4 if qt == 0 else NU))
                        act.activation(OT[:, qt, :], pOT[qt][:, :], ACT.Copy).then_inc(S[f"ot{qt}"], 1)

                    def exps(g, n):
                        act.wait_ge(S["xp"], g + 4)
                        act.wait_ge(S["pv"], g + 1)
                        act.activation(ET[:, n % 3, :], pX[n % 2][:, :], ACT.Relu, scale=-1.0).then_inc(S["relu"], 1)
                        act.wait_ge(S["relu"], g + 1)
                        act.activation(ET[:, n % 3, :], ET[:, n % 3, :], ACT.Exp, scale=-1.0).then_inc(S["exp"], 1)

                    def unseen(b, par):
                        act.wait_ge(S["dif"], b * NU + 4 + 2)
                        act.activation(low[:, par, :], MC[:, 0, :], ACT.Exp, scale=-1.0, bias=neg100[:, 0:1]).then_inc(S["low"], 1)

                    def attended_turned(b):
                        act.wait_ge(S["attT"], b + 1)
                        act.activation(attT[:, :], pA[:, 0:T], ACT.Copy).then_inc(S["attTs"], 1)

                    def slot(b, par, n, before, after):
                        g = b * NU + n
                        if n >= 2 or before:
                            exps(g - 2, (n - 2) % NU)
                        if before and n == 2:
                            keep_sums(b - 1)
                        if after and n == 2:
                            rows_turned(b + 1)
                        if after and n == 3:
                            keys(b + 1, 1 - par)
                            queries(0, 4, 1 - par)
                        if before and n == 4:
                            keep_values(b - 1, 1)
                        if after and n == 4:
                            v_rows(b + 1, 1 - par)
                            queries(4, 9, 1 - par)
                        if after and n == 5:
                            queries(9, HEADS, 1 - par)
                        if n == 8:
                            unseen(b, par)
                        if before and n == 9:
                            attended_turned(b - 1)
                        if n == 9:
                            keep_values(b, 0)

                    rows_turned(0)
                    keys(0, 0)
                    queries(0, HEADS, 0)
                    v_rows(0, 0)
                    for n in range(NU):
                        slot(0, 0, n, False, True)
                    with act.Fori(0, (B - 2) // 2) as i:
                        for par in (1, 0):
                            for n in range(NU):
                                slot(i * 2 + (2 - par), par, n, True, True)
                    for n in range(NU):
                        slot(B - 1, 1, n, True, False)
                    for n in range(2):
                        exps(B * NU + n - 2, n - 2 + NU)
                    keep_values(B - 1, 1)
                    keep_sums(B - 1)
                    attended_turned(B - 1)

                @block.vector
                def _(dve):
                    dve.sem_inc(S["dif"], 2)
                    dve.sem_inc(S["xp"], 3)
                    dve.sem_inc(S["x"], 3)
                    dve.wait_ge(S["c0"], 1)
                    dve.sem_inc(S["pv"], 3)
                    hw = lambda ap: ap.rearrange("p (h w) -> p h w", w=VW)
                    Of = lambda j: O[:, j, :, :].rearrange("p h w -> p (h w)")

                    def norm(b):
                        norm_tiles(dve, lambda j: xs[:, j * D:(j + 1) * D], X, b * (QT * D), b * (2 * QT), QT).then_inc(S["xs"], 1)

                    def unit(g, n, link):
                        qt, h0, nh = units[n]
                        dve.wait_ge(S["s"], g + 1)
                        sc = pS[n % 2][:, :].rearrange("p (h k) -> p h k", h=nh)
                        link(dve.tensor_reduce(mx[:, n % 2, 0:nh], sc, AX.X, ALU.max))
                        link(dve.tensor_scalar(MC[:, qt, h0:h0 + nh], mx[:, n % 2, 0:nh], -100.0, 100.0, ALU.max, ALU.min))
                        dve.wait_ge(S["xp"], g + 1)
                        dve.scalar_tensor_tensor(dif[:, n % 3, :].rearrange("p (h k) -> p h k", h=nh), sc, -100.0,
                                                 MC[:, qt, h0:h0 + nh].unsqueeze(2).broadcast_to([P, nh, P * (qt + 1)]),
                                                 ALU.max, ALU.subtract).then_inc(S["dif"], 1)

                    def finish_sums(b, par, link):
                        ow = lambda p: p[:, :].rearrange("p (h w) -> p h w", w=CW)[:, :, 0:VW]
                        dve.wait_ge(S["low"], b + 1)
                        dve.wait_ge(S["vkept"], b + 3)
                        link(dve.tensor_tensor(O[:, 0, :, :], hw(Vsum[:, VN:]), low[:, par, :].unsqueeze(2).broadcast_to([P, HEADS, VW]), ALU.mult))
                        dve.wait_ge(S["oturned0"], b + 1)
                        dve.tensor_tensor(O[:, 0, :, :], O[:, 0, :, :], ow(pA), ALU.add)
                        dve.wait_ge(S["oturned1"], b + 1)
                        link(dve.tensor_copy(O[:, 1, :, :], ow(pB)))

                    def finish_p(link):
                        link(dve.tensor_scalar(rs[:, :, :], O[:, :, :, HD], 1e-6, None, ALU.add))
                        link(dve.reciprocal(rs[:, :, :], rs[:, :, :]))
                        for j in range(QT):
                            l = dve.tensor_tensor(O[:, j, :, :], O[:, j, :, :], rs[:, j, :].unsqueeze(2).broadcast_to([P, HEADS, VW]), ALU.mult)
                        link(l)

                    def finish(link):
                        for j in range(QT):
                            l = dve.tensor_tensor(Of(j), Of(j), Vsum[:, 0:VN], ALU.add)
                        link(l)
                        link(dve.reciprocal(rs[:, :, :], O[:, :, :, HD]))
                        for j in range(QT):
                            l = dve.tensor_tensor(att[:, j * D:(j + 1) * D].rearrange("p (h d) -> p h d", d=HD), O[:, j, :, 0:HD],
                                                  rs[:, j, :].unsqueeze(2).broadcast_to([P, HEADS, HD]), ALU.mult)
                        l.then_inc(S["att"], 1)

                    def onto_x(b):
                        dve.wait_ge(S["out"], b + 1)
                        xv = X[:, bass.ds(b * (QT * D), QT * D)]
                        dve.tensor_tensor(xv, xv, pA[:, T:2 * T], ALU.add).then_inc(S["x"], 1)

                    def slot(b, par, n, before, after, link):
                        unit(b * NU + n, n, link)
                        if after and n == 0:
                            norm(b + 1)
                        if before and n == 6:
                            finish_sums(b - 1, 1 - par, link)
                        if before and n == 7:
                            finish_p(link)
                        if before and n == 8:
                            finish(link)
                        if before and n == 11:
                            onto_x(b - 1)

                    UNIT_LINKS, END_LINKS = 2 * NU, 7
                    LINKS = UNIT_LINKS + END_LINKS
                    norm(0)
                    link = chain(dve, S["d"])
                    for n in range(NU):
                        slot(0, 0, n, False, True, link)
                    with dve.Fori(0, (B - 2) // 2) as i:
                        link = chain(dve, S["d"], i * (2 * LINKS) + UNIT_LINKS)
                        for par in (1, 0):
                            for n in range(NU):
                                slot(i * 2 + (2 - par), par, n, True, True, link)
                    link = chain(dve, S["d"], (B - 2) * LINKS + UNIT_LINKS)
                    for n in range(NU):
                        slot(B - 1, 1, n, True, False, link)
                    finish_sums(B - 1, 1, link)
                    finish_p(link)
                    finish(link)
                    onto_x(B - 1)

        table = {"l0_ffn": l0_ffn, "l1_ffn": l1_ffn, "l0_attn": l0_attn, "l1_attn": l1_attn}
        end_stage()
        for s in stages:
            table[s]()
            end_stage()


        with ExitStack() as st:
            s_out = semaphore("s_out")
            block = st.enter_context(nc.Block())

            @block.sync
            def _(sp):
                sp.dma_start(out_tiles, X3).then_inc(s_out, 16)
                sp.wait_ge(s_out, 16)

_INS = ['L0_attn_x', 'L0_attn_Wq', 'L0_attn_Wk', 'L0_attn_Wv', 'L0_attn_Wa', 'L0_attn_Wg', 'L0_attn_Wo',
        'L0_attn_gn_scale', 'L0_attn_gn_bias', 'L0_attn_ln1_scale', 'L0_attn_ln1_bias', 'L0_attn_W1',
        'L0_attn_b1', 'L0_attn_W2', 'L0_attn_b2', 'L0_attn_ln2_scale', 'L0_attn_ln2_bias',
        'L0_ffn_router_w', 'L0_ffn_router_bias', 'L0_ffn_bank_mag', 'L0_ffn_bank_freq', 'L0_ffn_bank_phase',
        'L0_ffn_bank_down', 'L0_ffn_norm_w', 'L1_attn_w_qkv', 'L1_attn_w_proj', 'L1_ffn_Wg', 'L1_ffn_bg',
        'L1_ffn_W1', 'L1_ffn_W2']


def kernel(**inputs):
    import numpy as _np
    import concourse.bacc as _bacc
    from concourse import mybir as _mybir
    from concourse.bass_utils import run_bass_kernel_spmd as _run

    nc = _bacc.Bacc("TRN2", target_bir_lowering=False, num_devices=1)
    arrays, args = {}, {}
    for name in _INS:
        v = _np.ascontiguousarray(inputs[name])
        arrays[f"in_{name}_dram"] = v
        args[name] = nc.dram_tensor(f"in_{name}_dram", v.shape, _mybir.dt.from_np(v.dtype), kind="ExternalInput").ap()
    out = nc.dram_tensor("out_0_dram", (B, T, D), _mybir.dt.from_np(_np.dtype("float32")), kind="ExternalOutput").ap()
    macaron_kernel(nc, args, out)
    r = _run(nc, [arrays], core_ids=[0])
    return r.results[0]["out_0_dram"]
```

```python
from contextlib import ExitStack

import concourse.bass as bass
from concourse import mybir

F32 = mybir.dt.float32
BF16 = mybir.dt.bfloat16
I32 = mybir.dt.int32
U32 = mybir.dt.uint32
ALU = mybir.AluOpType
ACT = mybir.ActivationFunctionType
AX = mybir.AxisListType

P = 128
D = 128
B, T = 32, 256
N = B * T
TILES = N // P
GROUP = 4
GW = GROUP * D
GROUPS = TILES // GROUP
LN_EPS = 1e-5
EPS = 1e-6
MAGIC = 1.5 * 2.0 ** 23
PI = 3.141592653589793
TURN = 6.283185

E0, H0 = 16, 256
UNITS = 2 * TILES + E0
BATCH = 4
NBATCH = UNITS // BATCH
PADDED = UNITS + 2 * BATCH
SLOTS = PADDED * P
DW = D + 1
CLEAR = 8
E1, R1 = 8, 64
ER = E1 * R1
FF = 512
GN_GROUP = 4
HEADS, HD = 16, 8
VW = HD + 1
NEG = -1e30
SEM0 = 120

ALL = ("l0_ffn", "l0_attn", "l0_ffn", "l1_ffn", "l1_attn", "l1_ffn")


def macaron_kernel(nc, a, out, stages=ALL):
    ctx = ExitStack()
    names = [0]

    def uniq(n):
        names[0] += 1
        return f"{n}_{names[0]}"

    def dram(n, shape, dt=F32):
        return nc.dram_tensor(uniq(n), shape, dt, kind="Internal").ap()

    def chain(eng, sem, base=0):
        count = [0]

        def link(ins):
            count[0] += 1
            ins.then_inc(sem, 1)
            eng.wait_ge(sem, base + count[0])
        return link

    with ctx:
        def sb(n, shape, dt=F32):
            return ctx.enter_context(nc.sbuf_tensor(uniq(n), shape, dt))

        stage_sems = []

        def semaphore(n):
            stage_sems.append(nc.alloc_semaphore(name=uniq(n), num=SEM0 + len(stage_sems)))
            return stage_sems[-1]

        def gather_semaphore(n):
            return nc.alloc_semaphore(name=uniq(n))

        def end_stage():
            nc.all_engine_barrier(sems_to_clear=range(SEM0, SEM0 + len(stage_sems)))
            for s in stage_sems:
                nc.release_semaphore(s)
            stage_sems.clear()

        X = sb("X", [P, TILES * D])
        XW = sb("XW", [P, TILES * DW])
        XN = XW[:, 0:TILES * D]
        ident = sb("ident", [P, P])
        ident_b = sb("ident_b", [P, P], BF16)
        ones = sb("ones", [P, P])
        ones_b = sb("ones_b", [P, P], BF16)
        strict_b = sb("strict_b", [P, P], BF16)
        strict = sb("strict", [P, P])
        causal_b = sb("causal_b", [P, P], BF16)
        blockg = sb("blockg", [P, P])
        router_wT = sb("router_wT", [D, E0])
        gate_wT = sb("gate_wT", [D, E1])
        up1T = sb("up1T", [D, ER])
        down1T = sb("down1T", [P, ER])
        qkvT = sb("qkvT", [D, 3 * D])
        projT = sb("projT", [D, D])
        rbias = sb("rbias", [P, E0])
        gbias = sb("gbias", [P, E1])
        norm_w = sb("norm_w", [P, D])
        MV = sb("MV", [P, TILES * 2])
        stats = sb("stats", [P, TILES * 6])
        MV2 = MV[:, :].rearrange("p (t k) -> p t k", k=2)

        x_tiles = a["L0_attn_x"].rearrange("b t d -> (b t) d").rearrange("(t p) d -> p t d", p=P)
        out_tiles = out.rearrange("b t d -> (b t) d").rearrange("(t p) d -> p t d", p=P)
        X3 = X[:, :].rearrange("p (t d) -> p t d", d=D)

        def row_to_all(ap, n):
            return ap.rearrange("(o n) -> o n", o=1).broadcast_to([P, n])

        def row_stats(dve, src, col, tile, n):
            for j in range(n):
                last = dve.bn_stats(stats[:, bass.ds(tile * 6 + 6 * j, 6)], src[:, bass.ds(col + j * D, D)])
            return last

        with ExitStack() as st:
            raw = {}
            for n, shape in (("rw", [E0, D]), ("gw", [E1, D]), ("w1", [P, 4, D]), ("w2", [D, ER]),
                             ("qkv", [P, 3, D]), ("proj", [D, D])):
                raw[n] = st.enter_context(nc.sbuf_tensor(uniq("raw_" + n), shape, F32))
            turned = [st.enter_context(nc.psum_tensor(uniq("turned"), [P, 512], F32)) for _ in range(4)]
            s_in = semaphore("s_in")
            s_const = semaphore("s_const")
            s_id = semaphore("s_id")
            s_turn = semaphore("s_turn")
            block = st.enter_context(nc.Block())
            QUARTER = TILES // 4
            s_x = [semaphore(f"s_x{c}") for c in range(4)]
            loads = [
                (raw["rw"][:, :], a["L0_ffn_router_w"]), (raw["gw"][:, :], a["L1_ffn_Wg"]),
                (raw["w1"][:, :, :], a["L1_ffn_W1"].rearrange("e r d -> (e r) d").rearrange("(c p) d -> p c d", p=P)),
                (raw["w2"][:, :].rearrange("d (e r) -> d e r", r=R1), a["L1_ffn_W2"].rearrange("e d r -> d e r")),
                (raw["qkv"][:, :, :], a["L1_attn_w_qkv"].rearrange("(c p) d -> p c d", p=P)),
                (raw["proj"][:, :], a["L1_attn_w_proj"]),
                (rbias[:, :], row_to_all(a["L0_ffn_router_bias"], E0)),
                (gbias[:, :], row_to_all(a["L1_ffn_bg"], E1)),
                (norm_w[:, :], row_to_all(a["L0_ffn_norm_w"], D)),
            ]

            @block.sync
            def _(sp):
                for dst, src in loads:
                    sp.dma_start(dst, src).then_inc(s_in, 16)
                for c in range(4):
                    tiles = slice(c * QUARTER, (c + 1) * QUARTER)
                    sp.dma_start(X3[:, tiles, :], x_tiles[:, tiles, :]).then_inc(s_x[c], 16)

            @block.gpsimd
            def _(pool):
                pool.memset(ident[:, :], 0.0)
                pool.memset(ones[:, :], 1.0)
                pool.memset(blockg[:, :], 1.0 / (GN_GROUP * T))
                pool.memset(causal_b[:, :], 0.0)
                pool.memset(ones_b[:, :], 1.0).then_inc(s_const, 1)
                pool.wait_ge(s_const, 1)
                pool.affine_select(out=ident[:, :], in_=ident[:, :], compare_op=ALU.not_equal, fill=1.0,
                                   base=0, pattern=[[-1, P]], channel_multiplier=1)
                pool.affine_select(out=strict[:, :], in_=ones[:, :], compare_op=ALU.is_gt, fill=0.0,
                                   base=0, pattern=[[1, P]], channel_multiplier=-1)
                pool.affine_select(out=causal_b[:, :], in_=causal_b[:, :], compare_op=ALU.is_ge, fill=NEG,
                                   base=0, pattern=[[-1, P]], channel_multiplier=1)
                pool.affine_select(out=blockg[:, :].rearrange("p (g j) -> p g j", j=GN_GROUP),
                                   in_=blockg[:, :].rearrange("p (g j) -> p g j", j=GN_GROUP),
                                   compare_op=ALU.is_ge, fill=0.0, base=0,
                                   pattern=[[-GN_GROUP, P // GN_GROUP], [0, GN_GROUP]],
                                   channel_multiplier=1).then_inc(s_const, 1)
                pool.wait_ge(s_const, 2)
                pool.affine_select(out=blockg[:, :].rearrange("p (g j) -> p g j", j=GN_GROUP),
                                   in_=blockg[:, :].rearrange("p (g j) -> p g j", j=GN_GROUP),
                                   compare_op=ALU.is_ge, fill=0.0, base=GN_GROUP - 1,
                                   pattern=[[GN_GROUP, P // GN_GROUP], [0, GN_GROUP]],
                                   channel_multiplier=-1)
                pool.tensor_copy(ident_b[:, :], ident[:, :])
                pool.tensor_copy(strict_b[:, :], strict[:, :]).then_inc(s_id, 1)

            @block.vector
            def _(dve):
                for c in range(4):
                    dve.wait_ge(s_x[c], 16)
                    with dve.Fori(0, QUARTER // 8) as i:
                        row_stats(dve, X, i * (8 * D) + c * QUARTER * D, i * 8 + c * QUARTER, 8)

            turns = [(router_wT[:, :], raw["rw"][:, :], E0), (gate_wT[:, :], raw["gw"][:, :], E1),
                     (projT[:, :], raw["proj"][:, :], P)]
            turns += [(up1T[:, c * P:(c + 1) * P], raw["w1"][:, c, :], P) for c in range(4)]
            turns += [(down1T[:, c * P:(c + 1) * P], raw["w2"][:, c * P:(c + 1) * P], P) for c in range(4)]
            turns += [(qkvT[:, c * P:(c + 1) * P], raw["qkv"][:, c, :], P) for c in range(3)]

            @block.tensor
            def _(pe):
                pe.wait_ge(s_id, 1)
                pe.wait_ge(s_in, 16 * len(loads))
                for n, (dst, src, rows) in enumerate(turns):
                    o = turned[n // 4][:, (n % 4) * P:(n % 4) * P + rows]
                    pe.transpose(o, src, ident[0:rows, 0:rows]).then_inc(s_turn, 1)

            @block.scalar
            def _(act):
                for n, (dst, src, rows) in enumerate(turns):
                    act.wait_ge(s_turn, len(turns))
                    act.activation(dst, turned[n // 4][:, (n % 4) * P:(n % 4) * P + rows], ACT.Copy)

        def top2(dve, link, SC, E, tmp, idx, big=3e38):
            m1, m2, k, oh1, oh2, sc2 = tmp
            v = lambda t: t[:, :].rearrange("p (t e) -> p t e", e=E)
            up = lambda t: t[:, :].unsqueeze(2).broadcast_to([P, TILES, E])
            for src, m, oh in ((SC, m1, oh1), (sc2, m2, oh2)):
                link(dve.tensor_reduce(m[:, :], v(src), AX.X, ALU.max))
                link(dve.tensor_tensor(v(oh), v(src), up(m), ALU.is_equal))
                link(dve.tensor_tensor(oh[:, :], oh[:, :], idx[:, :], ALU.mult))
                link(dve.tensor_reduce(k[:, :], v(oh), AX.X, ALU.max))
                link(dve.tensor_tensor(v(oh), v(idx), up(k), ALU.is_equal))
                if src is SC:
                    link(dve.scalar_tensor_tensor(sc2[:, :], oh[:, :], -big, SC[:, :], ALU.mult, ALU.add))

        def norm_stats(src, eps, gathered):
            with ExitStack() as st:
                half = st.enter_context(nc.sbuf_tensor(uniq("half"), [P, TILES], F32))
                s_stat = semaphore("s_stat")
                s_var = semaphore("s_var")
                s_std = semaphore("s_std")
                block = st.enter_context(nc.Block())
                each = stats[:, :].rearrange("p (t k) -> p t k", k=6)

                @block.vector
                def _(dve):
                    if not gathered:
                        with dve.Fori(0, TILES // 8) as i:
                            row_stats(dve, src, i * (8 * D), i * 8, 8).then_inc(s_stat, 1)
                        dve.wait_ge(s_stat, TILES // 8)
                    link = chain(dve, s_stat, 0 if gathered else TILES // 8)
                    dve.tensor_tensor(MV2[:, :, 0], each[:, :, 1], each[:, :, 4], ALU.add)
                    dve.tensor_tensor(half[:, :], each[:, :, 1], each[:, :, 4], ALU.subtract)
                    link(dve.tensor_tensor(MV2[:, :, 1], each[:, :, 2], each[:, :, 5], ALU.add))
                    dve.tensor_scalar(MV2[:, :, 0], MV2[:, :, 0], 0.5, None, ALU.mult)
                    dve.tensor_scalar(MV2[:, :, 1], MV2[:, :, 1], 1.0 / D, eps, ALU.mult, ALU.add)
                    link(dve.scalar_tensor_tensor(half[:, :], half[:, :], 0.25, half[:, :], ALU.mult, ALU.mult))
                    dve.tensor_tensor(MV2[:, :, 1], MV2[:, :, 1], half[:, :], ALU.add).then_inc(s_var, 1)
                    dve.wait_ge(s_std, 1)
                    dve.reciprocal(MV2[:, :, 1], MV2[:, :, 1])

                @block.scalar
                def _(act):
                    act.wait_ge(s_var, 1)
                    act.activation(MV2[:, :, 1], MV2[:, :, 1], ACT.Sqrt).then_inc(s_std, 1)

        def norm_tiles(dve, dst, src, col, first, n=GROUP):
            for j in range(n):
                last = dve.tensor_scalar(dst(j), src[:, bass.ds(col + j * D, D)], MV[:, bass.ds(first + 2 * j, 1)],
                                         MV[:, bass.ds(first + 2 * j + 1, 1)], ALU.subtract, ALU.mult)
            return last

        def one_ahead(eng, early, late):
            early(0, 0)
            with eng.Fori(0, GROUPS // 2 - 1) as i:
                for u in range(2):
                    early(i * 2 + u + 1, 1 - u)
                    late(i * 2 + u, u)
            early(GROUPS - 1, 1)
            late(GROUPS - 2, 0)
            late(GROUPS - 1, 1)

        def l0_ffn(gathered, gather):
            norm_stats(X, LN_EPS, gathered)
            xs_sorted = dram("xs_sorted", [SLOTS, DW])
            y_rows = dram("y_rows", [2 * TILES * P + CLEAR * P, D])
            with ExitStack() as st:
                def sb(n, shape, dt=F32):
                    return st.enter_context(nc.sbuf_tensor(uniq(n), shape, dt))

                MF = sb("MF", [P, E0 * 2 * H0])
                DN = sb("DN", [P, E0 * 2 * D])
                PH = sb("PH", [P, E0 * H0])
                slot1 = sb("slot1", [P, TILES], I32)
                slot2 = sb("slot2", [P, TILES], I32)
                w1 = sb("w1", [P, TILES])
                w2 = sb("w2", [P, TILES])
                experts_of = sb("experts_of", [P, PADDED // BATCH], I32)
                EBITS = E0.bit_length() - 1
                assert E0 == 1 << EBITS and PADDED % BATCH == 0

                def batch_experts(eng, b):
                    word = eng.value_load(experts_of[0:1, bass.ds(b, 1)], min_val=0, max_val=E0 ** BATCH - 1)
                    return [(word >> (EBITS * j)) & (E0 - 1) for j in range(BATCH)]

                numbers = XW[:, :].bitcast(I32).rearrange("p (t d) -> p t d", d=DW)[:, :, D:DW]
                s_weights = semaphore("s_weights")
                s_zero = semaphore("s_zero")

                with ExitStack() as st2:
                    def sb2(n, shape, dt=F32):
                        return st2.enter_context(nc.sbuf_tensor(uniq(n), shape, dt))

                    SC = sb2("SC", [P, TILES * E0])
                    bias_of_all = rbias[:, :].unsqueeze(1).broadcast_to([P, TILES, E0])
                    with ExitStack() as st3:
                        xs = st3.enter_context(nc.sbuf_tensor(uniq("xs"), [P, 2, GW], F32))
                        xsT = st3.enter_context(nc.sbuf_tensor(uniq("xsT"), [P, 2, GW], F32))
                        zero = st3.enter_context(nc.sbuf_tensor(uniq("zero"), [P, CLEAR * DW], F32))
                        pT = [st3.enter_context(nc.psum_tensor(uniq("pT"), [P, 512], F32)) for _ in range(2)]
                        pR = st3.enter_context(nc.psum_tensor(uniq("pR"), [P, TILES * E0], F32))
                        S = {n: semaphore(n) for n in
                             ("xs", "turned", "xsT", "kept", "scores", "number", "z")}
                        block = st3.enter_context(nc.Block())

                        @block.sync
                        def _(sp):
                            MFv = MF[:, :].rearrange("p (e k h) -> p e k h", k=2, h=H0)
                            sp.dma_start(MFv[:, :, 0, :], a["L0_ffn_bank_mag"].rearrange("e d h -> d e h")).then_inc(s_weights, 16)
                            sp.dma_start(MFv[:, :, 1, :], a["L0_ffn_bank_freq"].rearrange("e d h -> d e h")).then_inc(s_weights, 16)
                            sp.dma_start(DN[:, :].rearrange("p (e c d) -> p e c d", c=2, d=D),
                                         a["L0_ffn_bank_down"].rearrange("e (c p) d -> p e c d", p=P)).then_inc(s_weights, 16)
                            sp.dma_start(PH[:, :], row_to_all(a["L0_ffn_bank_phase"].rearrange("e h -> (e h)"), E0 * H0)).then_inc(s_weights, 16)
                            sp.wait_ge(S["z"], 1)
                            for u in range(0, PADDED, CLEAR):
                                sp.dma_start(xs_sorted[u * P:(u + CLEAR) * P, :].rearrange("(p t) d -> p (t d)", p=P),
                                             zero[:, :]).then_inc(s_zero, 16)
                            sp.wait_ge(s_weights, 64)
                            sp.wait_ge(s_zero, 16 * (PADDED // CLEAR))

                        @block.gpsimd
                        def _(pool):
                            pool.memset(zero[:, :], 0.0).then_inc(S["number"], 1)
                            pool.wait_ge(S["number"], 1)
                            pool.iota(zero[:, :].bitcast(I32).rearrange("p (t d) -> p t d", d=DW)[:, :, D:DW], pattern=[[1, CLEAR], [0, 1]],
                                      base=2 * TILES * P, channel_multiplier=CLEAR).then_inc(S["z"], 1)
                            pool.iota(numbers, pattern=[[2 * P, TILES], [0, 1]], base=0, channel_multiplier=2)
                            with pool.Fori(0, GROUPS // 2) as i:
                                for u in range(2):
                                    pool.wait_ge(S["xs"], i * 2 + u + 1)
                                    pool.tensor_copy(XW[:, bass.ds(i * (2 * GROUP * DW) + u * GROUP * DW, GROUP * DW)]
                                                     .rearrange("p (t d) -> p t d", d=DW)[:, :, 0:D],
                                                     xs[:, u, :].rearrange("p (t d) -> p t d", d=D)).then_inc(S["kept"], 1)

                        @block.vector
                        def _(dve):
                            dve.sem_inc(S["kept"], 2)

                            def norm(g, u):
                                dve.wait_ge(S["kept"], g + 1)
                                dve.wait_ge(S["turned"], g + 1)
                                norm_tiles(dve, lambda j: xs[:, u, j * D:(j + 1) * D], X, g * GW, g * (2 * GROUP)).then_inc(S["xs"], 1)

                            with dve.Fori(0, GROUPS // 2) as i:
                                for u in range(2):
                                    norm(i * 2 + u, u)
                            dve.wait_ge(S["scores"], GROUPS + 2)
                            dve.tensor_tensor(SC[:, :].rearrange("p (t e) -> p t e", e=E0), pR[:, :].rearrange("p (t e) -> p t e", e=E0),
                                              bias_of_all, ALU.add)

                        @block.tensor
                        def _(pe):
                            pe.sem_inc(S["turned"], 2)
                            pe.sem_inc(S["scores"], 2)

                            def turn(g, u):
                                pe.wait_ge(S["xs"], g + 1)
                                pe.wait_ge(S["xsT"], g + 1)
                                for j in range(GROUP):
                                    last = pe.transpose(pT[u][:, j * P:(j + 1) * P], xs[:, u, j * D:(j + 1) * D], ident[:, :])
                                last.then_inc(S["turned"], 1)

                            def scores(g, u):
                                pe.wait_ge(S["xsT"], g + 3)
                                for j in range(GROUP):
                                    last = pe.matmul(pR[:, bass.ds(g * (GROUP * E0) + j * E0, E0)], xsT[:, u, j * P:(j + 1) * P],
                                                     router_wT[:, :], start=True, stop=True)
                                last.then_inc(S["scores"], 1)
                            one_ahead(pe, turn, scores)

                        @block.scalar
                        def _(act):
                            act.sem_inc(S["xsT"], 2)
                            with act.Fori(0, GROUPS // 2) as i:
                                for u in range(2):
                                    act.wait_ge(S["turned"], i * 2 + u + 3)
                                    act.wait_ge(S["scores"], i * 2 + u + 1)
                                    act.activation(xsT[:, u, :], pT[u][:, :], ACT.Copy).then_inc(S["xsT"], 1)

                    with ExitStack() as st3:
                        def sb3(n, shape, dt=F32):
                            return st3.enter_context(nc.sbuf_tensor(uniq(n), shape, dt))
                        idx = sb3("idx", [P, TILES * E0])
                        notfirst = sb3("notfirst", [P, TILES * E0])
                        unit_no = sb3("unit_no", [P, PADDED])
                        m1, m2, k = (sb3(n, [P, TILES]) for n in ("m1", "m2", "k"))
                        oh1, oh2, sc2 = (sb3(n, [P, TILES * E0]) for n in ("oh1", "oh2", "sc2"))
                        cnt = sb3("cnt", [P, TILES * E0], BF16)
                        tot = sb3("tot", [P, TILES * E0])
                        run = sb3("run", [P, TILES * E0])
                        slot = sb3("slot", [P, TILES * E0])
                        nt, ci, base = (sb3(n, [P, E0]) for n in ("nt", "ci", "base"))
                        cmp = sb3("cmp", [P, PADDED * E0])
                        unit_f = sb3("unit_f", [P, PADDED])
                        pE = [st3.enter_context(nc.psum_tensor(uniq("pE"), [P, 512], F32)) for _ in range(2)]
                        pS = [st3.enter_context(nc.psum_tensor(uniq("pS"), [P, 512], F32)) for _ in range(2)]
                        S = {n: semaphore(n) for n in ("c", "iota", "delta", "exp", "cnt", "sums", "slots", "numbers")}
                        s_moved = gather_semaphore("s_moved")
                        block = st3.enter_context(nc.Block())
                        te = lambda t: t[:, :].rearrange("p (t e) -> p t e", e=E0)
                        et = lambda t: t[:, :].rearrange("p (e t) -> p e t", t=TILES)
                        te_as_et = lambda t: t[:, :].rearrange("p (t e) -> p e t", e=E0)

                        @block.gpsimd
                        def _(pool):
                            pool.iota(te(idx), pattern=[[0, TILES], [-1, E0]], base=E0, channel_multiplier=0,
                                      allow_small_or_imprecise_dtypes=True)
                            pool.iota(unit_no[:, :], pattern=[[1, PADDED]], base=0, channel_multiplier=0,
                                      allow_small_or_imprecise_dtypes=True)
                            pool.memset(notfirst[:, :], 1.0).then_inc(S["iota"], 1)
                            pool.wait_ge(S["iota"], 1)
                            pool.memset(et(notfirst)[:, :, 0:1], 0.0).then_inc(S["iota"], 1)
                            for k, s in enumerate((slot1, slot2)):
                                pool.wait_ge(S["slots"], k + 1)
                                if k == 1:
                                    pool.wait_ge(s_moved, 16 * TILES)
                                    pool.iota(numbers, pattern=[[2 * P, TILES], [0, 1]], base=1, channel_multiplier=2).then_inc(S["numbers"], 1)
                                    pool.wait_ge(S["numbers"], 1)
                                for t in range(TILES):
                                    pool.indirect_dma_start(
                                        out=xs_sorted, out_offset=bass.IndirectOffsetOnAxis(ap=s[:, t:t + 1].bitcast(U32), axis=0),
                                        in_=XW[:, t * DW:(t + 1) * DW], in_offset=None).then_inc(s_moved, 16)
                            pool.wait_ge(s_moved, 16 * 2 * TILES)

                        @block.scalar
                        def _(act):
                            act.wait_ge(S["delta"], 1)
                            act.activation(w2[:, :], k[:, :], ACT.Exp).then_inc(S["exp"], 1)

                        @block.tensor
                        def _(pe):
                            pe.wait_ge(S["cnt"], 1)
                            for h in range(2):
                                pe.matmul(pE[h][:, :], strict_b[:, :], cnt[:, h * 512:(h + 1) * 512], start=True, stop=True)
                                last = pe.matmul(pS[h][:, :], ones_b[:, :], cnt[:, h * 512:(h + 1) * 512], start=True, stop=True)
                            last.then_inc(S["sums"], 1)

                        @block.vector
                        def _(dve):
                            link = chain(dve, S["c"])
                            dve.wait_ge(S["iota"], 2)
                            top2(dve, link, SC, E0, (m1, m2, k, oh1, oh2, sc2), idx)
                            dve.tensor_tensor(cnt[:, :], oh1[:, :], oh2[:, :], ALU.add).then_inc(S["cnt"], 1)
                            dve.tensor_tensor(k[:, :], m2[:, :], m1[:, :], ALU.subtract).then_inc(S["delta"], 1)
                            dve.wait_ge(S["exp"], 1)
                            link(dve.tensor_scalar(w1[:, :], w2[:, :], 1.0, None, ALU.add))
                            link(dve.reciprocal(w1[:, :], w1[:, :]))
                            link(dve.tensor_tensor(w2[:, :], w2[:, :], w1[:, :], ALU.mult))
                            dve.wait_ge(S["sums"], 1)
                            for h in range(2):
                                l = dve.tensor_copy(et(tot)[:, :, h * 32:(h + 1) * 32],
                                                    pS[h][:, :].rearrange("p (t e) -> p e t", e=E0))
                            link(l)
                            link(dve.tensor_tensor_scan(run[:, :], notfirst[:, :], tot[:, :], 0.0, ALU.mult, ALU.add))
                            link(dve.tensor_scalar(nt[:, :], et(run)[:, :, TILES - 1], 1.0 / P,
                                                   (P - 1.0) / P - 0.5 + 0.5 / P, ALU.mult, ALU.add))
                            link(dve.tensor_scalar(nt[:, :], nt[:, :], MAGIC, MAGIC, ALU.add, ALU.subtract))
                            link(dve.tensor_tensor_scan(ci[:, :], ones[:, 0:E0], nt[:, :], 0.0, ALU.mult, ALU.add))
                            link(dve.tensor_tensor(base[:, :], ci[:, :], nt[:, :], ALU.subtract))
                            link(dve.tensor_scalar(base[:, :], base[:, :], float(P), None, ALU.mult))
                            link(dve.tensor_tensor(run[:, :], run[:, :], tot[:, :], ALU.subtract))
                            link(dve.tensor_tensor(et(run), et(run), base[:, :].unsqueeze(2).broadcast_to([P, E0, TILES]), ALU.add))
                            for h in range(2):
                                l = dve.tensor_tensor(te_as_et(slot)[:, :, h * 32:(h + 1) * 32], et(run)[:, :, h * 32:(h + 1) * 32],
                                                      pE[h][:, :].rearrange("p (t e) -> p e t", e=E0), ALU.add)
                            link(l)
                            for n, (oh, dst) in enumerate(((oh1, slot1), (oh2, slot2))):
                                link(dve.tensor_tensor(oh[:, :], oh[:, :], slot[:, :], ALU.mult))
                                link(dve.tensor_reduce(k[:, :], te(oh), AX.X, ALU.add))
                                dve.tensor_copy(dst[:, :], k[:, :]).then_inc(S["slots"], 1)
                                dve.wait_ge(S["slots"], n + 1)
                            cv = cmp[:, :].rearrange("p (u e) -> p u e", e=E0)
                            link(dve.tensor_tensor(cv, unit_no[:, :].unsqueeze(2).broadcast_to([P, PADDED, E0]),
                                                   ci[:, :].unsqueeze(1).broadcast_to([P, PADDED, E0]), ALU.is_ge))
                            link(dve.tensor_reduce(unit_f[:, :], cv, AX.X, ALU.add))
                            link(dve.tensor_scalar(unit_f[:, :], unit_f[:, :], float(E0 - 1), None, ALU.min))
                            uf = unit_f[:, :].rearrange("p (b j) -> p b j", j=BATCH)
                            for j in range(BATCH - 2, -1, -1):
                                link(dve.scalar_tensor_tensor(uf[:, :, j], uf[:, :, j + 1], float(E0), uf[:, :, j], ALU.mult, ALU.add))
                            link(dve.tensor_copy(experts_of[:, :], uf[:, :, 0]))

                with ExitStack() as st3:
                    def sb3(n, shape, dt=F32):
                        return st3.enter_context(nc.sbuf_tensor(uniq(n), shape, dt))
                    BW = BATCH * H0
                    tanhs = [XN[:, k * BW:(k + 1) * BW] for k in range(4)]
                    freqs = [XN[:, (4 + k) * BW:(5 + k) * BW] for k in range(4)]
                    xg = sb3("xg", [P, 4, BATCH * DW])
                    ids = sb3("ids", [P, 4, BATCH], I32)
                    none = sb3("none", [P, BATCH], I32)
                    xgT = sb3("xgT", [P, 2, BATCH * P])
                    fb = sb3("fb", [P, 2, BW])
                    turns = sb3("turns", [P, 2, BW])
                    hT = sb3("hT", [P, 2, BW])
                    yo = sb3("yo", [P, 2, BATCH * D])
                    pMag = st3.enter_context(nc.psum_tensor(uniq("pMag"), [P, BW], F32))
                    pFreq = st3.enter_context(nc.psum_tensor(uniq("pFreq"), [P, BW], F32))
                    pT = st3.enter_context(nc.psum_tensor(uniq("pT"), [P, 512], F32))
                    pH = st3.enter_context(nc.psum_tensor(uniq("pH"), [P, BW], F32))
                    pO = st3.enter_context(nc.psum_tensor(uniq("pO"), [P, 512], F32))
                    S = {n: semaphore(n) for n in
                         ("turned", "xgT", "up", "upfreq", "freq", "front", "low", "exp", "ln", "d", "angle", "sin", "hid", "hTp", "hT",
                          "down", "yo", "begun", "none", "ids", "stored", "phase")}
                    S |= {n: gather_semaphore(n) for n in ("in0", "in1", "in2", "in3", "scattered")}
                    block = st3.enter_context(nc.Block())
                    PAIRS = NBATCH // 2
                    LOOPS = (PAIRS - 2) // 2
                    assert NBATCH == 2 * PAIRS and PAIRS == 2 * LOOPS + 2

                    def load(pool, n, slot):
                        pool.dma_start(xg[:, slot, :].rearrange("p (t d) -> p t d", d=DW),
                                       xs_sorted[bass.ds(n * (BATCH * P), BATCH * P), :].rearrange("(t p) d -> p t d", p=P)
                                       ).then_inc(S[f"in{slot}"], 16)

                    @block.gpsimd
                    def _(pool):
                        def step(n, k, scatter=True, more=True):
                            if scatter:
                                pool.wait_ge(S["yo"], n - 2)
                                pool.sem_inc(S["begun"], 1)
                                for j in range(BATCH):
                                    pool.indirect_dma_start(
                                        out=y_rows, out_offset=bass.IndirectOffsetOnAxis(ap=ids[:, k, j:j + 1].bitcast(U32), axis=0),
                                        in_=yo[:, k % 2, j * D:(j + 1) * D], in_offset=None).then_inc(S["scattered"], 16)
                                pool.wait_ge(S["scattered"], n * (16 * BATCH) - 3 * (16 * BATCH))
                                pool.sem_inc(S["stored"], 1)
                            if more is not None:
                                pool.wait_ge(S["turned"], n + 1)
                                pool.tensor_tensor(ids[:, k, :], xg[:, k, :].bitcast(I32).rearrange("p (t d) -> p t d", d=DW)[:, :, D],
                                                   none[:, :], ALU.add).then_inc(S["ids"], 1)
                                pool.wait_ge(S["ids"], n + 1)
                            if more:
                                load(pool, n + 4, k)

                        for n in range(4):
                            load(pool, n, n)
                        pool.memset(none[:, :], 0).then_inc(S["none"], 1)
                        pool.wait_ge(S["none"], 1)
                        for n in range(4):
                            step(n, n, scatter=False)
                        loops = NBATCH // 4 - 2
                        with pool.Fori(0, loops) as i:
                            for k in range(4):
                                step(i * 4 + k + 4, k)
                        for k in range(4):
                            step(NBATCH - 4 + k, k, more=k < 2)
                        for k in range(4):
                            step(NBATCH + k, k, more=None)

                    @block.tensor
                    def _(pe):
                        def experts(b):
                            return batch_experts(pe, b)

                        def turn(b, slot, loads):
                            pe.wait_ge(S[f"in{slot}"], loads)
                            pe.wait_ge(S["xgT"], b + 1)
                            for j in range(BATCH):
                                last = pe.transpose(pT[:, j * P:(j + 1) * P], xg[:, slot, j * DW:j * DW + D], ident[:, :])
                            last.then_inc(S["turned"], 1)

                        def up(b, slot):
                            es = experts(b)
                            pe.wait_ge(S["xgT"], b + 2)
                            pe.wait_ge(S["freq"], b + 1)
                            for j, e in enumerate(es):
                                last = pe.matmul(pFreq[:, j * H0:(j + 1) * H0], xgT[:, slot % 2, j * P:(j + 1) * P],
                                                 MF[:, bass.ds(e * (2 * H0) + H0, H0)], start=True, stop=True)
                            last.then_inc(S["upfreq"], 1)
                            pe.wait_ge(S["front"], b + 1)
                            for j, e in enumerate(es):
                                last = pe.matmul(pMag[:, j * H0:(j + 1) * H0], xgT[:, slot % 2, j * P:(j + 1) * P],
                                                 MF[:, bass.ds(e * (2 * H0), H0)], start=True, stop=True)
                            last.then_inc(S["up"], 1)

                        def turn_hidden(b, slot):
                            pe.wait_ge(S["hid"], b + 1)
                            pe.wait_ge(S["hT"], b + 1)
                            for j in range(2 * BATCH):
                                last = pe.transpose(pH[:, j * P:(j + 1) * P], tanhs[slot][:, j * P:(j + 1) * P], ident[:, :])
                            last.then_inc(S["hTp"], 1)

                        def down(b, slot):
                            es = experts(b)
                            pe.wait_ge(S["hT"], b + 2)
                            pe.wait_ge(S["yo"], b + 1)
                            for j, e in enumerate(es):
                                for c in range(2):
                                    last = pe.matmul(pO[:, j * D:(j + 1) * D], hT[:, slot % 2, (2 * j + c) * P:(2 * j + c + 1) * P],
                                                     DN[:, bass.ds(e * (2 * D) + c * D, D)], start=(c == 0), stop=(c == 1))
                            last.then_inc(S["down"], 1)

                        def step(b, k, loads, before=True, after=True):
                            c = (k + 2) % 4
                            if before:
                                turn_hidden(b - 2, c)
                            if after:
                                up(b + 2, c)
                                turn(b + 4, k, loads)
                            if before:
                                down(b - 2, c)
                                turn_hidden(b - 1, c + 1)
                            if after:
                                up(b + 3, c + 1)
                                turn(b + 5, k + 1, loads)
                            if before:
                                down(b - 1, c + 1)

                        turn(0, 0, 16)
                        up(0, 0)
                        turn(1, 1, 16)
                        turn_next = lambda n: turn(n, n, 16)
                        up(1, 1)
                        turn_next(2)
                        turn_next(3)
                        step(0, 0, 32, before=False)
                        with pe.Fori(0, LOOPS) as i:
                            step(i * 4 + 2, 2, i * 16 + 32)
                            step(i * 4 + 4, 0, i * 16 + 48)
                        step(NBATCH - 2, 2, 0, after=False)
                        step(NBATCH, 0, 0, after=False)

                    @block.scalar
                    def _(act):
                        act.sem_inc(S["xgT"], 1)
                        act.sem_inc(S["front"], 1)
                        act.sem_inc(S["freq"], 1)
                        act.sem_inc(S["hT"], 1)

                        def turned(b, slot):
                            act.wait_ge(S["turned"], b + 1)
                            act.activation(xgT[:, slot % 2, :], pT[:, :], ACT.Copy).then_inc(S["xgT"], 1)

                        def front(b, slot):
                            act.wait_ge(S["upfreq"], b + 1)
                            act.activation(freqs[slot], pFreq[:, :], ACT.Copy).then_inc(S["freq"], 1)
                            act.wait_ge(S["up"], b + 1)
                            act.wait_ge(S["hTp"], b + 1)
                            act.activation(tanhs[slot], pMag[:, :], ACT.Tanh).then_inc(S["front"], 1)

                        def hidden_turned(b, slot):
                            act.wait_ge(S["hTp"], b + 5)
                            act.wait_ge(S["down"], b + 1)
                            act.activation(hT[:, slot % 2, :], pH[:, :], ACT.Copy).then_inc(S["hT"], 1)

                        def exp(b, slot):
                            act.wait_ge(S["low"], b + 1)
                            act.activation(fb[:, slot % 2, :], fb[:, slot % 2, :], ACT.Exp).then_inc(S["exp"], 1)

                        def ln(b, slot):
                            act.wait_ge(S["exp"], b + 1)
                            act.activation(fb[:, slot % 2, :], fb[:, slot % 2, :], ACT.Ln, bias=1.0).then_inc(S["ln"], 1)

                        def sin(b, slot):
                            act.wait_ge(S["angle"], b + 1)
                            act.activation(turns[:, slot % 2, :], turns[:, slot % 2, :], ACT.Sin, scale=-TURN).then_inc(S["sin"], 1)

                        def step(b, k, before=True, after=True):
                            c = (k + 2) % 4
                            act.preload_act_table_set("natural_log_exp_and_others")
                            exp(b, k)
                            exp(b + 1, k + 1)
                            if before:
                                hidden_turned(b - 2, c)
                            ln(b, k)
                            ln(b + 1, k + 1)
                            act.preload_act_table_set("silu_and_others")
                            if after:
                                front(b + 2, c)
                            if before:
                                hidden_turned(b - 1, c + 1)
                            if after:
                                turned(b + 4, k)
                            sin(b, k)
                            if after:
                                front(b + 3, c + 1)
                                turned(b + 5, k + 1)
                            sin(b + 1, k + 1)

                        act.preload_act_table_set("silu_and_others")
                        turned(0, 0)
                        turned(1, 1)
                        front(0, 0)
                        turned(2, 2)
                        front(1, 1)
                        turned(3, 3)
                        step(0, 0, before=False)
                        with act.Fori(0, LOOPS) as i:
                            step(i * 4 + 2, 2)
                            step(i * 4 + 4, 0)
                        step(NBATCH - 2, 2, after=False)
                        hidden_turned(NBATCH - 2, 2)
                        hidden_turned(NBATCH - 1, 3)

                    @block.vector
                    def _(dve):
                        dve.sem_inc(S["yo"], 1)
                        dve.sem_inc(S["stored"], 2)
                        dve.sem_inc(S["hTp"], 4)
                        dve.sem_inc(S["down"], 2)
                        dve.tensor_scalar(PH[:, :], PH[:, :], 0.1 + PI / 2, 1.0 / (2 * PI), ALU.add, ALU.mult).then_inc(S["phase"], 1)
                        dve.wait_ge(S["phase"], 1)

                        def low(b, slot):
                            dve.wait_ge(S["freq"], b + 2)
                            dve.wait_ge(S["angle"], b - 1)
                            dve.tensor_scalar(fb[:, slot % 2, :], freqs[slot], 40.0, None, ALU.min).then_inc(S["low"], 1)

                        def angle(b, slot, link):
                            u = slot % 2
                            es = batch_experts(dve, b)
                            dve.wait_ge(S["ln"], b + 1)
                            link(dve.tensor_tensor(fb[:, u, :], fb[:, u, :], freqs[slot], ALU.max))
                            for j, e in enumerate(es):
                                last = dve.scalar_tensor_tensor(fb[:, u, j * H0:(j + 1) * H0], fb[:, u, j * H0:(j + 1) * H0],
                                                                1.0 / (2 * PI), PH[:, bass.ds(e * H0, H0)], ALU.mult, ALU.add)
                            link(last)
                            link(dve.tensor_scalar(turns[:, u, :], fb[:, u, :], MAGIC, None, ALU.add))
                            dve.scalar_tensor_tensor(turns[:, u, :], turns[:, u, :], MAGIC, fb[:, u, :],
                                                     ALU.subtract, ALU.subtract).then_inc(S["angle"], 1)

                        def hidden(b, slot):
                            dve.wait_ge(S["sin"], b + 1)
                            dve.tensor_tensor(tanhs[slot], tanhs[slot], turns[:, slot % 2, :], ALU.mult).then_inc(S["hid"], 1)

                        def store(b, slot):
                            dve.wait_ge(S["down"], b + 3)
                            dve.wait_ge(S["stored"], b + 1)
                            dve.tensor_copy(yo[:, slot % 2, :], pO[:, :]).then_inc(S["yo"], 1)

                        def step(b, k, link, before=True, after=True):
                            c = (k + 2) % 4
                            if before:
                                hidden(b - 1, c + 1)
                            angle(b, k, link)
                            if before:
                                store(b - 2, c)
                            angle(b + 1, k + 1, link)
                            if after:
                                low(b + 2, c)
                            hidden(b, k)
                            if before:
                                store(b - 1, c + 1)
                            if after:
                                low(b + 3, c + 1)

                        def first_low(b):
                            dve.wait_ge(S["freq"], b + 2)
                            dve.tensor_scalar(fb[:, b % 2, :], freqs[b], 40.0, None, ALU.min).then_inc(S["low"], 1)

                        first_low(0)
                        first_low(1)
                        link = chain(dve, S["d"])
                        step(0, 0, link, before=False)
                        with dve.Fori(0, LOOPS) as i:
                            link = chain(dve, S["d"], i * 12 + 6)
                            step(i * 4 + 2, 2, link)
                            step(i * 4 + 4, 0, link)
                        link = chain(dve, S["d"], LOOPS * 12 + 6)
                        step(NBATCH - 2, 2, link, after=False)
                        hidden(NBATCH - 1, 3)
                        store(NBATCH - 2, 2)
                        store(NBATCH - 1, 3)

                with ExitStack() as st3:
                    def sb3(n, shape, dt=F32):
                        return st3.enter_context(nc.sbuf_tensor(uniq(n), shape, dt))
                    G = 8
                    R = TILES // G
                    y = sb3("y", [P, 3, G * 2 * D])
                    ya = sb3("ya", [P, 2, G * D])
                    sq = sb3("sq", [P, G * D])
                    ms = sb3("ms", [P, 2, G])
                    eps = sb3("eps", [P, 1])
                    S = {n: semaphore(n) for n in ("g0", "g1", "g2", "second", "mixed", "ms", "rms", "c")}
                    block = st3.enter_context(nc.Block())

                    @block.sync
                    def _(sp):
                        for r in range(R):
                            if r >= 3:
                                sp.wait_ge(S["mixed"], r - 2)
                            sp.dma_start(y[:, r % 3, :].rearrange("p (t d) -> p t d", d=2 * D),
                                         y_rows[r * G * 2 * P:(r + 1) * G * 2 * P, :].rearrange("(t p k) d -> p t (k d)", p=P, k=2)
                                         ).then_inc(S[f"g{r % 3}"], 16)

                    part = lambda r, k: y[:, r % 3, :].rearrange("p (t k d) -> p t k d", k=2, d=D)[:, :, k, :]
                    weight = lambda w, r: w[:, r * G:(r + 1) * G].unsqueeze(2).broadcast_to([P, G, D])

                    @block.gpsimd
                    def _(pool):
                        for r in range(R):
                            pool.wait_ge(S[f"g{r % 3}"], 16 * (r // 3 + 1))
                            pool.tensor_tensor(part(r, 1), part(r, 1), weight(w2, r), ALU.mult).then_inc(S["second"], 1)

                    @block.scalar
                    def _(act):
                        act.preload_act_table_set("sqrt_and_others")
                        for r in range(R):
                            act.wait_ge(S["mixed"], r + 1)
                            if r:
                                act.wait_ge(S["ms"], r)
                            for g in range(G):
                                last = act.activation(sq[:, g * D:(g + 1) * D], ya[:, r % 2, g * D:(g + 1) * D], ACT.Square,
                                                      accum_out=ms[:, r % 2, g:g + 1])
                            last.then_inc(S["ms"], 1)
                            act.wait_ge(S["ms"], r + 1)
                            act.activation(ms[:, r % 2, :], ms[:, r % 2, :], ACT.Sqrt, scale=1.0 / D, bias=eps[:, 0:1]).then_inc(S["rms"], 1)

                    @block.vector
                    def _(dve):
                        dve.memset(eps[:, :], EPS)
                        link = chain(dve, S["c"])
                        v = lambda t: t.rearrange("p (t d) -> p t d", d=D)

                        def mix(r):
                            dve.wait_ge(S[f"g{r % 3}"], 16 * (r // 3 + 1))
                            link(dve.tensor_tensor(part(r, 0), part(r, 0), weight(w1, r), ALU.mult))
                            dve.wait_ge(S["second"], r + 1)
                            dve.tensor_tensor(v(ya[:, r % 2, :]), part(r, 0), part(r, 1), ALU.add).then_inc(S["mixed"], 1)

                        mix(0)
                        for r in range(R):
                            if r + 1 < R:
                                mix(r + 1)
                            u = ya[:, r % 2, :]
                            dve.wait_ge(S["rms"], r + 1)
                            link(dve.reciprocal(ms[:, r % 2, :], ms[:, r % 2, :]))
                            link(dve.tensor_tensor(v(u), v(u), ms[:, r % 2, :].unsqueeze(2).broadcast_to([P, G, D]), ALU.mult))
                            link(dve.tensor_tensor(v(u), v(u), norm_w[:, :].unsqueeze(1).broadcast_to([P, G, D]), ALU.mult))
                            xr = X[:, r * G * D:(r + 1) * G * D]
                            dve.scalar_tensor_tensor(xr, u, 0.5, xr, ALU.mult, ALU.add)

        def l1_ffn(gathered, gather):
            norm_stats(X, LN_EPS, gathered)
            XNT = XN
            with ExitStack() as st:
                SC = st.enter_context(nc.sbuf_tensor(uniq("SC"), [P, TILES * E1], F32))
                GA = st.enter_context(nc.sbuf_tensor(uniq("GA"), [P, (TILES + GROUP) * E1], F32))
                bias_of_all = gbias[:, :].unsqueeze(1).broadcast_to([P, TILES, E1])
                with ExitStack() as st3:
                    xs = st3.enter_context(nc.sbuf_tensor(uniq("xs"), [P, 2, GW], F32))
                    xsT = st3.enter_context(nc.sbuf_tensor(uniq("xsT"), [P, 2, GW], F32))
                    pT = [st3.enter_context(nc.psum_tensor(uniq("pT"), [P, 512], F32)) for _ in range(2)]
                    pR = st3.enter_context(nc.psum_tensor(uniq("pR"), [P, TILES * E1], F32))
                    S = {n: semaphore(n) for n in ("xs", "turned", "xsT", "kept", "scores")}
                    block = st3.enter_context(nc.Block())

                    @block.gpsimd
                    def _(pool):
                        pool.sem_inc(S["kept"], 2)
                        with pool.Fori(0, GROUPS // 2) as i:
                            for u in range(2):
                                pool.wait_ge(S["xsT"], i * 2 + u + 3)
                                pool.tensor_copy(XNT[:, bass.ds(i * (2 * GW) + u * GW, GW)], xsT[:, u, :]).then_inc(S["kept"], 1)

                    @block.vector
                    def _(dve):
                        def norm(g, u):
                            dve.wait_ge(S["turned"], g + 1)
                            norm_tiles(dve, lambda j: xs[:, u, j * D:(j + 1) * D], X, g * GW, g * (2 * GROUP)).then_inc(S["xs"], 1)

                        with dve.Fori(0, GROUPS // 2) as i:
                            for u in range(2):
                                norm(i * 2 + u, u)
                        dve.wait_ge(S["scores"], GROUPS + 2)
                        dve.tensor_tensor(SC[:, :].rearrange("p (t e) -> p t e", e=E1), pR[:, :].rearrange("p (t e) -> p t e", e=E1),
                                          bias_of_all, ALU.add)

                    @block.tensor
                    def _(pe):
                        pe.sem_inc(S["turned"], 2)
                        pe.sem_inc(S["scores"], 2)

                        def turn(g, u):
                            pe.wait_ge(S["xs"], g + 1)
                            pe.wait_ge(S["xsT"], g + 1)
                            for j in range(GROUP):
                                last = pe.transpose(pT[u][:, j * P:(j + 1) * P], xs[:, u, j * D:(j + 1) * D], ident[:, :])
                            last.then_inc(S["turned"], 1)

                        def scores(g, u):
                            pe.wait_ge(S["xsT"], g + 3)
                            for j in range(GROUP):
                                last = pe.matmul(pR[:, bass.ds(g * (GROUP * E1) + j * E1, E1)], xsT[:, u, j * P:(j + 1) * P],
                                                 gate_wT[:, :], start=True, stop=True)
                            last.then_inc(S["scores"], 1)
                        one_ahead(pe, turn, scores)

                    @block.scalar
                    def _(act):
                        act.sem_inc(S["xsT"], 2)
                        with act.Fori(0, GROUPS // 2) as i:
                            for u in range(2):
                                act.wait_ge(S["turned"], i * 2 + u + 3)
                                act.wait_ge(S["scores"], i * 2 + u + 1)
                                act.wait_ge(S["kept"], i * 2 + u + 1)
                                act.activation(xsT[:, u, :], pT[u][:, :], ACT.Copy).then_inc(S["xsT"], 1)

                with ExitStack() as st3:
                    def sb3(n, shape, dt=F32):
                        return st3.enter_context(nc.sbuf_tensor(uniq(n), shape, dt))
                    idx = sb3("idx", [P, TILES * E1])
                    m1, m2, k, w1, w2 = (sb3(n, [P, TILES]) for n in ("m1", "m2", "k", "w1", "w2"))
                    oh1, oh2, sc2 = (sb3(n, [P, TILES * E1]) for n in ("oh1", "oh2", "sc2"))
                    S = {n: semaphore(n) for n in ("c", "iota", "delta", "exp")}
                    block = st3.enter_context(nc.Block())
                    te = lambda t: t[:, :].rearrange("p (t e) -> p t e", e=E1)

                    @block.gpsimd
                    def _(pool):
                        pool.memset(GA[:, TILES * E1:], 0.0)
                        pool.iota(te(idx), pattern=[[0, TILES], [-1, E1]], base=E1, channel_multiplier=0,
                                  allow_small_or_imprecise_dtypes=True).then_inc(S["iota"], 1)

                    @block.scalar
                    def _(act):
                        act.wait_ge(S["delta"], 1)
                        act.activation(w2[:, :], k[:, :], ACT.Exp).then_inc(S["exp"], 1)

                    @block.vector
                    def _(dve):
                        link = chain(dve, S["c"])
                        dve.wait_ge(S["iota"], 1)
                        top2(dve, link, SC, E1, (m1, m2, k, oh1, oh2, sc2), idx)
                        dve.tensor_tensor(k[:, :], m2[:, :], m1[:, :], ALU.subtract).then_inc(S["delta"], 1)
                        dve.wait_ge(S["exp"], 1)
                        link(dve.tensor_scalar(w1[:, :], w2[:, :], 1.0, None, ALU.add))
                        link(dve.reciprocal(w1[:, :], w1[:, :]))
                        link(dve.tensor_tensor(w2[:, :], w2[:, :], w1[:, :], ALU.mult))
                        up = lambda t: t[:, :].unsqueeze(2).broadcast_to([P, TILES, E1])
                        link(dve.tensor_tensor(te(oh1), te(oh1), up(w1), ALU.mult))
                        link(dve.tensor_tensor(te(oh2), te(oh2), up(w2), ALU.mult))
                        dve.tensor_tensor(GA[:, 0:TILES * E1], oh1[:, :], oh2[:, :], ALU.add)

                with ExitStack() as st3:
                    def sb3(n, shape, dt=F32):
                        return st3.enter_context(nc.sbuf_tensor(uniq(n), shape, dt))
                    CH = ER // P
                    gates = sb3("gates", [P, 2, GROUP * ER])
                    hid = sb3("hid", [P, 2, GW])
                    gated = sb3("gated", [P, 4, GW])
                    pU, pG, pO = ([st3.enter_context(nc.psum_tensor(uniq(n), [P, 512], F32)) for _ in range(2)] for n in ("pU", "pG", "pO"))
                    S = {n: semaphore(n) for n in ("gates", "up", "gelu", "gated", "out", "taken", "stored")}
                    block = st3.enter_context(nc.Block())
                    UN = 2
                    LAG = 2
                    KS = UN * CH

                    if not gather:
                        @block.sync
                        def _(sp):
                            with sp.Fori(0, GROUPS) as g:
                                sp.wait_ge(S["taken"], g + 3)
                                sp.dma_start(out_tiles[:, bass.ds(g * GROUP, GROUP), :],
                                             X[:, bass.ds(g * GW, GW)].rearrange("p (t d) -> p t d", d=D)).then_inc(S["stored"], 16)
                            sp.wait_ge(S["stored"], 16 * GROUPS)

                    @block.tensor
                    def _(pe):
                        pe.sem_inc(S["up"], 2 * CH)
                        pe.sem_inc(S["out"], 4)

                        def up(i, kk):
                            g, c = kk // CH, kk % CH
                            if c == 0:
                                pe.wait_ge(S["gates"], i * UN + g + 1)
                            pe.wait_ge(S["gated"], i * KS + kk + 1)
                            pe.matmul(pU[kk % 2][:, :], up1T[:, c % CH * P:(c % CH + 1) * P],
                                      XNT[:, bass.ds(i * (UN * GW) + g * GW, GW)], start=True, stop=True)
                            for j in range(GROUP):
                                gs = gates[:, g % 2, j * ER + c * P:j * ER + (c + 1) * P]
                                last = pe.transpose(pG[kk % 2][:, j * P:(j + 1) * P], gs, ident[:, :])
                            last.then_inc(S["up"], 1)

                        def down(i, kk):
                            g, c = kk // CH, kk % CH
                            pe.wait_ge(S["gated"], i * KS + kk + 3)
                            if c == 0:
                                pe.wait_ge(S["taken"], i * UN + g + 1)
                            for j in range(GROUP):
                                last = pe.matmul(pO[g % 2][:, j * D:(j + 1) * D], gated[:, kk % 4, j * P:(j + 1) * P],
                                                 down1T[:, c * P:(c + 1) * P], start=(c == 0 and j == 0),
                                                 stop=(c == CH - 1), skip_group_check=True)
                            last.then_inc(S["out"], 1)

                        for kk in range(LAG):
                            up(0, kk)
                        with pe.Fori(0, GROUPS // UN - 1) as i:
                            for kk in range(KS):
                                up(i, kk + LAG)
                                down(i, kk)
                        for kk in range(KS):
                            if kk + LAG < KS:
                                up(GROUPS // UN - 1, kk + LAG)
                            down(GROUPS // UN - 1, kk)

                    @block.scalar
                    def _(act):
                        act.preload_act_table_set("gelu_and_others")
                        def expand(group, u, cols):
                            act.wait_ge(S["up"], group * CH + CH)
                            act.activation(gates[:, u, :].rearrange("p (e r) -> p e r", r=R1),
                                           GA[:, bass.ds(cols, GROUP * E1)].unsqueeze(2).broadcast_to([P, GROUP * E1, R1]),
                                           ACT.Copy).then_inc(S["gates"], 1)

                        expand(0, 0, 0)
                        with act.Fori(0, GROUPS // UN) as i:
                            for kk in range(KS):
                                act.wait_ge(S["up"], i * KS + kk + 2 * CH + 1)
                                act.wait_ge(S["gated"], i * KS + kk + 1)
                                act.activation(hid[:, kk % 2, :], pU[kk % 2][:, :], ACT.Gelu).then_inc(S["gelu"], 1)
                                if kk % CH == 1:
                                    g = kk // CH + 1
                                    expand(i * UN + g, g % 2, i * (UN * GROUP * E1) + g * GROUP * E1)

                    @block.vector
                    def _(dve):
                        dve.sem_inc(S["gated"], 2)
                        dve.sem_inc(S["taken"], 2)

                        def onto_x(i, g):
                            dve.wait_ge(S["out"], i * KS + (g + 1) * CH + 4)
                            xv = X[:, bass.ds(i * (UN * GW) + g * GW, GW)]
                            dve.tensor_tensor(xv, xv, pO[g % 2][:, :], ALU.add).then_inc(S["taken"], 1)
                            if gather:
                                dve.wait_ge(S["taken"], i * UN + g + 3)
                                row_stats(dve, X, i * (UN * GW) + g * GW, i * (UN * GROUP) + g * GROUP, GROUP)

                        def step(i, first):
                            for kk in range(KS):
                                dve.wait_ge(S["gelu"], i * KS + kk + 1)
                                dve.wait_ge(S["out"], i * KS + kk + 1)
                                dve.tensor_tensor(gated[:, kk % 4, :], hid[:, kk % 2, :], pG[kk % 2][:, :], ALU.mult).then_inc(S["gated"], 1)
                                if kk % CH == LAG and not (first and kk < CH):
                                    onto_x(i, kk // CH - 1)

                        step(0, True)
                        with dve.Fori(0, GROUPS // UN - 1) as i:
                            step(i + 1, False)
                        onto_x(GROUPS // UN - 1, UN - 1)

        def l0_attn(gathered, gather):
            norm_stats(X, LN_EPS, gathered)
            W = 2 * T
            with ExitStack() as st:
                def sb3(n, shape, dt=F32):
                    return st.enter_context(nc.sbuf_tensor(uniq(n), shape, dt))
                wp = sb3("wp", [D, 6 * D])
                wo = sb3("wo", [D, D])
                wf1 = sb3("wf1", [D, FF])
                wf2 = sb3("wf2", [P, 4 * D])
                cols = sb3("cols", [P, 2])
                b1c = sb3("b1c", [P, 4])
                rows = {n: sb3(n, [P, D]) for n in ("ln1_scale", "ln1_bias", "b2", "ln2_scale", "ln2_bias")}
                first = sb3("first", [P, W])
                halfpi = sb3("halfpi", [P, 1])
                with ExitStack() as st3:
                    def t(n, shape=None, dt=F32):
                        return st3.enter_context(nc.sbuf_tensor(uniq(n), shape or [P, W], dt))
                    xs, xT, k, g, s1, s2, aar, aai, ai, hx, hy = (t(n) for n in ("xs", "xT", "k", "g", "s1", "s2", "aar", "aai", "ai", "hx", "hy"))
                    den, tt, ta, th, ph, sn, cs, r, sg = (t(n) for n in ("den", "tt", "ta", "th", "ph", "sn", "cs", "r", "sg"))
                    qc, qs, kc, ks, ur, ui, yr, yi, tb, tc, z = (t(n) for n in ("qc", "qs", "kc", "ks", "ur", "ui", "yr", "yi", "tb", "tc", "z"))
                    junk = [t("junk") for _ in range(2)]
                    q, kv, gs = ([t(n) for _ in range(2)] for n in ("q", "kv", "gs"))
                    sums = t("sums", [P, 8])
                    mean = t("mean", [P, 8])
                    gn = t("gn", [P, 6])
                    lnv = t("lnv", [P, 2])
                    pT, pq, pk, pv, par, pai, pg, pW = (st3.enter_context(nc.psum_tensor(uniq("p"), [P, 512], F32)) for _ in range(8))
                    S = {n: semaphore(n) for n in
                         ("w", "fi", "xs", "kept", "turned", "xT", "proj", "sq1", "abs", "k", "hx", "ai", "q", "g", "d", "mag2", "lnm", "mag",
                          "den", "lnd", "inv", "ang", "at", "turns", "ph", "trig", "rot", "cross", "kcs", "scanned", "silu", "sig", "r", "hy", "kv",
                          "y", "sums", "mean", "var", "lnv", "rstd", "z", "wo", "out")}
                    block = st3.enter_context(nc.Block())
                    col = lambda ap: ap.rearrange("(p o) -> p o", o=1)
                    loads = [(wp[:, n * D:(n + 1) * D], a["L0_attn_" + w]) for n, w in enumerate(("Wq", "Wk", "Wv"))]
                    loads += [(wp[:, 3 * D:5 * D], a["L0_attn_Wa"]), (wp[:, 5 * D:6 * D], a["L0_attn_Wg"]), (wo[:, :], a["L0_attn_Wo"]),
                              (wf1[:, :], a["L0_attn_W1"]),
                              (wf2[:, :].rearrange("p (c d) -> p c d", d=D), a["L0_attn_W2"].rearrange("(c p) d -> p c d", p=P)),
                              (cols[:, 0:1], col(a["L0_attn_gn_scale"])), (cols[:, 1:2], col(a["L0_attn_gn_bias"])),
                              (b1c[:, :], a["L0_attn_b1"].rearrange("(c p) -> p c", p=P))]
                    loads += [(rows[n][:, :], row_to_all(a["L0_attn_" + n], D)) for n in rows]
                    f = lambda x: x[:, :]
                    HALVES = [slice(h * T, (h + 1) * T) for h in range(2)]

                    def steps(eng, step):
                        for n in range(-2, 1):
                            step(n, n)
                        loops = (GROUPS - 4) // 2
                        with eng.Fori(0, loops) as it:
                            step(it * 2 + 1, 1)
                            step(it * 2 + 2, 2)
                        for n in range(2 * loops + 1, GROUPS + 1):
                            step(n, n)

                    exists = lambda n: 0 <= n < GROUPS

                    @block.sync
                    def _(sp):
                        with nc.allow_non_contiguous_dma(reason="a few columns of 4 bytes"):
                            for dst, src in loads:
                                sp.dma_start(dst, src).then_inc(S["w"], 16)

                    @block.gpsimd
                    def _(pool):
                        pool.memset(first[:, :], 1.0).then_inc(S["fi"], 1)
                        pool.wait_ge(S["fi"], 1)
                        pool.memset(first[:, 0:W:T], 0.0)
                        pool.memset(halfpi[:, :], PI / 2).then_inc(S["fi"], 1)

                        def step(i, n):
                            if exists(n):
                                pool.wait_ge(S["trig"], i + 1)
                                pool.wait_ge(S["q"], i + 1)
                                pool.tensor_tensor(f(qc), f(cs), f(q[n % 2]), ALU.mult)
                                pool.tensor_tensor(f(qs), f(sn), f(q[n % 2]), ALU.mult).then_inc(S["rot"], 1)
                                pool.wait_ge(S["scanned"], i + 1)
                                pool.wait_ge(S["rot"], i + 1)
                                pool.tensor_tensor(f(tb), f(qs), f(ui), ALU.mult)
                                pool.tensor_tensor(f(tc), f(qs), f(ur), ALU.mult).then_inc(S["cross"], 1)
                            if exists(n + 2):
                                pool.wait_ge(S["xs"], i + 3)
                                pool.tensor_copy(XN[:, bass.ds(i * GW + 2 * GW, GW)],
                                                 xs[:, :]).then_inc(S["kept"], 1)
                            if exists(n + 1):
                                pool.wait_ge(S["sig"], i + 2)
                                pool.tensor_tensor(f(r), f(r), f(first), ALU.mult).then_inc(S["r"], 1)
                                pool.tensor_tensor(f(gs[(n + 1) % 2]), f(g), f(sg), ALU.mult).then_inc(S["silu"], 1)

                        steps(pool, step)

                    @block.tensor
                    def _(pe):
                        pe.wait_ge(S["w"], 16 * len(loads))

                        def step(i, n):
                            if exists(n + 2):
                                pe.wait_ge(S["xs"], i + 3)
                                for j in range(GROUP):
                                    last = pe.transpose(pT[:, j * P:(j + 1) * P], xs[:, j * D:(j + 1) * D], ident[:, :])
                                last.then_inc(S["turned"], 1)
                                pe.wait_ge(S["xT"], i + 3)
                                for m, pp, sem in ((3, par, "hx"), (4, pai, "ai"), (1, pk, "k"), (2, pv, "kv"), (0, pq, "q"), (5, pg, "g")):
                                    if exists(n + 1):
                                        pe.wait_ge(S[sem], i + 2)
                                    pe.matmul(pp[:, :], wp[:, m * D:(m + 1) * D], xT[:, :], start=True, stop=True).then_inc(S["proj"], 1)
                            if exists(n - 1):
                                pe.wait_ge(S["z"], i)
                                for j in range(GROUP):
                                    last = pe.matmul(pW[:, j * D:(j + 1) * D], z[:, j * P:(j + 1) * P], wo[:, :], start=True, stop=True)
                                last.then_inc(S["wo"], 1)
                            if exists(n):
                                pe.wait_ge(S["sums"], i + 1)
                                if exists(n - 1):
                                    pe.wait_ge(S["out"], i)
                                pe.matmul(pW[:, 0:8], blockg[:, :], sums[:, :], start=True, stop=True).then_inc(S["mean"], 1)

                        steps(pe, step)

                    @block.scalar
                    def _(act):
                        act.wait_ge(S["fi"], 2)

                        def step(i, n):
                            logs, gate, recur, rows_in = exists(n - 1) or exists(n + 1), exists(n + 1), exists(n), exists(n + 2)
                            if logs:
                                act.preload_act_table_set("natural_log_exp_and_others")
                            if gate:
                                act.wait_ge(S["mag2"], i + 2)
                                act.activation(f(s1), f(s1), ACT.Ln).then_inc(S["lnm"], 1)
                                act.wait_ge(S["lnm"], i + 2)
                                act.activation(f(s1), f(s1), ACT.Exp, scale=0.5).then_inc(S["mag"], 1)
                            if exists(n - 1):
                                act.wait_ge(S["var"], i)
                                act.activation(lnv[:, :], gn[:, 0:2], ACT.Ln).then_inc(S["lnv"], 1)
                                act.wait_ge(S["lnv"], i)
                                act.activation(gn[:, 0:2], lnv[:, :], ACT.Exp, scale=-0.5).then_inc(S["rstd"], 1)
                            if rows_in:
                                act.wait_ge(S["turned"], i + 3)
                                act.activation(f(xT), f(pT), ACT.Copy).then_inc(S["xT"], 1)
                            if gate:
                                act.wait_ge(S["proj"], i * 6 + 12)
                                if exists(n - 1):
                                    act.wait_ge(S["rot"], i)
                                act.activation(f(q[(n + 1) % 2]), f(pq), ACT.Copy).then_inc(S["q"], 1)
                                if recur:
                                    act.wait_ge(S["silu"], i + 1)
                                act.activation(f(g), f(pg), ACT.Copy).then_inc(S["g"], 1)
                                act.wait_ge(S["den"], i + 2)
                                act.activation(f(den), f(den), ACT.Ln).then_inc(S["lnd"], 1)
                                act.wait_ge(S["lnd"], i + 2)
                                act.activation(f(den), f(den), ACT.Exp, scale=-1.0).then_inc(S["inv"], 1)
                                act.preload_act_table_set("sigmoid_and_others")
                                act.wait_ge(S["ang"], i + 2)
                                act.activation(f(tt), f(tt), ACT.Arctan).then_inc(S["at"], 1)
                                if recur:
                                    act.wait_ge(S["scanned"], i + 1)
                                    act.wait_ge(S["silu"], i + 1)
                                act.activation(f(r), f(s1), ACT.Sigmoid)
                                act.wait_ge(S["g"], i + 2)
                                act.activation(f(sg), f(g), ACT.Sigmoid).then_inc(S["sig"], 1)
                            if rows_in:
                                act.wait_ge(S["proj"], i * 6 + 14)
                                if gate:
                                    act.wait_ge(S["sig"], i + 2)
                                act.activation(f(s1), f(par), ACT.Square)
                                act.activation(f(s2), f(pai), ACT.Square).then_inc(S["sq1"], 1)
                                act.activation(f(aar), f(par), ACT.Abs)
                                act.activation(f(aai), f(pai), ACT.Abs).then_inc(S["abs"], 1)
                                act.wait_ge(S["proj"], i * 6 + 15)
                                act.activation(f(k), f(pk), ACT.Copy).then_inc(S["k"], 1)
                            if gate:
                                act.preload_act_table_set("trig_and_small")
                                act.wait_ge(S["turns"], i + 2)
                                if recur:
                                    act.wait_ge(S["rot"], i + 1)
                                    act.wait_ge(S["kcs"], i + 1)
                                act.activation(f(ph), f(th), ACT.Abs).then_inc(S["ph"], 1)
                                act.activation(f(sn), f(th), ACT.Sin, scale=TURN)
                                act.wait_ge(S["ph"], i + 2)
                                act.activation(f(cs), f(ph), ACT.Sin, scale=-TURN, bias=halfpi[:, 0:1]).then_inc(S["trig"], 1)
                            if recur:
                                act.wait_ge(S["y"], i + 1)
                                if exists(n - 1):
                                    act.wait_ge(S["mean"], i)
                                for c, y, squares in ((4, yr, junk[0]), (6, yi, junk[1])):
                                    for h in range(2):
                                        last = act.activation(squares[:, HALVES[h]], y[:, HALVES[h]], ACT.Square,
                                                              accum_out=sums[:, c + h:c + h + 1])
                                last.then_inc(S["sums"], 1)
                            if rows_in:
                                act.activation(f(hx), f(par), ACT.Sign).then_inc(S["hx"], 1)
                                if gate:
                                    act.wait_ge(S["hy"], i + 2)
                                act.activation(f(ai), f(pai), ACT.Copy).then_inc(S["ai"], 1)

                        steps(act, step)

                    @block.vector
                    def _(dve):
                        dve.wait_ge(S["w"], 16 * len(loads))
                        dve.wait_ge(S["fi"], 2)
                        count = [0]
                        base = [0]

                        def link(ins):
                            count[0] += 1
                            ins.then_inc(S["d"], 1)
                            dve.wait_ge(S["d"], base[0] + count[0])

                        def norm(col, t0):
                            norm_tiles(dve, lambda j: xs[:, j * D:(j + 1) * D], X, col, t0).then_inc(S["xs"], 1)

                        def step(i, n):
                            gate, recur, rows_in, ends = exists(n + 1), exists(n), exists(n + 2), exists(n - 1)
                            if gate:
                                dve.wait_ge(S["sq1"], i + 2)
                                dve.scalar_tensor_tensor(f(s1), f(s1), 1e-36, f(s2), ALU.add, ALU.add).then_inc(S["mag2"], 1)
                            if recur:
                                dve.wait_ge(S["trig"], i + 1)
                                dve.tensor_tensor(f(kc), f(kv[n % 2]), f(cs), ALU.mult)
                                link(dve.scalar_tensor_tensor(f(ks), f(kv[n % 2]), -1.0, f(sn), ALU.mult, ALU.mult))
                                dve.sem_inc(S["kcs"], 1)
                            if ends:
                                dve.wait_ge(S["mean"], i)
                                link(dve.tensor_copy(mean[:, :], pW[:, 0:8]))
                                link(dve.tensor_tensor(gn[:, 2:6], mean[:, 0:4], mean[:, 0:4], ALU.mult))
                                link(dve.tensor_tensor(gn[:, 2:6], mean[:, 4:8], gn[:, 2:6], ALU.subtract))
                                dve.scalar_tensor_tensor(gn[:, 0:2], gn[:, 2:4], EPS, gn[:, 4:6], ALU.add, ALU.add).then_inc(S["var"], 1)
                            if recur:
                                dve.wait_ge(S["r"], i + 1)
                                dve.tensor_tensor_scan(f(ur), f(r), f(kc), 0.0, ALU.mult, ALU.add)
                            if gate:
                                dve.wait_ge(S["mag"], i + 2)
                                dve.wait_ge(S["abs"], i + 2)
                                dve.tensor_tensor(f(den), f(aar), f(s1), ALU.add).then_inc(S["den"], 1)
                                dve.wait_ge(S["ai"], i + 2)
                                dve.tensor_scalar(f(hy), f(ai), 0.0, 0.5, ALU.is_ge, ALU.subtract).then_inc(S["hy"], 1)
                            if recur:
                                link(dve.tensor_tensor_scan(f(ui), f(r), f(ks), 0.0, ALU.mult, ALU.add))
                                dve.sem_inc(S["scanned"], 1)
                            if ends:
                                dve.wait_ge(S["rstd"], i)
                                link(dve.tensor_scalar(gn[:, 0:2], gn[:, 0:2], cols[:, 0:1], None, ALU.mult))
                                link(dve.tensor_tensor(gn[:, 2:4], mean[:, 0:2], gn[:, 0:2], ALU.mult))
                                link(dve.tensor_scalar(gn[:, 2:4], gn[:, 2:4], -1.0, cols[:, 1:2], ALU.mult, ALU.add))
                                for h in range(2):
                                    l = dve.tensor_scalar(z[:, HALVES[h]], yr[:, HALVES[h]], gn[:, h:h + 1],
                                                          gn[:, 2 + h:3 + h], ALU.mult, ALU.add)
                                link(l)
                                dve.wait_ge(S["silu"], i)
                                dve.tensor_tensor(f(z), f(z), f(gs[(n - 1) % 2]), ALU.mult).then_inc(S["z"], 1)
                            if recur:
                                dve.wait_ge(S["rot"], i + 1)
                                dve.tensor_tensor(f(yr), f(qc), f(ur), ALU.mult)
                            if gate:
                                dve.wait_ge(S["inv"], i + 2)
                                dve.tensor_tensor(f(tt), f(aai), f(den), ALU.mult).then_inc(S["ang"], 1)
                            if recur:
                                link(dve.tensor_tensor(f(yi), f(qc), f(ui), ALU.mult))
                                dve.wait_ge(S["cross"], i + 1)
                                dve.tensor_tensor(f(yr), f(yr), f(tb), ALU.subtract)
                                link(dve.tensor_tensor(f(yi), f(yi), f(tc), ALU.add))
                            if ends:
                                dve.wait_ge(S["wo"], i)
                                dve.wait_ge(S["kept"], i)
                                xv = XN[:, bass.ds(i * GW - GW, GW)]
                                dve.tensor_tensor(xv, xv, f(pW), ALU.add).then_inc(S["out"], 1)
                            if gate:
                                dve.wait_ge(S["at"], i + 2)
                                dve.wait_ge(S["hx"], i + 2)
                                link(dve.tensor_scalar(f(tt), f(tt), 2.0 / PI, -0.5, ALU.mult, ALU.add))
                                link(dve.tensor_tensor(f(tt), f(tt), f(hx), ALU.mult))
                                dve.wait_ge(S["hy"], i + 2)
                                link(dve.scalar_tensor_tensor(f(tt), f(tt), 0.5, f(hy), ALU.add, ALU.mult))
                                link(dve.tensor_tensor_scan(f(th), f(first), f(tt), 0.0, ALU.mult, ALU.add))
                                link(dve.tensor_scalar(f(ta), f(th), MAGIC, MAGIC, ALU.add, ALU.subtract))
                                dve.tensor_tensor(f(th), f(th), f(ta), ALU.subtract).then_inc(S["turns"], 1)
                            if recur:
                                seq = lambda x: x[:, :].rearrange("p (s t) -> p s t", s=2)
                                dve.tensor_reduce(sums[:, 0:2], seq(yr), AX.X, ALU.add)
                                dve.tensor_reduce(sums[:, 2:4], seq(yi), AX.X, ALU.add).then_inc(S["y"], 1)
                            if rows_in:
                                dve.wait_ge(S["k"], i + 3)
                                dve.wait_ge(S["proj"], i * 6 + 16)
                                dve.tensor_tensor(f(kv[n % 2]), f(k), f(pv), ALU.mult).then_inc(S["kv"], 1)
                            if exists(n + 3):
                                dve.wait_ge(S["kept"], i + 3)
                                norm(i * GW + 3 * GW, i * (2 * GROUP) + 6 * GROUP)

                        norm(0, 0)
                        for n in range(-2, 1):
                            step(n, n)
                        loops = (GROUPS - 4) // 2
                        LINKS = 16
                        with dve.Fori(0, loops) as it:
                            before = count[0]
                            base[0] = it * (2 * LINKS)
                            step(it * 2 + 1, 1)
                            step(it * 2 + 2, 2)
                            assert count[0] - before == 2 * LINKS
                        base[0] = (loops - 1) * 2 * LINKS
                        for n in range(2 * loops + 1, GROUPS + 1):
                            step(n, n)

                norm_stats(XN, EPS, False)
                with ExitStack() as st3:
                    def t(n, shape=None, dt=F32):
                        return st3.enter_context(nc.sbuf_tensor(uniq(n), shape or [P, W], dt))
                    x1 = t("x1", [P, 2, W])
                    x1T = t("x1T", [P, 2, W])
                    hid = t("hid", [P, 4, W])
                    pT, pU, pO = ([st3.enter_context(nc.psum_tensor(uniq(n), [P, 512], F32)) for _ in range(2)] for n in ("pT", "pU", "pO"))
                    S = {n: semaphore(n) for n in ("d", "x1", "biased", "turned", "x1T", "up", "gelu", "down", "out")}
                    block = st3.enter_context(nc.Block())
                    over = lambda n: rows[n][:, :].unsqueeze(1).broadcast_to([P, GROUP, D])
                    CHUNKS = FF // P
                    PAIRS = GROUPS // 2

                    def pairs(eng, step):
                        with eng.Fori(0, PAIRS - 1) as i:
                            step(i * 2, 0, 2)
                            step(i * 2 + 1, 1, 2)
                        step(GROUPS - 2, 0, 1)
                        step(GROUPS - 1, 1, 0)

                    @block.vector
                    def _(dve):
                        def normed(g, u, base):
                            ln = chain(dve, S["d"], base)
                            v = x1[:, u, :].rearrange("p (t d) -> p t d", d=D)
                            ln(norm_tiles(dve, lambda j: x1[:, u, j * D:(j + 1) * D], XN, g * GW, g * (2 * GROUP)))
                            ln(dve.tensor_tensor(v, v, over("ln1_scale"), ALU.mult))
                            ln(dve.tensor_tensor(v, v, over("ln1_bias"), ALU.add))
                            dve.sem_inc(S["x1"], 1)
                            dve.tensor_tensor(XN[:, bass.ds(g * GW, GW)].rearrange("p (t d) -> p t d", d=D), v, over("b2"),
                                              ALU.add).then_inc(S["biased"], 1)

                        def step(g, u, rest):
                            if rest == 2:
                                dve.wait_ge(S["turned"], g + 1)
                                dve.wait_ge(S["biased"], g + 1)
                                normed(g + 2, u, g * 3 + 6)
                            dve.wait_ge(S["biased"], g + 1)
                            dve.wait_ge(S["down"], g * CHUNKS + 8)
                            xv = XN[:, bass.ds(g * GW, GW)]
                            dve.tensor_tensor(xv, xv, pO[u][:, :], ALU.add).then_inc(S["out"], 1)
                            dve.wait_ge(S["out"], g + 3)
                            row_stats(dve, XN, g * GW, g * GROUP, GROUP)

                        normed(0, 0, 0)
                        normed(1, 1, 3)
                        pairs(dve, step)

                    @block.tensor
                    def _(pe):
                        pe.sem_inc(S["down"], 4)
                        pe.sem_inc(S["out"], 2)

                        def turn(g, u):
                            pe.wait_ge(S["x1"], g + 1)
                            for j in range(GROUP):
                                last = pe.transpose(pT[u][:, j * P:(j + 1) * P], x1[:, u, j * D:(j + 1) * D], ident[:, :])
                            last.then_inc(S["turned"], 1)

                        def up(g, u, c):
                            if c == 0:
                                pe.wait_ge(S["x1T"], g + 1)
                            pe.wait_ge(S["gelu"], g * CHUNKS + c + 1)
                            pe.matmul(pU[c % 2][:, :], wf1[:, c * P:(c + 1) * P], x1T[:, u, :], start=True, stop=True).then_inc(S["up"], 1)

                        def down(g, u, c):
                            pe.wait_ge(S["gelu"], g * CHUNKS + c + 3)
                            if c == 0:
                                pe.wait_ge(S["out"], g + 1)
                            for j in range(GROUP):
                                last = pe.matmul(pO[u][:, j * D:(j + 1) * D], hid[:, c, j * P:(j + 1) * P],
                                                 wf2[:, c * D:(c + 1) * D], start=(c == 0 and j == 0), stop=(c == CHUNKS - 1),
                                                 skip_group_check=True)
                            last.then_inc(S["down"], 1)

                        def step(g, u, rest):
                            for c in range(CHUNKS):
                                if c == 0 and rest:
                                    turn(g + 1, 1 - u)
                                if c + 2 < CHUNKS:
                                    up(g, u, c + 2)
                                elif rest:
                                    up(g + 1, 1 - u, c + 2 - CHUNKS)
                                down(g, u, c)

                        turn(0, 0)
                        up(0, 0, 0)
                        up(0, 0, 1)
                        pairs(pe, step)

                    @block.scalar
                    def _(act):
                        act.sem_inc(S["gelu"], 2)
                        act.preload_act_table_set("gelu_apprx_tanh_and_others")

                        def turned(g, u):
                            act.wait_ge(S["turned"], g + 1)
                            act.activation(x1T[:, u, :], pT[u][:, :], ACT.Copy).then_inc(S["x1T"], 1)

                        def gelu(g, c):
                            act.wait_ge(S["up"], g * CHUNKS + c + 1)
                            act.wait_ge(S["down"], g * CHUNKS + c + 1)
                            act.activation(hid[:, c, :], pU[c % 2][:, :], ACT.Gelu_apprx_tanh,
                                           bias=b1c[:, c:c + 1]).then_inc(S["gelu"], 1)

                        def step(g, u, rest):
                            if rest:
                                turned(g + 1, 1 - u)
                            gelu(g, 2)
                            gelu(g, 3)
                            if rest:
                                gelu(g + 1, 0)
                                gelu(g + 1, 1)

                        turned(0, 0)
                        gelu(0, 0)
                        gelu(0, 1)
                        pairs(act, step)

                norm_stats(XN, EPS, True)
                with ExitStack() as st3:
                    ys = st3.enter_context(nc.sbuf_tensor(uniq("ys"), [P, 2, GW], F32))
                    S = {n: semaphore(n) for n in ("normed", "scaled", "biased", "added")}
                    block = st3.enter_context(nc.Block())
                    over = lambda n: rows[n][:, :].unsqueeze(1).broadcast_to([P, GROUP, D])
                    tiles = lambda u: ys[:, u, :].rearrange("p (t d) -> p t d", d=D)

                    @block.vector
                    def _(dve):
                        with dve.Fori(0, GROUPS // 2) as i:
                            for u in range(2):
                                g = i * 2 + u
                                dve.wait_ge(S["added"], g + 1)
                                norm_tiles(dve, lambda j: ys[:, u, j * D:(j + 1) * D], XN, g * GW, g * (2 * GROUP)).then_inc(S["normed"], 1)
                                dve.wait_ge(S["normed"], g + 1)
                                dve.tensor_tensor(tiles(u), tiles(u), over("ln2_scale"), ALU.mult).then_inc(S["scaled"], 1)

                    @block.gpsimd
                    def _(pool):
                        pool.sem_inc(S["added"], 2)
                        with pool.Fori(0, GROUPS // 2) as i:
                            for u in range(2):
                                g = i * 2 + u
                                pool.wait_ge(S["scaled"], g + 1)
                                pool.tensor_tensor(tiles(u), tiles(u), over("ln2_bias"), ALU.add).then_inc(S["biased"], 1)
                                pool.wait_ge(S["biased"], g + 1)
                                xv = X[:, bass.ds(g * GW, GW)]
                                pool.tensor_tensor(xv, xv, ys[:, u, :], ALU.add).then_inc(S["added"], 1)

        def l1_attn(gathered, gather):
            norm_stats(X, LN_EPS, gathered)
            SCALE = float(HD) ** -0.5
            QT = T // P
            units = [(0, h, 4) for h in range(0, HEADS, 4)] + [(1, h, 2) for h in range(0, HEADS, 2)]
            NU = len(units)
            with ExitStack() as st3:
                def t(n, shape, dt=F32):
                    return st3.enter_context(nc.sbuf_tensor(uniq(n), shape, dt))
                VN = HEADS * VW
                CW = 32
                HG = P // CW
                xs = t("xs", [P, QT * D])
                xT = t("xT", [P, T])
                kS = t("kS", [P, 2, T])
                qS = t("qS", [P, T])
                Qm = XN[:, :].rearrange("p (u h t) -> p u h t", u=2, h=HEADS)
                hm = t("hm", [P, HEADS])
                Vx = t("Vx", [P, 2, QT, HEADS, CW])
                Vsum = t("Vsum", [P, 2 * VN])
                OT = t("OT", [P, QT, 512])
                O = t("O", [P, QT, HEADS, VW])
                dif = t("dif", [P, 3, 512])
                ET = t("ET", [P, 4, 512])
                mx = t("mx", [P, 2, 4])
                MC = t("MC", [P, QT, HEADS])
                rs = t("rs", [P, QT, HEADS])
                att = t("att", [P, QT * D])
                attT = t("attT", [P, T])
                low = t("low", [P, 2, HEADS])
                neg100 = t("neg100", [P, 1])
                mask2 = t("mask2", [P, T], BF16)
                pS, pX, pOT = ([st3.enter_context(nc.psum_tensor(uniq(n), [P, 512], F32)) for _ in range(2)] for n in ("pS", "pX", "pOT"))
                pA, pB = (st3.enter_context(nc.psum_tensor(uniq(n), [P, 512], F32)) for n in ("pA", "pB"))
                S = {n: semaphore(n) for n in
                     ("c0", "mask", "xs", "turned", "xT", "qk", "qkept", "v", "q", "vx", "vsums", "vkept", "ot0", "ot1",
                      "oturned0", "oturned1", "s", "dif", "xp", "relu", "exp", "pv", "low", "d", "att", "attT", "attTs", "out", "x")}
                block = st3.enter_context(nc.Block())

                @block.gpsimd
                def _(pool):
                    pool.memset(neg100[:, :], -100.0)
                    pool.memset(Vx[:, :, :, :, :], 1.0)
                    pool.memset(mask2[:, 0:P], 0.0)
                    pool.tensor_copy(mask2[:, P:T], causal_b[:, :])
                    link = chain(pool, S["mask"])
                    link(pool.memset(hm[:, :], SCALE))
                    link(pool.affine_select(out=hm[:, :], in_=hm[:, :], compare_op=ALU.is_ge, fill=0.0, base=0,
                                            pattern=[[-HD, HEADS]], channel_multiplier=1))
                    pool.affine_select(out=hm[:, :], in_=hm[:, :], compare_op=ALU.is_ge, fill=0.0, base=HD - 1,
                                       pattern=[[HD, HEADS]], channel_multiplier=-1).then_inc(S["c0"], 1)

                @block.tensor
                def _(pe):
                    def rows_turned(b):
                        pe.wait_ge(S["xs"], b + 1)
                        pe.wait_ge(S["x"], b + 1)
                        for j in range(QT):
                            last = pe.transpose(pA[:, j * P:(j + 1) * P], xs[:, j * D:(j + 1) * D], ident[:, :])
                        last.then_inc(S["turned"], 1)

                    def qkv(b):
                        pe.wait_ge(S["xT"], b + 1)
                        pe.matmul(pA[:, 0:T], qkvT[:, 0:D], xT[:, :], start=True, stop=True)
                        pe.matmul(pA[:, T:2 * T], qkvT[:, D:2 * D], xT[:, :], start=True, stop=True).then_inc(S["qk"], 1)
                        pe.wait_ge(S["vkept"], b + 1)
                        for j in range(QT):
                            last = pe.matmul(pB[:, j * D:(j + 1) * D], xT[:, j * P:(j + 1) * P], qkvT[:, 2 * D:3 * D], start=True, stop=True)
                        last.then_inc(S["v"], 1)

                    def value_sums(b, par):
                        vrow = lambda j: Vx[:, par, j, :, 0:VW]
                        pe.matmul(pB[:, 0:VN], ones[:, :], vrow(0), start=True, stop=False)
                        pe.matmul(pB[:, 0:VN], ones[:, :], vrow(1), start=False, stop=True)
                        pe.matmul(pB[:, VN:2 * VN], ones[:, :], vrow(1), start=True, stop=True).then_inc(S["vsums"], 1)

                    def scores(g, n, par):
                        qt, h0, nh = units[n]
                        K = P * (qt + 1)
                        pe.wait_ge(S["dif"], g + 1)
                        rhs = mask2[:, T - K:T].unsqueeze(1).broadcast_to([P, nh, K])
                        pe.matmul(pS[n % 2][:, :], ident_b[:, :], rhs, start=True, stop=False, skip_group_check=True)
                        for m in range(nh):
                            last = pe.matmul(pS[n % 2][:, m * K:(m + 1) * K], Qm[:, par, h0 + m, qt * P:(qt + 1) * P],
                                             kS[:, par, 0:K], start=False, stop=(m == nh - 1), skip_group_check=True)
                        last.then_inc(S["s"], 1)

                    def turn(g, n):
                        pe.wait_ge(S["dif"], g + 3)
                        pe.wait_ge(S["exp"], g + 1)
                        for m in range(4):
                            last = pe.transpose(pX[n % 2][:, m * P:(m + 1) * P], dif[:, n % 3, m * P:(m + 1) * P], ident[:, :])
                        last.then_inc(S["xp"], 1)

                    def values(g, b, n, par):
                        qt, h0, nh = units[n]
                        pair = qt == 1
                        if pair and n % 2 == 0:
                            return
                        heads = [(n - 1, m) for m in range(nh)] if pair else []
                        heads += [(n, m) for m in range(nh)]
                        pe.wait_ge(S["exp"], g + 3)
                        if n == 0:
                            pe.wait_ge(S["ot0"], b + 1)
                        if n == HEADS // 4 + 1:
                            pe.wait_ge(S["ot1"], b + 1)
                        for kt in range(qt + 1):
                            for u, m in heads:
                                h = units[u][1] + m
                                c0 = CW * (h % HG)
                                last = pe.matmul(pOT[qt][c0:c0 + CW, (h // HG) * P:(h // HG + 1) * P], Vx[:, par, kt, h, :],
                                                 ET[:, u % 4, (m * (qt + 1) + kt) * P:(m * (qt + 1) + kt + 1) * P],
                                                 start=(kt == 0), stop=(kt == qt), tile_position=(0, c0), skip_group_check=True)
                        last.then_inc(S["pv"], 2 if pair else 1)

                    def sums_turned(b, after):
                        pe.wait_ge(S["ot0"], b + 2)
                        if after:
                            pe.wait_ge(S["qkept"], b + 3)
                        else:
                            pe.wait_ge(S["x"], b + 3)
                        for j in range(4):
                            last = pe.transpose(pA[:, j * P:(j + 1) * P], OT[:, 0, j * P:(j + 1) * P], ident[:, :])
                        last.then_inc(S["oturned0"], 1)
                        pe.wait_ge(S["ot1"], b + 2)
                        if after:
                            pe.wait_ge(S["vx"], b + 3)
                        else:
                            pe.wait_ge(S["vkept"], b + 3)
                        for j in range(4):
                            last = pe.transpose(pB[:, j * P:(j + 1) * P], OT[:, 1, j * P:(j + 1) * P], ident[:, :])
                        last.then_inc(S["oturned1"], 1)

                    def attended_turned(b):
                        pe.wait_ge(S["att"], b + 1)
                        for j in range(QT):
                            last = pe.transpose(pA[:, j * P:(j + 1) * P], att[:, j * D:(j + 1) * D], ident[:, :])
                        last.then_inc(S["attT"], 1)

                    def project(b):
                        pe.wait_ge(S["attTs"], b + 1)
                        for j in range(QT):
                            last = pe.matmul(pA[:, T + j * D:T + (j + 1) * D], attT[:, j * P:(j + 1) * P], projT[:, :], start=True, stop=True)
                        last.then_inc(S["out"], 1)

                    def slot(b, par, n, before, after):
                        g = b * NU + n
                        if n == 0:
                            pe.wait_ge(S["q"], b + 1)
                        scores(g, n, par)
                        if before and n == 1:
                            value_sums(b - 1, 1 - par)
                        if after and n == 2:
                            rows_turned(b + 1)
                        if before and n == 6:
                            sums_turned(b - 1, after)
                        if n >= 2 or before:
                            turn(g - 2, (n - 2) % NU)
                        if n >= 4:
                            values(g - 4, b, n - 4, par)
                        elif before:
                            values(g - 4, b - 1, n - 4 + NU, 1 - par)
                        if after and n == 3:
                            qkv(b + 1)
                        if before and n == 10:
                            attended_turned(b - 1)
                        if before and n == 11:
                            project(b - 1)

                    pe.wait_ge(S["c0"], 1)
                    rows_turned(0)
                    qkv(0)
                    pe.wait_ge(S["vx"], 1)
                    for n in range(NU):
                        slot(0, 0, n, False, True)
                    with pe.Fori(0, (B - 2) // 2) as i:
                        for par in (1, 0):
                            for n in range(NU):
                                slot(i * 2 + (2 - par), par, n, True, True)
                    for n in range(NU):
                        slot(B - 1, 1, n, True, False)
                    for n in range(2):
                        turn(B * NU + n - 2, n - 2 + NU)
                        values(B * NU + n - 4, B - 1, n - 4 + NU, 1)
                    for n in range(2, 4):
                        values(B * NU + n - 4, B - 1, n - 4 + NU, 1)
                    value_sums(B - 1, 1)
                    sums_turned(B - 1, False)
                    attended_turned(B - 1)
                    project(B - 1)

                @block.scalar
                def _(act):
                    act.sem_inc(S["exp"], 2)
                    act.sem_inc(S["vkept"], 2)
                    act.sem_inc(S["ot0"], 1)
                    act.sem_inc(S["ot1"], 1)
                    act.preload_act_table_set("exp_and_others")
                    act.wait_ge(S["c0"], 1)

                    def rows_turned(b):
                        act.wait_ge(S["turned"], b + 1)
                        act.activation(xT[:, :], pA[:, 0:T], ACT.Copy).then_inc(S["xT"], 1)

                    def keys(b, par, again=True):
                        act.wait_ge(S["qk"], b + 1)
                        act.activation(kS[:, par, :], pA[:, T:2 * T], ACT.Copy)
                        if again:
                            act.wait_ge(S["q"], b)
                        act.activation(qS[:, :], pA[:, 0:T], ACT.Copy).then_inc(S["qkept"], 1)

                    def queries(b, h0, h1, par):
                        act.wait_ge(S["qkept"], b + 1)
                        for h in range(h0, h1):
                            last = act.activation(Qm[:, par, h, :], qS[:, :], ACT.Copy, scale=hm[:, h:h + 1])
                        if h1 == HEADS:
                            last.then_inc(S["q"], 1)

                    def v_rows(b, par):
                        act.wait_ge(S["v"], b + 1)
                        act.activation(Vx[:, par, :, :, 0:HD], pB[:, 0:2 * D].rearrange("p (k h d) -> p k h d", k=QT, d=HD),
                                       ACT.Copy).then_inc(S["vx"], 1)

                    def keep_sums(b):
                        act.wait_ge(S["vsums"], b + 1)
                        act.activation(Vsum[:, 0:VN], pB[:, 0:VN], ACT.Copy, scale=1e-8)
                        act.activation(Vsum[:, VN:], pB[:, VN:2 * VN], ACT.Copy).then_inc(S["vkept"], 1)

                    def keep_values(b, qt):
                        act.wait_ge(S["pv"], b * NU + 4 + (HEADS // 4 if qt == 0 else NU))
                        act.activation(OT[:, qt, :], pOT[qt][:, :], ACT.Copy).then_inc(S[f"ot{qt}"], 1)

                    def exps(g, n):
                        act.wait_ge(S["xp"], g + 4)
                        act.wait_ge(S["pv"], g + 1)
                        act.activation(ET[:, n % 4, :], pX[n % 2][:, :], ACT.Relu, scale=-1.0).then_inc(S["relu"], 1)
                        act.wait_ge(S["relu"], g + 1)
                        act.activation(ET[:, n % 4, :], ET[:, n % 4, :], ACT.Exp, scale=-1.0).then_inc(S["exp"], 1)

                    def unseen(b, par):
                        act.wait_ge(S["dif"], b * NU + 4 + 2)
                        act.activation(low[:, par, :], MC[:, 0, :], ACT.Exp, scale=-1.0, bias=neg100[:, 0:1]).then_inc(S["low"], 1)

                    def attended_turned(b):
                        act.wait_ge(S["attT"], b + 1)
                        act.activation(attT[:, :], pA[:, 0:T], ACT.Copy).then_inc(S["attTs"], 1)

                    QSPLIT = [0, 3, 6, 9, 12, 14, HEADS]

                    def slot(b, par, n, before, after):
                        g = b * NU + n
                        if n >= 2 or before:
                            exps(g - 2, (n - 2) % NU)
                        if before and n == 2:
                            keep_sums(b - 1)
                        if after and n == 2:
                            rows_turned(b + 1)
                        if after and n == 3:
                            keys(b + 1, 1 - par)
                        if before and n == 4:
                            keep_values(b - 1, 1)
                        if after and n == 4:
                            v_rows(b + 1, 1 - par)
                        if after and 4 <= n < 10:
                            queries(b + 1, *QSPLIT[n - 4:n - 2], 1 - par)
                        if n == 8:
                            unseen(b, par)
                        if n == 9:
                            keep_values(b, 0)
                        if before and n == 10:
                            attended_turned(b - 1)

                    rows_turned(0)
                    keys(0, 0, again=False)
                    v_rows(0, 0)
                    queries(0, 0, HEADS, 0)
                    for n in range(NU):
                        slot(0, 0, n, False, True)
                    with act.Fori(0, (B - 2) // 2) as i:
                        for par in (1, 0):
                            for n in range(NU):
                                slot(i * 2 + (2 - par), par, n, True, True)
                    for n in range(NU):
                        slot(B - 1, 1, n, True, False)
                    for n in range(2):
                        exps(B * NU + n - 2, n - 2 + NU)
                    keep_values(B - 1, 1)
                    keep_sums(B - 1)
                    attended_turned(B - 1)

                @block.vector
                def _(dve):
                    dve.sem_inc(S["dif"], 2)
                    dve.sem_inc(S["xp"], 3)
                    dve.sem_inc(S["x"], 3)
                    dve.wait_ge(S["c0"], 1)
                    dve.sem_inc(S["pv"], 4)
                    hw = lambda ap: ap.rearrange("p (h w) -> p h w", w=VW)
                    Of = lambda j: O[:, j, :, :].rearrange("p h w -> p (h w)")

                    def norm(b):
                        norm_tiles(dve, lambda j: xs[:, j * D:(j + 1) * D], X, b * (QT * D), b * (2 * QT), QT).then_inc(S["xs"], 1)

                    def unit(g, n, link):
                        qt, h0, nh = units[n]
                        dve.wait_ge(S["s"], g + 1)
                        sc = pS[n % 2][:, :].rearrange("p (h k) -> p h k", h=nh)
                        link(dve.tensor_reduce(mx[:, n % 2, 0:nh], sc, AX.X, ALU.max))
                        link(dve.tensor_scalar(MC[:, qt, h0:h0 + nh], mx[:, n % 2, 0:nh], -100.0, 100.0, ALU.max, ALU.min))
                        dve.wait_ge(S["xp"], g + 1)
                        dve.scalar_tensor_tensor(dif[:, n % 3, :].rearrange("p (h k) -> p h k", h=nh), sc, -100.0,
                                                 MC[:, qt, h0:h0 + nh].unsqueeze(2).broadcast_to([P, nh, P * (qt + 1)]),
                                                 ALU.max, ALU.subtract).then_inc(S["dif"], 1)

                    def finish_sums(b, par, link):
                        ow = lambda p: p[:, :].rearrange("p (h w) -> p h w", w=CW)[:, :, 0:VW]
                        dve.wait_ge(S["low"], b + 1)
                        dve.wait_ge(S["vkept"], b + 3)
                        link(dve.tensor_tensor(O[:, 0, :, :], hw(Vsum[:, VN:]), low[:, par, :].unsqueeze(2).broadcast_to([P, HEADS, VW]), ALU.mult))
                        dve.wait_ge(S["oturned0"], b + 1)
                        dve.tensor_tensor(O[:, 0, :, :], O[:, 0, :, :], ow(pA), ALU.add)
                        dve.wait_ge(S["oturned1"], b + 1)
                        link(dve.tensor_copy(O[:, 1, :, :], ow(pB)))

                    def finish_p(link):
                        link(dve.tensor_scalar(rs[:, :, :], O[:, :, :, HD], 1e-6, None, ALU.add))
                        link(dve.reciprocal(rs[:, :, :], rs[:, :, :]))
                        for j in range(QT):
                            l = dve.tensor_tensor(O[:, j, :, :], O[:, j, :, :], rs[:, j, :].unsqueeze(2).broadcast_to([P, HEADS, VW]), ALU.mult)
                        link(l)

                    def finish(link):
                        for j in range(QT):
                            l = dve.tensor_tensor(Of(j), Of(j), Vsum[:, 0:VN], ALU.add)
                        link(l)
                        link(dve.reciprocal(rs[:, :, :], O[:, :, :, HD]))

                    def finish_rows():
                        for j in range(QT):
                            l = dve.tensor_tensor(att[:, j * D:(j + 1) * D].rearrange("p (h d) -> p h d", d=HD), O[:, j, :, 0:HD],
                                                  rs[:, j, :].unsqueeze(2).broadcast_to([P, HEADS, HD]), ALU.mult)
                        l.then_inc(S["att"], 1)

                    def onto_x(b):
                        dve.wait_ge(S["out"], b + 1)
                        xv = X[:, bass.ds(b * (QT * D), QT * D)]
                        dve.tensor_tensor(xv, xv, pA[:, T:2 * T], ALU.add).then_inc(S["x"], 1)
                        if gather:
                            dve.wait_ge(S["x"], b + 4)
                            row_stats(dve, X, b * (QT * D), b * QT, QT)

                    def slot(b, par, n, before, after, link):
                        if before and n == 9:
                            finish_rows()
                        unit(b * NU + n, n, link)
                        if after and n == 0:
                            norm(b + 1)
                        if before and n == 6:
                            finish_sums(b - 1, 1 - par, link)
                        if before and n == 7:
                            finish_p(link)
                        if before and n == 8:
                            finish(link)
                        if before and n == 11:
                            onto_x(b - 1)

                    UNIT_LINKS, END_LINKS = 2 * NU, 7
                    LINKS = UNIT_LINKS + END_LINKS
                    norm(0)
                    link = chain(dve, S["d"])
                    for n in range(NU):
                        slot(0, 0, n, False, True, link)
                    with dve.Fori(0, (B - 2) // 2) as i:
                        link = chain(dve, S["d"], i * (2 * LINKS) + UNIT_LINKS)
                        for par in (1, 0):
                            for n in range(NU):
                                slot(i * 2 + (2 - par), par, n, True, True, link)
                    link = chain(dve, S["d"], (B - 2) * LINKS + UNIT_LINKS)
                    for n in range(NU):
                        slot(B - 1, 1, n, True, False, link)
                    finish_sums(B - 1, 1, link)
                    finish_p(link)
                    finish(link)
                    finish_rows()
                    onto_x(B - 1)

        table = {"l0_ffn": l0_ffn, "l1_ffn": l1_ffn, "l0_attn": l0_attn, "l1_attn": l1_attn}
        end_stage()
        leaves_stats = ("l1_ffn", "l1_attn")
        for n, s in enumerate(stages):
            table[s](n == 0 or stages[n - 1] in leaves_stats, n + 1 < len(stages))
            end_stage()

        if not stages or stages[-1] != "l1_ffn":
            with ExitStack() as st:
                s_out = semaphore("s_out")
                block = st.enter_context(nc.Block())

                @block.sync
                def _(sp):
                    sp.dma_start(out_tiles, X3).then_inc(s_out, 16)
                    sp.wait_ge(s_out, 16)


_INS = ['L0_attn_x', 'L0_attn_Wq', 'L0_attn_Wk', 'L0_attn_Wv', 'L0_attn_Wa', 'L0_attn_Wg', 'L0_attn_Wo',
        'L0_attn_gn_scale', 'L0_attn_gn_bias', 'L0_attn_ln1_scale', 'L0_attn_ln1_bias', 'L0_attn_W1',
        'L0_attn_b1', 'L0_attn_W2', 'L0_attn_b2', 'L0_attn_ln2_scale', 'L0_attn_ln2_bias',
        'L0_ffn_router_w', 'L0_ffn_router_bias', 'L0_ffn_bank_mag', 'L0_ffn_bank_freq', 'L0_ffn_bank_phase',
        'L0_ffn_bank_down', 'L0_ffn_norm_w', 'L1_attn_w_qkv', 'L1_attn_w_proj', 'L1_ffn_Wg', 'L1_ffn_bg',
        'L1_ffn_W1', 'L1_ffn_W2']


def kernel(**inputs):
    import numpy as _np
    import concourse.bacc as _bacc
    from concourse import mybir as _mybir
    from concourse.bass_utils import run_bass_kernel_spmd as _run

    nc = _bacc.Bacc("TRN2", target_bir_lowering=False, num_devices=1)
    arrays, args = {}, {}
    for name in _INS:
        v = _np.ascontiguousarray(inputs[name])
        arrays[f"in_{name}_dram"] = v
        args[name] = nc.dram_tensor(f"in_{name}_dram", v.shape, _mybir.dt.from_np(v.dtype), kind="ExternalInput").ap()
    out = nc.dram_tensor("out_0_dram", (B, T, D), _mybir.dt.from_np(_np.dtype("float32")), kind="ExternalOutput").ap()
    macaron_kernel(nc, args, out)
    r = _run(nc, [arrays], core_ids=[0])
    return r.results[0]["out_0_dram"]
```
